# Optimizing a Trainium2 kernel written in Bass

```python
import numpy as np
import jax
import jax.numpy as jnp

def _softmax(x, axis=-1):
    return jax.nn.softmax(x, axis=axis)

def _gelu(x):
    return jax.nn.gelu(x, approximate=True)

def _silu(x):
    return jax.nn.silu(x)

def _sigmoid(x):
    return jax.nn.sigmoid(x)

def _layernorm(x, axis=-1, eps=1e-05):
    m = jnp.mean(x, axis=axis, keepdims=True)
    v = jnp.var(x, axis=axis, keepdims=True)
    return (x - m) / jnp.sqrt(v + eps)

def _scatter_add(tgt, idx, src, axis=0):
    return tgt.at[idx].add(src)

def _segment_sum(src, seg, n):
    return jax.ops.segment_sum(src, seg, n)
kernel_name = 'mk_decoder_preln_d2_seqx_r8_fd901f'

def setup_inputs(seed: int=0):
    np.random.seed(seed)
    _w = jnp.asarray

    def _rec_inputs():
        import jax
        import jax.numpy as jnp
        _rk = jax.random.key(seed)
        x = -0.000125 + 0.9999 * jax.random.normal(jax.random.fold_in(_rk, 1), (16, 128, 128), jnp.float32)
        _lenS = 128 - jax.random.randint(jax.random.fold_in(_rk, 7), (16,), 0, max(1, 128 // 4) + 1, jnp.int32)
        _lenS2 = 128 - jax.random.randint(jax.random.fold_in(_rk, 8), (16,), 0, max(1, 128 // 4) + 1, jnp.int32)
        _ctx_768P = jax.random.normal(jax.random.fold_in(_rk, 11), (16, 16, 96), jnp.float32)
        _ctx_768c = jax.random.dirichlet(jax.random.fold_in(_rk, 511), 0.3 * jnp.ones((16,), jnp.float32), (16, 128))
        _ctx_768t = jnp.einsum('bsk,bkd->bsd', _ctx_768c, _ctx_768P)
        _ctx_768t = _ctx_768t * jax.lax.rsqrt(jnp.mean(jnp.square(_ctx_768t)) + 1e-12) * 0.953939
        ctx_768 = 0.00272024 + 0.999456 * (_ctx_768t + 0.3 * jax.random.normal(jax.random.fold_in(_rk, 611), (16, 128, 96), jnp.float32))
        return (x, ctx_768)
    x, ctx_768 = _rec_inputs()

    def _L0_attn_setup():
        import jax, jax.numpy as jnp
        import numpy as np
        import math
        HIDDEN = 128
        HEADS = 16
        HEAD_DIM = HIDDEN // HEADS
        B, S = (2, 256)

        def _xavier(key, shape):
            fan_in, fan_out = (shape[1], shape[0])
            limit = math.sqrt(6.0 / (fan_in + fan_out))
            return jax.random.uniform(key, shape, jnp.float32, -limit, limit)
        key = jax.random.key(seed)
        ks = jax.random.split(key, 5)
        x = jax.random.normal(ks[0], (B, S, HIDDEN), jnp.float32)
        Wq = _xavier(ks[1], (HIDDEN, HIDDEN))
        Wk = _xavier(ks[2], (HIDDEN, HIDDEN))
        Wv = _xavier(ks[3], (HIDDEN, HIDDEN))
        Wo = _xavier(ks[4], (HIDDEN, HIDDEN))
        bq = jnp.zeros((HIDDEN,), jnp.float32)
        bk = jnp.zeros((HIDDEN,), jnp.float32)
        bv = jnp.zeros((HIDDEN,), jnp.float32)
        bo = jnp.zeros((HIDDEN,), jnp.float32)
        return {'x': x, 'Wq': Wq, 'bq': bq, 'Wk': Wk, 'bk': bk, 'Wv': Wv, 'bv': bv, 'Wo': Wo, 'bo': bo}
    _L0_attn_all = _L0_attn_setup()
    _L0_attn_in = {k: v for k, v in _L0_attn_all.items() if k in ('Wq', 'bq', 'Wk', 'bk', 'Wv', 'bv', 'Wo', 'bo')}
    del _L0_attn_all

    def _L0_xattn_setup():
        import jax, jax.numpy as jnp
        import numpy as np
        QUERY_DIM = 128
        CONTEXT_DIM = 96
        HEADS = 8
        DIM_HEAD = 64
        INNER = HEADS * DIM_HEAD
        key = jax.random.key(seed)
        ks = jax.random.split(key, 7)
        B, S, L = (8, 512, 77)
        x = jax.random.normal(ks[0], (B, S, QUERY_DIM), dtype=jnp.float32)
        context = jax.random.normal(ks[1], (B, L, CONTEXT_DIM), dtype=jnp.float32)
        Wq = jax.random.normal(ks[2], (QUERY_DIM, INNER), dtype=jnp.float32) * QUERY_DIM ** (-0.5)
        Wk = jax.random.normal(ks[3], (CONTEXT_DIM, INNER), dtype=jnp.float32) * CONTEXT_DIM ** (-0.5)
        Wv = jax.random.normal(ks[4], (CONTEXT_DIM, INNER), dtype=jnp.float32) * CONTEXT_DIM ** (-0.5)
        Wo = jax.random.normal(ks[5], (INNER, QUERY_DIM), dtype=jnp.float32) * INNER ** (-0.5)
        bo = jax.random.normal(ks[6], (QUERY_DIM,), dtype=jnp.float32) * 0.01
        return {'x': x, 'context': context, 'Wq': Wq, 'Wk': Wk, 'Wv': Wv, 'Wo': Wo, 'bo': bo}
    _L0_xattn_all = _L0_xattn_setup()
    _L0_xattn_in = {k: v for k, v in _L0_xattn_all.items() if k in ('Wq', 'Wk', 'Wv', 'Wo', 'bo')}
    del _L0_xattn_all

    def _L0_ffn_setup():
        import jax, jax.numpy as jnp
        import numpy as np
        DIM = 128
        MOE_HID = 64
        SHARED_HID = 256
        N_EXPERTS = 16
        TOP_K = 2
        NORM_TOPK_PROB = True
        key = jax.random.key(seed)
        ks = jax.random.split(key, 9)
        s = 0.02
        x = jax.random.normal(ks[0], (2, 128, DIM), dtype=jnp.float32)
        Wg = jax.random.normal(ks[1], (N_EXPERTS, DIM), dtype=jnp.float32) * s
        We_gate = jax.random.normal(ks[2], (N_EXPERTS, MOE_HID, DIM), dtype=jnp.float32) * s
        We_up = jax.random.normal(ks[3], (N_EXPERTS, MOE_HID, DIM), dtype=jnp.float32) * s
        We_down = jax.random.normal(ks[4], (N_EXPERTS, DIM, MOE_HID), dtype=jnp.float32) * s
        Ws_gate = jax.random.normal(ks[5], (SHARED_HID, DIM), dtype=jnp.float32) * s
        Ws_up = jax.random.normal(ks[6], (SHARED_HID, DIM), dtype=jnp.float32) * s
        Ws_down = jax.random.normal(ks[7], (DIM, SHARED_HID), dtype=jnp.float32) * s
        Wsg = jax.random.normal(ks[8], (1, DIM), dtype=jnp.float32) * s
        return {'x': x, 'Wg': Wg, 'We_gate': We_gate, 'We_up': We_up, 'We_down': We_down, 'Ws_gate': Ws_gate, 'Ws_up': Ws_up, 'Ws_down': Ws_down, 'Wsg': Wsg}
    _L0_ffn_all = _L0_ffn_setup()
    _L0_ffn_in = {k: v for k, v in _L0_ffn_all.items() if k in ('Wg', 'We_gate', 'We_up', 'We_down', 'Ws_gate', 'Ws_up', 'Ws_down', 'Wsg')}
    del _L0_ffn_all

    def _L1_attn_setup():
        import jax, jax.numpy as jnp
        import numpy as np
        D_MODEL = 128
        NUM_HEADS = 16
        D_HEAD = 64
        N_CTX = 256
        BATCH = 4
        NEG_INF = -10000000000.0
        key = jax.random.key(seed)
        k1, k2, k3, k4, k5 = jax.random.split(key, 5)
        s = 1.0 / np.sqrt(D_MODEL).astype(np.float32)
        x = jax.random.normal(k1, (BATCH, N_CTX, D_MODEL), dtype=jnp.float32)
        W_K = jax.random.normal(k2, (NUM_HEADS, D_HEAD, D_MODEL), dtype=jnp.float32) * s
        W_Q = jax.random.normal(k3, (NUM_HEADS, D_HEAD, D_MODEL), dtype=jnp.float32) * s
        W_V = jax.random.normal(k4, (NUM_HEADS, D_HEAD, D_MODEL), dtype=jnp.float32) * s
        W_O = jax.random.normal(k5, (D_MODEL, NUM_HEADS * D_HEAD), dtype=jnp.float32) * s
        return {'x': x, 'W_K': W_K, 'W_Q': W_Q, 'W_V': W_V, 'W_O': W_O}
    _L1_attn_all = _L1_attn_setup()
    _L1_attn_in = {k: v for k, v in _L1_attn_all.items() if k in ('W_K', 'W_Q', 'W_V', 'W_O')}
    del _L1_attn_all

    def _L1_xattn_setup():
        import jax, jax.numpy as jnp
        import numpy as np
        EPS = 1e-05
        key = jax.random.key(seed)
        ks = jax.random.split(key, 6)
        B, Nq, Nk, Dq, Dk = (16, 256, 256, 128, 96)
        s = lambda d: 1.0 / np.sqrt(d)
        return {'q': jax.random.normal(ks[0], (B, Nq, Dq), dtype=jnp.float32), 'k': jax.random.normal(ks[1], (B, Nk, Dk), dtype=jnp.float32), 'Wq': jax.random.normal(ks[2], (Dq, Dq), dtype=jnp.float32) * s(Dq), 'Wk': jax.random.normal(ks[3], (Dq, Dk), dtype=jnp.float32) * s(Dk), 'Wv': jax.random.normal(ks[4], (Dq, Dk), dtype=jnp.float32) * s(Dk), 'Wo': jax.random.normal(ks[5], (Dq, Dq), dtype=jnp.float32) * s(Dq)}
    _L1_xattn_all = _L1_xattn_setup()
    _L1_xattn_in = {k: v for k, v in _L1_xattn_all.items() if k in ('Wq', 'Wk', 'Wv', 'Wo')}
    del _L1_xattn_all

    def _L1_ffn_setup():
        import jax, jax.numpy as jnp
        import numpy as np
        E = 8
        TOP_K = 2
        D = 128
        DFF = 4 * D
        key = jax.random.key(seed)
        ks = jax.random.split(key, 6)
        b, s = (4, 128)
        x = jax.random.normal(ks[0], (b, s, D), dtype=jnp.float32)
        centroids = jax.random.normal(ks[1], (E, D), dtype=jnp.float32)
        W1 = jax.random.normal(ks[2], (E, D, DFF), dtype=jnp.float32) * (1.0 / np.sqrt(D))
        b1 = jax.random.normal(ks[3], (E, DFF), dtype=jnp.float32) * 0.01
        W2 = jax.random.normal(ks[4], (E, DFF, D), dtype=jnp.float32) * (1.0 / np.sqrt(DFF))
        b2 = jax.random.normal(ks[5], (E, D), dtype=jnp.float32) * 0.01
        return {'x': x, 'centroids': centroids, 'W1': W1, 'b1': b1, 'W2': W2, 'b2': b2}
    _L1_ffn_all = _L1_ffn_setup()
    _L1_ffn_in = {k: v for k, v in _L1_ffn_all.items() if k in ('centroids', 'W1', 'b1', 'W2', 'b2')}
    del _L1_ffn_all
    return {'x': x, 'ctx_768': ctx_768, 'L0_attn_Wq': _L0_attn_in['Wq'], 'L0_attn_bq': _L0_attn_in['bq'], 'L0_attn_Wk': _L0_attn_in['Wk'], 'L0_attn_bk': _L0_attn_in['bk'], 'L0_attn_Wv': _L0_attn_in['Wv'], 'L0_attn_bv': _L0_attn_in['bv'], 'L0_attn_Wo': _L0_attn_in['Wo'], 'L0_attn_bo': _L0_attn_in['bo'], 'L0_xattn_Wq': _L0_xattn_in['Wq'], 'L0_xattn_Wk': _L0_xattn_in['Wk'], 'L0_xattn_Wv': _L0_xattn_in['Wv'], 'L0_xattn_Wo': _L0_xattn_in['Wo'], 'L0_xattn_bo': _L0_xattn_in['bo'], 'L0_ffn_Wg': _L0_ffn_in['Wg'], 'L0_ffn_We_gate': _L0_ffn_in['We_gate'], 'L0_ffn_We_up': _L0_ffn_in['We_up'], 'L0_ffn_We_down': _L0_ffn_in['We_down'], 'L0_ffn_Ws_gate': _L0_ffn_in['Ws_gate'], 'L0_ffn_Ws_up': _L0_ffn_in['Ws_up'], 'L0_ffn_Ws_down': _L0_ffn_in['Ws_down'], 'L0_ffn_Wsg': _L0_ffn_in['Wsg'], 'L1_attn_W_K': _L1_attn_in['W_K'], 'L1_attn_W_Q': _L1_attn_in['W_Q'], 'L1_attn_W_V': _L1_attn_in['W_V'], 'L1_attn_W_O': _L1_attn_in['W_O'], 'L1_xattn_Wq': _L1_xattn_in['Wq'], 'L1_xattn_Wk': _L1_xattn_in['Wk'], 'L1_xattn_Wv': _L1_xattn_in['Wv'], 'L1_xattn_Wo': _L1_xattn_in['Wo'], 'L1_ffn_centroids': _L1_ffn_in['centroids'], 'L1_ffn_W1': _L1_ffn_in['W1'], 'L1_ffn_b1': _L1_ffn_in['b1'], 'L1_ffn_W2': _L1_ffn_in['W2'], 'L1_ffn_b2': _L1_ffn_in['b2']}

def reference(x, ctx_768, L0_attn_Wq, L0_attn_bq, L0_attn_Wk, L0_attn_bk, L0_attn_Wv, L0_attn_bv, L0_attn_Wo, L0_attn_bo, L0_xattn_Wq, L0_xattn_Wk, L0_xattn_Wv, L0_xattn_Wo, L0_xattn_bo, L0_ffn_Wg, L0_ffn_We_gate, L0_ffn_We_up, L0_ffn_We_down, L0_ffn_Ws_gate, L0_ffn_Ws_up, L0_ffn_Ws_down, L0_ffn_Wsg, L1_attn_W_K, L1_attn_W_Q, L1_attn_W_V, L1_attn_W_O, L1_xattn_Wq, L1_xattn_Wk, L1_xattn_Wv, L1_xattn_Wo, L1_ffn_centroids, L1_ffn_W1, L1_ffn_b1, L1_ffn_W2, L1_ffn_b2):
    import jax
    import jax.numpy as jnp

    def _L0_attn_ref(x, Wq, bq, Wk, bk, Wv, bv, Wo, bo):
        import jax, jax.numpy as jnp
        import numpy as np
        import math
        HIDDEN = 128
        HEADS = 16
        HEAD_DIM = HIDDEN // HEADS
        B, S = (2, 256)

        def _xavier(key, shape):
            fan_in, fan_out = (shape[1], shape[0])
            limit = math.sqrt(6.0 / (fan_in + fan_out))
            return jax.random.uniform(key, shape, jnp.float32, -limit, limit)
        b, s, d = x.shape
        h, hd = (HEADS, HEAD_DIM)
        q = (x @ Wq.T + bq).reshape(b, s, h, hd).transpose(0, 2, 1, 3)
        k = (x @ Wk.T + bk).reshape(b, s, h, hd).transpose(0, 2, 1, 3)
        v = (x @ Wv.T + bv).reshape(b, s, h, hd).transpose(0, 2, 1, 3)
        scores = jnp.einsum('bhqd,bhkd->bhqk', q, k) / math.sqrt(hd)
        causal = jnp.tril(jnp.ones((s, s), bool))
        scores = jnp.where(causal, scores, -jnp.inf)
        attn = jax.nn.softmax(scores, axis=-1)
        out = jnp.einsum('bhqk,bhkd->bhqd', attn, v)
        out = out.transpose(0, 2, 1, 3).reshape(b, s, d)
        return out @ Wo.T + bo

    def _L0_xattn_ref(x, context, Wq, Wk, Wv, Wo, bo):
        import jax, jax.numpy as jnp
        import numpy as np
        QUERY_DIM = 128
        CONTEXT_DIM = 96
        HEADS = 8
        DIM_HEAD = 64
        INNER = HEADS * DIM_HEAD
        B, S, _ = x.shape
        L = context.shape[1]
        scale = DIM_HEAD ** (-0.5)
        q = (x @ Wq).reshape(B, S, HEADS, DIM_HEAD).transpose(0, 2, 1, 3)
        k = (context @ Wk).reshape(B, L, HEADS, DIM_HEAD).transpose(0, 2, 1, 3)
        v = (context @ Wv).reshape(B, L, HEADS, DIM_HEAD).transpose(0, 2, 1, 3)
        attn = jnp.einsum('bhsd,bhld->bhsl', q, k) * scale
        attn = jax.nn.softmax(attn, axis=-1)
        out = jnp.einsum('bhsl,bhld->bhsd', attn, v)
        out = out.transpose(0, 2, 1, 3).reshape(B, S, INNER)
        return out @ Wo + bo

    def _L0_ffn_ref(x, Wg, We_gate, We_up, We_down, Ws_gate, Ws_up, Ws_down, Wsg):
        import jax, jax.numpy as jnp
        import numpy as np
        DIM = 128
        MOE_HID = 64
        SHARED_HID = 256
        N_EXPERTS = 16
        TOP_K = 2
        NORM_TOPK_PROB = True
        B, S, D = x.shape
        xt = x.reshape(-1, D)
        gates = jax.nn.softmax(xt @ Wg.T, axis=-1)
        scores, inds = jax.lax.top_k(gates, TOP_K)
        if NORM_TOPK_PROB:
            scores = scores / jnp.sum(scores, axis=-1, keepdims=True)
        g = jnp.einsum('td,ehd->teh', xt, We_gate)
        u = jnp.einsum('td,ehd->teh', xt, We_up)
        h = jax.nn.silu(g) * u
        y_all = jnp.einsum('teh,edh->ted', h, We_down)
        y_sel = jnp.take_along_axis(y_all, inds[:, :, None], axis=1)
        y = jnp.sum(y_sel * scores[:, :, None], axis=1)
        shared = jax.nn.silu(xt @ Ws_gate.T) * (xt @ Ws_up.T) @ Ws_down.T
        y = y + jax.nn.sigmoid(xt @ Wsg.T) * shared
        return y.reshape(B, S, D)

    def _L1_attn_ref(x, W_K, W_Q, W_V, W_O):
        import jax, jax.numpy as jnp
        import numpy as np
        D_MODEL = 128
        NUM_HEADS = 16
        D_HEAD = 64
        N_CTX = 256
        BATCH = 4
        NEG_INF = -10000000000.0
        b, q_len, d_model = x.shape
        d_head = W_K.shape[1]
        K = jnp.einsum('bpd,ihd->biph', x, W_K)
        Q = jnp.einsum('bpd,ihd->biph', x, W_Q)
        V = jnp.einsum('bpd,ihd->biph', x, W_V)
        scores = jnp.einsum('biph,biqh->biqp', K, Q)
        mask = jnp.tril(jnp.ones((q_len, q_len), dtype=bool))
        scores = jnp.where(mask[None, None, :, :], scores, NEG_INF)
        attn = jax.nn.softmax(scores / np.sqrt(d_head).astype(np.float32), axis=-1)
        z = jnp.einsum('biph,biqp->biqh', V, attn)
        z_flat = jnp.transpose(z, (0, 2, 1, 3)).reshape(b, q_len, -1)
        out = jnp.einsum('bqf,df->bqd', z_flat, W_O)
        return out

    def _L1_xattn_ref(q, k, Wq, Wk, Wv, Wo):
        import jax, jax.numpy as jnp
        import numpy as np
        EPS = 1e-05
        query = q @ Wq.T
        key_p = k @ Wk.T
        value = k @ Wv.T
        sim = jnp.einsum('bqd,bkd->bqk', query, key_p)
        mean = jnp.mean(sim, axis=(1, 2), keepdims=True)
        var = jnp.var(sim, axis=(1, 2), keepdims=True)
        sim = (sim - mean) * jax.lax.rsqrt(var + EPS)
        attn = jax.nn.softmax(sim, axis=-1)
        out = jnp.einsum('bqk,bkd->bqd', attn, value)
        return out @ Wo.T

    def _L1_ffn_ref(x, centroids, W1, b1, W2, b2):
        import jax, jax.numpy as jnp
        import numpy as np
        E = 8
        TOP_K = 2
        D = 128
        DFF = 4 * D
        b, s, d = x.shape
        u = x.reshape(b * s, d)
        n = u.shape[0]
        gates = jax.nn.sigmoid(u @ centroids.T)
        if TOP_K < E:
            topk_vals, topk_idx = jax.lax.top_k(gates, TOP_K)
            mask = jnp.zeros_like(gates).at[jnp.arange(n)[:, None], topk_idx].set(topk_vals)
            gates = mask / jnp.sum(mask, axis=-1, keepdims=True)
        h = jax.nn.gelu(jnp.einsum('nd,edf->enf', u, W1) + b1[:, None, :], approximate=False)
        outs = jnp.einsum('enf,efd->end', h, W2) + b2[:, None, :]
        out = jnp.einsum('ne,end->nd', gates, outs)
        return out.reshape(b, s, d)
    x = x + _L0_attn_ref(_layernorm(x, axis=-1), L0_attn_Wq, L0_attn_bq, L0_attn_Wk, L0_attn_bk, L0_attn_Wv, L0_attn_bv, L0_attn_Wo, L0_attn_bo)
    x = x + _L0_xattn_ref(_layernorm(x, axis=-1), ctx_768, L0_xattn_Wq, L0_xattn_Wk, L0_xattn_Wv, L0_xattn_Wo, L0_xattn_bo)
    x = x + _L0_ffn_ref(_layernorm(x, axis=-1), L0_ffn_Wg, L0_ffn_We_gate, L0_ffn_We_up, L0_ffn_We_down, L0_ffn_Ws_gate, L0_ffn_Ws_up, L0_ffn_Ws_down, L0_ffn_Wsg)
    x = x + _L1_attn_ref(_layernorm(x, axis=-1), L1_attn_W_K, L1_attn_W_Q, L1_attn_W_V, L1_attn_W_O)
    x = x + _L1_xattn_ref(_layernorm(x, axis=-1), ctx_768, L1_xattn_Wq, L1_xattn_Wk, L1_xattn_Wv, L1_xattn_Wo)
    x = x + _L1_ffn_ref(_layernorm(x, axis=-1), L1_ffn_centroids, L1_ffn_W1, L1_ffn_b1, L1_ffn_W2, L1_ffn_b2)
    return x

_drawn_inputs = setup_inputs


def setup_inputs(seed=0):
    import zlib

    import numpy as np

    out = dict(_drawn_inputs(seed))
    spreads = {'L0_attn_bq': (0.0, 0.1),
     'L0_attn_bk': (0.0, 2.0),
     'L0_attn_bv': (0.0, 0.1),
     'L0_attn_bo': (0.0, 0.1)}
    factors = {'L0_ffn_Wg': 4.135,
     'L0_ffn_We_gate': 5.591,
     'L0_ffn_We_up': 5.53,
     'L0_ffn_We_down': 4.664,
     'L0_ffn_Ws_gate': 3.842,
     'L0_ffn_Ws_up': 3.696,
     'L0_ffn_Ws_down': 3.911,
     'L0_ffn_Wsg': 8.0,
     'L1_ffn_b1': 23.951,
     'L1_ffn_b2': 8.0}
    for name, (base, spread) in spreads.items():
        noise = np.random.default_rng([zlib.crc32(name.encode()), seed]).standard_normal(out[name].shape)
        drawn = base * np.exp(spread * noise) if base else spread * noise
        out[name] = jnp.asarray(drawn.astype(out[name].dtype))
    for name, factor in factors.items():
        out[name] = (out[name] * factor).astype(out[name].dtype)
    return out
```

```python
from contextlib import ExitStack

import concourse.bass as bass
from concourse import mybir

F32 = mybir.dt.float32
BF16 = mybir.dt.bfloat16
U32 = mybir.dt.uint32
ALU = mybir.AluOpType
ACT = mybir.ActivationFunctionType
AX = mybir.AxisListType

P = 128
NB = 16
CTX = 96
GB = 4
NG = NB // GB
EPS = 1e-5
NEG = -1e30
E0, E1 = 16, 8
NC0 = 10
G0 = E0 + 1


def wait(eng, sem, value):
    if isinstance(value, int) and value <= 0:
        return
    eng.wait_ge(sem, value)


def seq(b):
    return slice(b, b + 1) if isinstance(b, int) else bass.ds(b, 1)


class Shared:

    def __init__(self, nc):
        self.nc, self.phase_sems, self.cleared = nc, [], []

    def sem(self, name):
        self.phase_sems.append(self.nc.alloc_semaphore(name))
        return self.phase_sems[-1]

    def clear(self):
        for s in self.cleared:
            self.nc.release_semaphore(s)
        for s in self.phase_sems:
            self.nc.gpsimd.sem_clear(s)
        self.phase_sems, self.cleared = [], self.phase_sems


def loop(eng, first, body, last):
    body(first)
    with eng.Fori(first + 1, last) as b:
        body(b)
    body(last)


def loop_groups(eng, body):
    body(0)
    with eng.Fori(1, NG) as g:
        body(g)


def attention(K, name, heads, hd, lag, causal, cross, wq, wk, wv, wo, bq=None, bk=None, bv=None, bo=None,
              weights=()):
    nc = K.nc
    nt = heads * hd // P
    nq = heads // 4
    hb = max(1, nt // 4)
    small = hd < 64
    scale = float(hd) ** -0.5
    pj, sc, tr, ov = K.bank[0:2], K.bank[2:4], K.bank[4:6], K.bank[6:8]
    with ExitStack() as ctx:
        def sb(n, shape, dt=F32):
            return ctx.enter_context(nc.sbuf_tensor(f"{name}_{n}", shape, dt))

        def sem(n):
            return K.sem(f"{name}_{n}")

        st, mv, ve, rs = sb("st", [P, 6]), sb("mv", [P, 2]), sb("ve", [P, 1]), sb("rs", [P, 1])
        xn, xT = sb("xn", [P, P]), sb("xT", [P, P])
        carrier = sb("carrier", [P, 1])
        cb = sb("cb", [CTX, P])
        qT = sb("qT", [P, nt, P])
        kblk = sb("kblk", [P, heads, P])
        v = sb("v", [P, 16 * 136 if small else nt * P])
        p = sb("p", [P, nq, 4, P])
        pT = sb("pT", [P, 2, 4, P])
        oT = sb("oT", [P, nt, P])
        negmax, total, rtotal = sb("negmax", [P, nq, 4]), sb("total", [P, nq, 4]), sb("rtotal", [P, nq, 4])

        zeroed, stats, varied, rooted = sem("zeroed"), sem("stats"), sem("varied"), sem("rooted")
        normed, turned, x_turned = sem("normed"), sem("turned"), sem("x_turned")
        ctx_copied = sem("ctx_copied")
        q_made, k_made, v_made = sem("q_made"), sem("k_made"), sem("v_made")
        q_kept, k_kept, k_kept2, v_kept = sem("q_kept"), sem("k_kept"), sem("k_kept2"), sem("v_kept")
        scored, maxed, exped, inverted, scaled = (sem(n) for n in ("scored", "maxed", "exped", "inverted", "scaled"))
        p_turned, p_kept, attended, o_kept, projected, added = (
            sem(n) for n in ("p_turned", "p_kept", "attended", "o_kept", "projected", "added"))
        block = ctx.enter_context(nc.Block())

        def bank_of(use, n=0):
            if nt == 8:
                return {"v": n, "o": 0, "x": 1, "q": n, "k": n}[use]
            return {"v": 0, "o": 1, "x": 0, "q": 1, "k": 0}[use]

        @block.tensor
        def _(pe):
            for s, n in weights:
                pe.wait_ge(s, n)

            def turn_x(b):
                wait(pe, normed, b + 1)
                wait(pe, v_kept, hb * b)
                pe.transpose(pj[bank_of("x")][:, 0:P], xn[:, :], K.ident[:, :]).then_inc(turned, 1)

            def make_qk(b):
                wait(pe, x_turned, b + 1)
                for n in range(hb):
                    if n == 0:
                        wait(pe, added, b - 1)
                        wait(pe, q_kept, hb * b)
                        wait(pe, v_kept, hb * b)
                    for t in range(4 * n, min(4 * n + 4, nt)):
                        mm = pe.matmul(pj[bank_of("q", n)][:, (t % 4) * P:(t % 4 + 1) * P],
                                       wq[:, t * P:(t + 1) * P], xT[:, :], start=True, stop=True)
                    mm.then_inc(q_made, 1)
                if cross:
                    wait(pe, ctx_copied, b + 1)
                for n in range(hb):
                    if nt == 8:
                        wait(pe, q_kept, hb * b + n + 1)
                    for t in range(4 * n, min(4 * n + 4, nt)):
                        mm = pe.matmul(pj[bank_of("k", n)][:, (t % 4) * P:(t % 4 + 1) * P],
                                       wk[:, t * P:(t + 1) * P], cb[:, :] if cross else xT[:, :],
                                       start=True, stop=True)
                    mm.then_inc(k_made, 1)

            def make_v(b):
                width = min(512, nt * P)
                for n in range(hb):
                    wait(pe, k_kept, hb * b + n + 1)
                    if not small:
                        wait(pe, k_kept2, hb * b + n + 1)
                    pe.matmul(pj[bank_of("v", n)][:, 0:width], cb[:, :] if cross else xT[:, :],
                              wv[:, n * 512:n * 512 + width], start=True, stop=True).then_inc(v_made, 1)

            def score(b, j):
                i = nq * b + j
                s = sc[j % 2]
                wait(pe, q_kept, hb * (b + 1))
                wait(pe, k_kept, hb * (b + 1))
                if not small:
                    wait(pe, k_kept2, hb * (b + 1))
                wait(pe, exped, i - 1)
                if causal:
                    pe.matmul(s[:, :], K.identb[:, :], K.maskb[:, :], start=True, stop=False)
                if small:
                    mm = pe.matmul(s[:, :], qT[:, 0, :], kblk[:, 4 * j:4 * j + 4, :],
                                   start=not causal, stop=True)
                else:
                    for t in range(2 * j, 2 * j + 2):
                        mm = pe.matmul(s[:, (t % 2) * 256:(t % 2 + 1) * 256], qT[:, t, :],
                                       kblk[:, 2 * t:2 * t + 2, :], start=not causal,
                                       stop=not causal or t == 2 * j + 1)
                mm.then_inc(scored, 1)

            def turn_p(b, j):
                i = nq * b + j
                wait(pe, scaled, i + 1)
                wait(pe, p_kept, i - 1)
                for h in range(4):
                    mm = pe.transpose(tr[j % 2][:, h * P:(h + 1) * P], p[:, j, h, :], K.ident[:, :])
                mm.then_inc(p_turned, 1)

            def attend(b, j):
                i = nq * b + j
                wait(pe, p_kept, i + 1)
                if j == 0:
                    wait(pe, v_kept, hb * (b + 1))
                    wait(pe, o_kept, hb * b)
                for h in range(4 * j, 4 * j + 4):
                    if small:
                        mm = pe.matmul(ov[0][:, 0:P], v[:, h * P:(h + 1) * P], pT[:, j % 2, h % 4, :],
                                       start=h == 0, stop=h == heads - 1)
                    else:
                        t, r = h // 2, h % 2
                        mm = pe.matmul(ov[t // 4][64 * r:64 * r + 64, (t % 4) * P:(t % 4 + 1) * P],
                                       v[:, h * 64:(h + 1) * 64], pT[:, j % 2, h % 4, :],
                                       start=True, stop=True)
                mm.then_inc(attended, 1)

            def project(b):
                wait(pe, o_kept, hb * (b + 1))
                if isinstance(b, int):
                    wait(pe, added, b)
                wait(pe, v_kept, hb * (b + 1))
                o = pj[bank_of("o")][:, 0:P]
                for t in range(nt):
                    mm = pe.matmul(o, oT[:, t, :], wo[:, t, :], start=t == 0, stop=bo is None and t == nt - 1)
                if bo is not None:
                    mm = pe.matmul(o, K.ones[0:1, :], bo[0:1, :], start=False, stop=True)
                mm.then_inc(projected, 1)

            def body(b):
                final = isinstance(b, int) and b == NB - 1
                make_v(b)
                if not isinstance(b, int) or b > 0:
                    if hb == 2:
                        wait(pe, v_kept, hb * b + 1)
                    else:
                        wait(pe, q_kept, hb * (b + 1))
                    project(b - 1)
                for j in range(nq):
                    if j == nq - lag and not final:
                        wait(pe, v_kept, hb * (b + 1))
                        turn_x(b + 1)
                        make_qk(b + 1)
                    if j < nq - lag:
                        score(b, j + lag)
                    elif not final:
                        score(b + 1, j + lag - nq)
                    turn_p(b, j)
                    if j:
                        attend(b, j - 1)
                attend(b, nq - 1)

            turn_x(0)
            make_qk(0)
            for j in range(lag):
                score(0, j)
            loop(pe, 0, body, NB - 1)
            project(NB - 1)

        @block.vector
        def _(dve):
            def norm_stats(b):
                if isinstance(b, int):
                    wait(dve, K.x_loaded[b // GB], 16)
                else:
                    for s in K.x_loaded:
                        wait(dve, s, 16)
                nc.vector.bn_stats(st[:, :], K.x[:, seq(b), :].rearrange("p a d -> p (a d)")).then_inc(stats, 1)
                dve.wait_ge(stats, 3 * b + 1)
                nc.vector.memset(carrier[:, :], 0.0)
                nc.vector.bn_aggr(mv[:, :], st[:, :]).then_inc(stats, 1)
                dve.wait_ge(stats, 3 * b + 2)
                nc.vector.tensor_scalar(ve[:, :], mv[:, 1:2], EPS, None, ALU.add).then_inc(stats, 1)

            def norm(b):
                wait(dve, rooted, b + 1)
                wait(dve, turned, b)
                nc.vector.tensor_scalar(xn[:, :], K.x[:, seq(b), :].rearrange("p a d -> p (a d)"),
                                        mv[:, 0:1], rs[:, 0:1], ALU.subtract, ALU.mult).then_inc(normed, 1)

            def keep_x(b):
                wait(dve, turned, b + 1)
                nc.vector.tensor_copy(xT[:, :], pj[bank_of("x")][:, 0:P]).then_inc(x_turned, 1)

            def keep_qk(b):
                for n in range(hb):
                    wait(dve, q_made, hb * b + n + 1)
                    w = min(4, nt)
                    src = pj[bank_of("q", n)][:, 0:w * P]
                    dst = qT[:, 4 * n:4 * n + w, :].rearrange("p t d -> p (t d)")
                    if small:
                        nc.vector.tensor_scalar(dst, src, bq[:, 0:1], scale, ALU.add, ALU.mult).then_inc(q_kept, 1)
                    else:
                        nc.vector.tensor_scalar(dst, src, scale, None, ALU.mult).then_inc(q_kept, 1)
                for n in range(hb):
                    wait(dve, k_made, hb * b + n + 1)
                    src = pj[bank_of("k", n)]
                    if small:
                        for c in range(4):
                            mm = nc.vector.scalar_tensor_tensor(
                                out=kblk[:, 4 * c:4 * c + 4, :], in0=src[:, 0:P].unsqueeze(1).to_broadcast([P, 4, P]),
                                scalar=bk[:, 0:1],
                                in1=K.headmask[:, 4 * c:4 * c + 4].unsqueeze(2).to_broadcast([P, 4, P]),
                                op0=ALU.add, op1=ALU.mult)
                        mm.then_inc(k_kept, 1)
                    else:
                        dst = kblk[0:64, 8 * n:8 * n + 8, :].rearrange("p (t r) d -> p t r d", r=2)[:, :, 0, :]
                        nc.vector.tensor_copy(dst, src[0:64, :].rearrange("p (t d) -> p t d", t=4)).then_inc(k_kept, 1)

            def keep_v(b):
                wait(dve, attended, nq * b)
                for n in range(hb):
                    wait(dve, v_made, hb * b + n + 1)
                    src = pj[bank_of("v", n)]
                    if small:
                        dst = v[:, :].rearrange("p (h s) -> p h s", s=136)[:, :, 0:hd]
                        nc.vector.tensor_copy(dst, src[:, 0:P].rearrange("p (h d) -> p h d", h=heads)).then_inc(v_kept, 1)
                    else:
                        nc.vector.tensor_copy(v[:, n * 512:(n + 1) * 512], src[:, :]).then_inc(v_kept, 1)

            def find_max(b, j):
                wait(dve, scored, nq * b + j + 1)
                nc.vector.tensor_reduce(negmax[:, j, :], sc[j % 2][:, :].rearrange("p (h k) -> p h k", h=4),
                                        AX.X, ALU.max, negate=True).then_inc(maxed, 1)

            def invert(b, j):
                wait(dve, exped, nq * b + j + 1)
                nc.vector.reciprocal(rtotal[:, j, :], total[:, j, :]).then_inc(inverted, 1)

            def keep_p(b, j):
                wait(dve, p_turned, nq * b + j + 1)
                wait(dve, attended, nq * b + j - 1)
                nc.vector.tensor_copy(pT[:, j % 2, :, :].rearrange("p h q -> p (h q)"), tr[j % 2][:, :]).then_inc(p_kept, 1)

            def add(b):
                wait(dve, projected, b + 1)
                xb = K.x[:, seq(b), :].rearrange("p a d -> p (a d)")
                nc.vector.tensor_tensor(xb, pj[bank_of("o")][:, 0:P], xb, ALU.add).then_inc(added, 1)

            def body(b):
                final = isinstance(b, int) and b == NB - 1
                keep_v(b)
                if not final:
                    norm_stats(b + 1)
                if not isinstance(b, int) or b > 0:
                    add(b - 1)
                if not final:
                    norm(b + 1)
                for j in range(nq):
                    if j == nq - lag and not final:
                        keep_x(b + 1)
                        keep_qk(b + 1)
                    if j < nq - lag:
                        find_max(b, j + lag)
                    elif not final:
                        find_max(b + 1, j + lag - nq)
                    if j + lag - 1 < nq:
                        invert(b, j + lag - 1)
                    elif not final:
                        invert(b + 1, j + lag - 1 - nq)
                    keep_p(b, j)

            nc.vector.memset(kblk[:, :, :], 0.0).then_inc(zeroed, 1)
            nc.vector.memset(v[:, :], 0.0).then_inc(zeroed, 1)
            dve.wait_ge(zeroed, 2)
            for s, n in weights:
                dve.wait_ge(s, n)
            norm_stats(0)
            norm(0)
            keep_x(0)
            keep_qk(0)
            for j in range(lag):
                find_max(0, j)
                if j:
                    invert(0, j - 1)
            loop(dve, 0, body, NB - 1)
            add(NB - 1)

        @block.gpsimd
        def _(pool):
            def root(b):
                wait(pool, stats, 3 * b + 3)
                nc.gpsimd.tensor_tensor(rs[:, :], ve[:, :], K.mhalf[:, :], ALU.pow).then_inc(rooted, 1)
                if cross:
                    wait(pool, v_made, hb * b)
                    nc.gpsimd.tensor_copy(cb[:, :], K.ctxT[:, seq(b), :].rearrange("p a d -> p (a d)")).then_inc(ctx_copied, 1)

            def divide(b, j):
                wait(pool, inverted, nq * b + j + 1)
                nc.gpsimd.tensor_tensor(p[:, j, :, :], p[:, j, :, :],
                                        rtotal[:, j, :].unsqueeze(2).to_broadcast([P, 4, P]), ALU.mult).then_inc(scaled, 1)

            def body(b):
                final = isinstance(b, int) and b == NB - 1
                if not final:
                    root(b + 1)
                for j in range(nq):
                    if j + lag - 1 < nq:
                        divide(b, j + lag - 1)
                    elif not final:
                        divide(b + 1, j + lag - 1 - nq)

            for s, n in weights:
                pool.wait_ge(s, n)
            root(0)
            for j in range(lag - 1):
                divide(0, j)
            loop(pool, 0, body, NB - 1)

        @block.scalar
        def _(act):
            def exps(b, j):
                wait(act, maxed, nq * b + j + 1)
                wait(act, p_turned, nq * (b - 1) + j + 1)
                for h in range(4):
                    e = nc.scalar.activation(p[:, j, h, :], sc[j % 2][:, h * P:(h + 1) * P], ACT.Exp,
                                             bias=negmax[:, j, h:h + 1], accum_out=total[:, j, h:h + 1])
                e.then_inc(exped, 1)

            def keep_k(b):
                if not small:
                    for n in range(hb):
                        wait(act, k_made, hb * b + n + 1)
                        dst = kblk[64:128, 8 * n:8 * n + 8, :].rearrange("p (t r) d -> p t r d", r=2)[:, :, 1, :]
                        nc.scalar.activation(dst, pj[bank_of("k", n)][64:128, :].rearrange("p (t d) -> p t d", t=4),
                                             ACT.Copy).then_inc(k_kept2, 1)

            def keep_o(b):
                wait(act, attended, nq * (b + 1))
                wait(act, projected, b)
                for n in range(hb):
                    w = min(4, nt)
                    dst = oT[:, 4 * n:4 * n + w, :].rearrange("p t d -> p (t d)")
                    if small:
                        nc.scalar.activation(dst, ov[n][:, 0:w * P], ACT.Identity, bias=bv[:, 0:1]).then_inc(o_kept, 1)
                    else:
                        nc.scalar.activation(dst, ov[n][:, 0:w * P], ACT.Copy).then_inc(o_kept, 1)

            def body(b):
                final = isinstance(b, int) and b == NB - 1
                for j in range(nq):
                    if j == nq - lag and not final:
                        keep_k(b + 1)
                    if j < nq - lag:
                        exps(b, j + lag)
                    elif not final:
                        exps(b + 1, j + lag - nq)
                keep_o(b)

            act.wait_ge(zeroed, 2)
            for s, n in weights:
                act.wait_ge(s, n)
            keep_k(0)
            for j in range(lag):
                exps(0, j)
            loop(act, 0, body, NB - 1)



def normalise(K, name, logits=None, wr=None, n=0, weights=()):
    nc = K.nc
    turned_ps, logit_ps = K.bank[0:2], K.bank[2:4]
    with ExitStack() as ctx:
        def sb(s, shape, dt=F32):
            return ctx.enter_context(nc.sbuf_tensor(f"{name}_{s}", shape, dt))

        def sem(s):
            return K.sem(f"{name}_{s}")

        st, mv = sb("st", [P, GB, 6]), sb("mv", [P, GB, 2])
        ve, rs, xn = sb("ve", [P, GB]), sb("rs", [P, GB]), sb("xn", [P, GB, P])
        xg, carrier = sb("xg", [P, GB, P]), sb("carrier", [P, 1])
        stats, aggregated, varied, rooted = sem("stats"), sem("aggregated"), sem("varied"), sem("rooted")
        normed, turned, kept, copied = sem("normed"), sem("turned"), sem("kept"), sem("copied")
        multiplied, saved = sem("multiplied"), sem("saved")
        block = ctx.enter_context(nc.Block())

        @block.tensor
        def _(pe):
            for s, c in weights:
                pe.wait_ge(s, c)
            def group(g):
                wait(pe, normed, g + 1)
                wait(pe, kept, g)
                for i in range(GB):
                    mm = pe.transpose(turned_ps[0][:, i * P:(i + 1) * P], xn[:, i, :], K.ident[:, :])
                mm.then_inc(turned, 1)
                if wr is not None:
                    wait(pe, kept, g + 1)
                    wait(pe, saved, g)
                    for i in range(GB):
                        mm = pe.matmul(logit_ps[0][:, 32 * i:32 * i + n], xg[:, i, :], wr, start=True, stop=True)
                    mm.then_inc(multiplied, 1)

            loop_groups(pe, group)

        @block.vector
        def _(dve):
            def group(g):
                for i in range(GB):
                    last = nc.vector.bn_stats(st[:, i, :],
                                              K.x[:, bass.ds(g * GB + i, 1), :].rearrange("p a d -> p (a d)"))
                last.then_inc(stats, 1)
                wait(dve, stats, g + 1)
                nc.vector.memset(carrier[:, :], 0.0)
                for i in range(GB):
                    last = nc.vector.bn_aggr(mv[:, i, :], st[:, i, :])
                last.then_inc(aggregated, 1)
                wait(dve, aggregated, g + 1)
                nc.vector.tensor_scalar(ve[:, :], mv[:, :, 1], EPS, None, ALU.add).then_inc(varied, 1)
                wait(dve, rooted, g + 1)
                wait(dve, turned, g)
                for i in range(GB):
                    last = nc.vector.tensor_scalar(
                        xn[:, i, :], K.x[:, bass.ds(g * GB + i, 1), :].rearrange("p a d -> p (a d)"),
                        mv[:, i, 0:1], rs[:, i:i + 1], ALU.subtract, ALU.mult)
                last.then_inc(normed, 1)
                wait(dve, turned, g + 1)
                wait(dve, copied, g)
                if wr is not None:
                    wait(dve, multiplied, g)
                nc.vector.tensor_copy(xg[:, :, :].rearrange("p i t -> p (i t)"), turned_ps[0][:, :]).then_inc(kept, 1)
                if wr is not None:
                    wait(dve, multiplied, g + 1)
                    nc.vector.tensor_copy(logits[:, bass.ds(g * GB, GB), :],
                                          logit_ps[0][:, 0:P].rearrange("p (i e) -> p i e", i=GB)[:, :, 0:n]).then_inc(saved, 1)

            loop_groups(dve, group)

        @block.gpsimd
        def _(pool):
            def group(g):
                wait(pool, varied, g + 1)
                nc.gpsimd.tensor_tensor(rs[:, :], ve[:, :], K.mhalf4[:, :], ALU.pow).then_inc(rooted, 1)
                wait(pool, kept, g + 1)
                nc.gpsimd.tensor_copy(K.xT[:, bass.ds(g * GB * P, GB * P)],
                                      xg[:, :, :].rearrange("p i t -> p (i t)")).then_inc(copied, 1)

            loop_groups(pool, group)


def route(K, name, logits, gates, experts, shared, gT=None, b2=None, weights=()):
    nc = K.nc
    E = experts
    with ExitStack() as ctx:
        def sb(s, shape, dt=F32):
            return ctx.enter_context(nc.sbuf_tensor(f"{name}_{s}", shape, dt))

        def sem(s):
            return K.sem(f"{name}_{s}")

        e, prob = sb("e", [P, NB, E]), sb("prob", [P, NB, E])
        z, mx, tot = sb("z", [P, NB]), sb("mx", [P, NB]), sb("tot", [P, NB])
        top, idx, idxf = sb("top", [P, NB, 8]), sb("idx", [P, NB, 8], U32), sb("idxf", [P, NB, 8])
        hot0, hot1 = sb("hot0", [P, NB, E]), sb("hot1", [P, NB, E])
        chain, shifted, exped, routed = sem("chain"), sem("shifted"), sem("exped"), sem("routed")
        turned, kept, biased, added = sem("turned"), sem("kept"), sem("biased"), sem("added")
        gTf = sb("gTf", [E, GB * P]) if b2 is not None else None
        block = ctx.enter_context(nc.Block())

        def over(t):
            return t.unsqueeze(2).to_broadcast([P, NB, E])

        @block.scalar
        def _(act):
            if shared:
                act.wait_ge(shifted, 1)
                nc.scalar.activation(z[:, :], logits[:, :, E], ACT.Exp, scale=-1.0)
                nc.scalar.activation(prob[:, :, :], e[:, :, :], ACT.Exp).then_inc(exped, 1)
            else:
                nc.scalar.activation(e[:, :, :], logits[:, :, :], ACT.Exp, scale=-1.0).then_inc(exped, 1)

        @block.vector
        def _(dve):
            done = [0]

            def link(ins):
                done[0] += 1
                ins.then_inc(chain, 1)
                dve.wait_ge(chain, done[0])

            if shared:
                link(nc.vector.tensor_reduce(mx[:, :], logits[:, :, 0:E], AX.X, ALU.max))
                nc.vector.tensor_tensor(e[:, :, :], logits[:, :, 0:E], over(mx[:, :]), ALU.subtract).then_inc(shifted, 1)
                dve.wait_ge(exped, 1)
                link(nc.vector.tensor_reduce(tot[:, :], prob[:, :, :], AX.X, ALU.add))
                link(nc.vector.reciprocal(mx[:, :], tot[:, :]))
                link(nc.vector.tensor_tensor(prob[:, :, :], prob[:, :, :], over(mx[:, :]), ALU.mult))
            else:
                dve.wait_ge(exped, 1)
                link(nc.vector.tensor_scalar(e[:, :, :], e[:, :, :], 1.0, None, ALU.add))
                link(nc.vector.reciprocal(prob[:, :, :], e[:, :, :]))
            for b in range(NB):
                last = nc.vector.max(top[:, b, :], prob[:, b, :])
            link(last)
            for b in range(NB):
                last = nc.vector.max_index(idx[:, b, :], top[:, b, :], prob[:, b, :])
            link(last)
            link(nc.vector.tensor_copy(idxf[:, :, :], idx[:, :, :]))
            iota = K.iota[:, 0:E].unsqueeze(1).to_broadcast([P, NB, E])
            nc.vector.tensor_tensor(hot0[:, :, :], iota, over(idxf[:, :, 0]), ALU.is_equal)
            nc.vector.tensor_tensor(tot[:, :], top[:, :, 0], top[:, :, 1], ALU.add)
            link(nc.vector.tensor_tensor(hot1[:, :, :], iota, over(idxf[:, :, 1]), ALU.is_equal))
            nc.vector.reciprocal(mx[:, :], tot[:, :])
            link(nc.vector.tensor_tensor(hot0[:, :, :], hot0[:, :, :], hot1[:, :, :], ALU.add))
            link(nc.vector.tensor_tensor(hot0[:, :, :], hot0[:, :, :], prob[:, :, :], ALU.mult))
            last = nc.vector.tensor_tensor(gates[:, :, 0:E], hot0[:, :, :], over(mx[:, :]), ALU.mult)
            if shared:
                link(nc.vector.tensor_scalar(z[:, :], z[:, :], 1.0, None, ALU.add))
                last = nc.vector.reciprocal(gates[:, :, E], z[:, :])
            last.then_inc(routed, 1)
            for g in range(NG):
                dve.wait_ge(turned, g + 1)
                if gT is not None:
                    nc.vector.tensor_copy(gT[:, g * GB * P:(g + 1) * GB * P], K.bank[g % 2][0:G0, :]).then_inc(kept, 1)
                if b2 is not None:
                    nc.vector.tensor_copy(gTf[:, :], K.bank[g % 2][0:E, :]).then_inc(kept, 1)
                    dve.wait_ge(biased, g + 1)
                    xg = K.x[:, GB * g:GB * g + GB, :].rearrange("p i d -> p (i d)")
                    nc.vector.tensor_tensor(xg, K.bank[2 + g % 2][:, :], xg, ALU.add).then_inc(added, 1)

        @block.tensor
        def _(pe):
            for s, c in weights:
                pe.wait_ge(s, c)
            pe.wait_ge(routed, 1)
            n = E + 1 if shared else E
            for g in range(NG):
                wait(pe, kept, g - 1)
                for i in range(GB):
                    mm = pe.transpose(K.bank[g % 2][0:n, i * P:(i + 1) * P], gates[:, GB * g + i, :], K.ident[:, :])
                mm.then_inc(turned, 1)
                if b2 is not None:
                    pe.wait_ge(kept, g + 1)
                    wait(pe, added, g - 1)
                    for i in range(GB):
                        mm = pe.matmul(K.bank[2 + g % 2][:, i * P:(i + 1) * P], gTf[:, i * P:(i + 1) * P], b2,
                                       start=True, stop=True)
                    mm.then_inc(biased, 1)


def shared_mixture(K, name, gT, w_gate, w_up, w_down, sel, weights=()):
    nc = K.nc
    gate_ps, up_ps, spread_ps, down_ps = K.bank[0:2], K.bank[2:4], K.bank[4:6], K.bank[6]
    W = GB * P
    with ExitStack() as ctx:
        def sb(s, shape, dt=F32):
            return ctx.enter_context(nc.sbuf_tensor(f"{name}_{s}", shape, dt))

        def sem(s):
            return K.sem(f"{name}_{s}")

        silu, prod, hT = sb("silu", [P, 2, W]), sb("prod", [P, 2, W]), sb("hT", [P, NC0, W])
        gated, raised, spread, silued, produced, hidden, lowered, added = (
            sem(s) for s in ("gated", "raised", "spread", "silued", "produced", "hidden", "lowered", "added"))
        block = ctx.enter_context(nc.Block())

        @block.tensor
        def _(pe):
            for s, c in weights:
                pe.wait_ge(s, c)
            def group(g):
                xg = K.xT[:, bass.ds(g * W, W)]
                for c in range(NC0):
                    i = NC0 * g + c
                    cols = slice(c * P, (c + 1) * P)
                    if c >= 2:
                        wait(pe, silued, i - 1)
                        wait(pe, hidden, i - 1)
                    else:
                        wait(pe, hidden, NC0 * g)
                    pe.matmul(gate_ps[c % 2][:, :], w_gate[:, cols], xg, start=True, stop=True).then_inc(gated, 1)
                    pe.matmul(up_ps[c % 2][:, :], w_up[:, cols], xg, start=True, stop=True).then_inc(raised, 1)
                    pe.matmul(spread_ps[c % 2][:, :], sel[:, cols], gT[:, bass.ds(g * W, W)],
                              start=True, stop=True).then_inc(spread, 1)
                wait(pe, hidden, NC0 * (g + 1))
                wait(pe, added, g)
                for b in range(GB):
                    for c in range(NC0):
                        mm = pe.matmul(down_ps[:, b * P:(b + 1) * P], hT[:, c, b * P:(b + 1) * P], w_down[:, c, :],
                                       start=c == 0, stop=c == NC0 - 1)
                mm.then_inc(lowered, 1)

            loop_groups(pe, group)

        @block.scalar
        def _(act):
            def group(g):
                for c in range(NC0):
                    i = NC0 * g + c
                    wait(act, gated, i + 1)
                    if c >= 2:
                        wait(act, produced, i - 1)
                    else:
                        wait(act, produced, NC0 * g)
                    nc.scalar.activation(silu[:, c % 2, :], gate_ps[c % 2][:, :], ACT.Silu).then_inc(silued, 1)

            loop_groups(act, group)

        @block.vector
        def _(dve):
            def group(g):
                for c in range(NC0):
                    i = NC0 * g + c
                    wait(dve, silued, i + 1)
                    wait(dve, raised, i + 1)
                    if c >= 2:
                        wait(dve, hidden, i - 1)
                    else:
                        wait(dve, hidden, NC0 * g)
                    nc.vector.tensor_tensor(prod[:, c % 2, :], silu[:, c % 2, :], up_ps[c % 2][:, :],
                                            ALU.mult).then_inc(produced, 1)
                    wait(dve, produced, i + 1)
                    wait(dve, spread, i + 1)
                    if c == 0:
                        wait(dve, lowered, g)
                    nc.vector.tensor_tensor(hT[:, c, :], prod[:, c % 2, :], spread_ps[c % 2][:, :],
                                            ALU.mult).then_inc(hidden, 1)
                wait(dve, lowered, g + 1)
                xg = K.x[:, bass.ds(g * GB, GB), :]
                nc.vector.tensor_tensor(xg, down_ps[:, :].rearrange("p (i d) -> p i d", i=GB), xg,
                                        ALU.add).then_inc(added, 1)

            loop_groups(dve, group)


def mixture(K, name, gates, w1, b1, w2, out, stored, weights=()):
    nc = K.nc
    W = GB * P
    NF = 4
    up_ps, down_ps = K.bank[0:4], K.bank[4:6]
    with ExitStack() as ctx:
        def sb(s, shape, dt=F32):
            return ctx.enter_context(nc.sbuf_tensor(f"{name}_{s}", shape, dt))

        def sem(s):
            return K.sem(f"{name}_{s}")

        hT = sb("hT", [P, 2, NF, W])
        raised, hidden, lowered, added = (sem(s) for s in ("raised", "hidden", "lowered", "added"))
        block = ctx.enter_context(nc.Block())

        @block.tensor
        def _(pe):
            def up(g, e):
                for f in range(NF):
                    i = (g * E1 + e) * NF + f
                    if e:
                        pe.wait_ge(hidden, i - 3)
                    else:
                        pe.wait_ge(hidden, g * (E1 * NF))
                    pe.matmul(up_ps[f][:, :], w1[:, (e * NF + f) * P:(e * NF + f + 1) * P],
                              K.xT[:, bass.ds(g * W, W)], start=True, stop=True).then_inc(raised, 1)

            def down(g, e):
                pe.wait_ge(hidden, (g * E1 + e + 1) * NF)
                if e >= 2:
                    pe.wait_ge(added, g * (E1 * GB) + (e - 1) * GB)
                else:
                    pe.wait_ge(added, g * (E1 * GB))
                for b in range(GB):
                    for f in range(NF):
                        mm = pe.matmul(down_ps[e % 2][:, b * P:(b + 1) * P], hT[:, e % 2, f, b * P:(b + 1) * P],
                                       w2[:, e * NF + f, :], start=f == 0, stop=f == NF - 1)
                mm.then_inc(lowered, 1)

            for s, c in weights:
                pe.wait_ge(s, c)
            def group(g):
                up(g, 0)
                for e in range(E1):
                    if e + 1 < E1:
                        up(g, e + 1)
                    down(g, e)

            loop_groups(pe, group)

        @block.scalar
        def _(act):
            for s, c in weights:
                act.wait_ge(s, c)
            def group(g):
                for e in range(E1):
                    if e >= 2:
                        wait(act, lowered, g * E1 + e - 1)
                    else:
                        wait(act, lowered, g * E1)
                    for f in range(NF):
                        wait(act, raised, (g * E1 + e) * NF + f + 1)
                        nc.scalar.activation(hT[:, e % 2, f, :], up_ps[f][:, :], ACT.Gelu,
                                             bias=b1[:, e * NF + f:e * NF + f + 1]).then_inc(hidden, 1)

            loop_groups(act, group)

        @block.vector
        def _(dve):
            def group(g):
                for e in range(E1):
                    wait(dve, lowered, g * E1 + e + 1)
                    for b in range(GB):
                        if e:
                            wait(dve, added, (g * E1 + e - 1) * GB + b + 1)
                        xb = K.x[:, bass.ds(g * GB + b, 1), :].rearrange("p a d -> p (a d)")
                        nc.vector.scalar_tensor_tensor(
                            out=xb, in0=down_ps[e % 2][:, b * P:(b + 1) * P],
                            scalar=gates[:, bass.ds(g * GB + b, 1), e:e + 1].rearrange("p a e -> p (a e)"),
                            in1=xb, op0=ALU.mult, op1=ALU.add).then_inc(added, 1)

            loop_groups(dve, group)

        @block.sync
        def _(sp):
            def group(g):
                wait(sp, added, (g + 1) * (E1 * GB))
                sp.dma_start(out[bass.ds(g * GB, GB), :, :].rearrange("b t d -> t b d"),
                             K.x[:, bass.ds(g * GB, GB), :]).then_inc(stored, 16)

            loop_groups(sp, group)
            sp.wait_ge(stored, 16 * NG)


def standardised_attention(K, name, wq, wk, wv, wo, weights=()):
    nc = K.nc
    W = GB * P
    with ExitStack() as ctx:
        def sb(s, shape, dt=F32):
            return ctx.enter_context(nc.sbuf_tensor(f"{name}_{s}", shape, dt))

        def sem(s):
            return K.sem(f"{name}_{s}")

        cg = sb("cg", [CTX, W])
        qT, kT, v = sb("qT", [P, W]), sb("kT", [P, W]), sb("v", [P, W])
        st, mv, means, dev, vp = (sb("st", [P, GB, 6]), sb("mv", [P, GB, 2]), sb("means", [P, GB]),
                                  sb("dev", [P, GB]), sb("vp", [P, GB]))
        ve, rs, negmax, shift, tot, rtot = (sb(s, [P, GB]) for s in ("ve", "rs", "negmax", "shift", "tot", "rtot"))
        p, pT, oT = sb("p", [P, W]), sb("pT", [P, W]), sb("oT", [P, W])
        copied, made, kept, scored, spread = sem("copied"), sem("made"), sem("kept"), sem("scored"), sem("spread")
        chain, rooted, exped, turned, attended, projected = (
            sem(s) for s in ("chain", "rooted", "exped", "turned", "attended", "projected"))
        okept = sem("okept")
        block = ctx.enter_context(nc.Block())
        CH = 16

        def part(t, i):
            return t[:, i * P:(i + 1) * P]

        @block.gpsimd
        def _(pool):
            def group(g):
                wait(pool, made, 3 * g)
                nc.gpsimd.tensor_copy(cg[:, :], K.ctxT[:, bass.ds(g * GB, GB), :].rearrange("p i t -> p (i t)")).then_inc(copied, 1)
                wait(pool, chain, CH * g + 8)
                nc.gpsimd.tensor_tensor(rs[:, :], ve[:, :], K.mhalf4[:, :], ALU.pow).then_inc(rooted, 1)

            loop_groups(pool, group)

        @block.tensor
        def _(pe):
            for s, c in weights:
                pe.wait_ge(s, c)
            def group(g):
                wait(pe, copied, g + 1)
                wait(pe, chain, CH * g)
                pe.matmul(K.bank[0][:, :], wq, K.xT[:, bass.ds(g * W, W)], start=True, stop=True).then_inc(made, 1)
                pe.matmul(K.bank[1][:, :], wk, cg[:, :], start=True, stop=True).then_inc(made, 1)
                for i in range(GB):
                    mm = pe.matmul(part(K.bank[2], i), part(cg, i), wv, start=True, stop=True)
                mm.then_inc(made, 1)
                wait(pe, kept, 2 * g + 2)
                for i in range(GB):
                    mm = pe.matmul(part(K.bank[3], i), part(qT, i), part(kT, i), start=True, stop=True)
                mm.then_inc(scored, 1)
                wait(pe, chain, CH * g + 4)
                pe.matmul(K.bank[4][:, 0:GB], K.mean[:, :], means[:, :], start=True, stop=True).then_inc(spread, 1)
                wait(pe, chain, CH * g + 7)
                pe.matmul(K.bank[4][:, 8:8 + GB], K.mean[:, :], vp[:, :], start=True, stop=True).then_inc(spread, 1)
                wait(pe, chain, CH * g + 12)
                for i in range(GB):
                    mm = pe.transpose(part(K.bank[5], i), part(p, i), K.ident[:, :])
                mm.then_inc(turned, 1)
                wait(pe, chain, CH * g + 13)
                for i in range(GB):
                    mm = pe.matmul(part(K.bank[6], i), part(v, i), part(pT, i), start=True, stop=True)
                mm.then_inc(attended, 1)
                wait(pe, okept, g + 1)
                for i in range(GB):
                    mm = pe.matmul(part(K.bank[7], i), part(oT, i), wo, start=True, stop=True)
                mm.then_inc(projected, 1)

            loop_groups(pe, group)

        @block.scalar
        def _(act):
            def group(g):
                wait(act, made, 3 * g + 1)
                nc.scalar.activation(qT[:, :], K.bank[0][:, :], ACT.Copy).then_inc(kept, 1)
                wait(act, made, 3 * g + 2)
                nc.scalar.activation(kT[:, :], K.bank[1][:, :], ACT.Copy).then_inc(kept, 1)
                wait(act, chain, CH * g + 10)
                for i in range(GB):
                    e = nc.scalar.activation(part(p, i), part(K.bank[3], i), ACT.Exp, bias=shift[:, i:i + 1],
                                             scale=rs[:, i:i + 1], accum_out=tot[:, i:i + 1])
                e.then_inc(exped, 1)
                wait(act, attended, g + 1)
                nc.scalar.activation(oT[:, :], K.bank[6][:, :], ACT.Copy).then_inc(okept, 1)

            loop_groups(act, group)

        @block.vector
        def _(dve):
            def group(g):
                step = [0]

                def link(ins):
                    step[0] += 1
                    ins.then_inc(chain, 1)
                    wait(dve, chain, CH * g + step[0])

                wait(dve, made, 3 * g + 3)
                link(nc.vector.tensor_copy(v[:, :], K.bank[2][:, :]))
                wait(dve, scored, g + 1)
                for i in range(GB):
                    last = nc.vector.bn_stats(st[:, i, :], part(K.bank[3], i))
                link(last)
                nc.vector.memset(dev[:, :], 0.0)
                for i in range(GB):
                    last = nc.vector.bn_aggr(mv[:, i, :], st[:, i, :])
                link(last)
                link(nc.vector.tensor_copy(means[:, :], mv[:, :, 0]))
                wait(dve, spread, 2 * g + 1)
                link(nc.vector.tensor_tensor(dev[:, :], means[:, :], K.bank[4][:, 0:GB], ALU.subtract))
                link(nc.vector.tensor_tensor(dev[:, :], dev[:, :], dev[:, :], ALU.mult))
                link(nc.vector.tensor_tensor(vp[:, :], dev[:, :], mv[:, :, 1], ALU.add))
                wait(dve, spread, 2 * g + 2)
                link(nc.vector.tensor_scalar(ve[:, :], K.bank[4][:, 8:8 + GB], EPS, None, ALU.add))
                link(nc.vector.tensor_reduce(negmax[:, :], K.bank[3][:, :].rearrange("p (i k) -> p i k", i=GB),
                                             AX.X, ALU.max, negate=True))
                wait(dve, rooted, g + 1)
                link(nc.vector.tensor_tensor(shift[:, :], negmax[:, :], rs[:, :], ALU.mult))
                wait(dve, exped, g + 1)
                link(nc.vector.reciprocal(rtot[:, :], tot[:, :]))
                p4 = p[:, :].rearrange("p (i k) -> p i k", i=GB)
                link(nc.vector.tensor_tensor(p4, p4, rtot[:, :].unsqueeze(2).to_broadcast([P, GB, P]), ALU.mult))
                wait(dve, turned, g + 1)
                link(nc.vector.tensor_copy(pT[:, :], K.bank[5][:, :]))
                wait(dve, projected, g + 1)
                xg = K.x[:, bass.ds(g * GB, GB), :]
                link(nc.vector.tensor_tensor(xg, K.bank[7][:, :].rearrange("p (i d) -> p i d", i=GB), xg, ALU.add))
                last = nc.vector.memset(dev[:, 0:1], 0.0)
                link(last)
                link(nc.vector.memset(dev[:, 1:2], 0.0))
                assert step[0] == CH

            loop_groups(dve, group)


def decoder(nc, A, out, phases=7):
    K = Shared(nc)
    with ExitStack() as ctx:
        def sb(n, shape, dt=F32):
            return ctx.enter_context(nc.sbuf_tensor(n, shape, dt))

        def sem(n):
            return ctx.enter_context(nc.semaphore(n))

        K.bank = [ctx.enter_context(nc.psum_tensor(f"bank{i}", [P, 512], F32)) for i in range(8)]
        K.x = sb("x_sb", [P, NB, P])
        K.xT = sb("xT_all", [P, NB * P])
        K.ctxT = sb("ctxT_sb", [CTX, NB, P])
        K.ident, K.identb = sb("ident_sb", [P, P]), sb("identb", [P, P], BF16)
        mask, K.maskb = sb("mask_sb", [P, P]), sb("maskb", [P, 4, P], BF16)
        K.headmask, K.iota = sb("headmask_sb", [P, 16]), sb("iota_sb", [P, 16])
        K.ones, K.mean = sb("ones", [1, P]), sb("mean", [P, P])
        K.mhalf4 = sb("mhalf", [P, GB])
        K.mhalf = K.mhalf4[:, 0:1]
        logits0, gates0 = sb("logits0", [P, NB, G0]), sb("gates0", [P, NB, G0])
        logits1, gates1 = sb("logits1", [P, NB, E1]), sb("gates1", [P, NB, E1])
        gT = sb("gT", [G0, NB * P])
        K.x_loaded = [sem(f"x_loaded{g}") for g in range(NG)]
        consts_loaded, consts_made = sem("consts_loaded"), sem("consts_made")
        stored = sem("stored")
        w, loaded = {}, {}

        with nc.Block() as block:
            groups = {"self0": ["a_w", "a_b", "a_bo"], "cross0": ["c_wq", "c_wkv", "c_wo", "c_bo"],
                      "ffn0": ["f_wr", "f_wgu", "f_wd", "f_sel"], "self1": ["s_wqkv", "s_wo"],
                      "cross1": ["t_wqo", "t_wkv"], "ffn1": ["m_wr", "m_w1", "m_b1", "m_w2", "m_b2"]}
            for gname, names in groups.items():
                loaded[gname] = (sem(f"loaded_{gname}"), 16 * len(names))
                for n in names:
                    w[n] = sb(f"{n}_sb", list(A[n].shape))

            @block.sync
            def _(sp):
                for g in range(NG):
                    sp.dma_start(K.x[:, GB * g:GB * (g + 1), :],
                                 A["x"][GB * g:GB * (g + 1), :, :].rearrange("b t d -> t b d")).then_inc(K.x_loaded[g], 16)
                sp.dma_start(K.ctxT[:, :, :], A["ctxT"]).then_inc(loaded["cross0"][0], 16)
                for gname in ("ffn0", "self1", "ffn1"):
                    for n in groups[gname]:
                        sp.dma_start(w[n][:, :], A[n]).then_inc(loaded[gname][0], 16)

            @block.scalar
            def _(act):
                for n, t in (("ident", K.ident), ("mask", mask), ("headmask", K.headmask), ("iota", K.iota)):
                    act.dma_start(t[:, :], A[n]).then_inc(consts_loaded, 16)
                for gname in ("self0", "cross0", "cross1"):
                    for n in groups[gname]:
                        act.dma_start(w[n][:, :], A[n]).then_inc(loaded[gname][0], 16)

            @block.vector
            def _(dve):
                nc.vector.memset(K.ones[:, :], 1.0)
                nc.vector.memset(K.mean[:, :], 1.0 / P)
                nc.vector.memset(K.mhalf4[:, :], -0.5)
                dve.wait_ge(consts_loaded, 64)
                nc.vector.tensor_copy(K.identb[:, :], K.ident[:, :])
                nc.vector.tensor_copy(K.maskb[:, :, :], mask[:, :].unsqueeze(1).to_broadcast([P, 4, P])).then_inc(consts_made, 1)

        loaded["cross0"] = (loaded["cross0"][0], loaded["cross0"][1] + 16)
        a = w["a_w"]
        tiles = lambda t, n: t[:, :].rearrange("p (t d) -> p t d", t=n)
        attention(K, "self0", 16, 8, 3, True, False, a[:, 0:P], a[:, P:2 * P], a[:, 2 * P:3 * P],
                  tiles(a[:, 3 * P:4 * P], 1), w["a_b"][:, 0:1], w["a_b"][:, 1:2], w["a_b"][:, 2:3], w["a_bo"],
                  weights=[loaded["self0"]])
        K.clear()
        if phases > 1:
            c = w["c_wkv"]
            attention(K, "cross0", 8, 64, 2, False, True, w["c_wq"], c[:, 0:512], c[:, 512:1024],
                      tiles(w["c_wo"], 4), bo=w["c_bo"], weights=[loaded["cross0"]])
            K.clear()
        if phases > 2:
            normalise(K, "norm_ffn0", logits0, w["f_wr"][:, :], G0, weights=[loaded["ffn0"]])
            K.clear()
            route(K, "route0", logits0, gates0, E0, True, gT=gT)
            K.clear()
            u = w["f_wgu"]
            shared_mixture(K, "ffn0", gT, u[:, 0:NC0 * P], u[:, NC0 * P:2 * NC0 * P], tiles(w["f_wd"], NC0), w["f_sel"],
                           weights=[loaded["ffn0"]])
            K.clear()
        if phases > 3:
            s = w["s_wqkv"]
            attention(K, "self1", 16, 64, 3, True, False, s[:, 0:1024], s[:, 1024:2048], s[:, 2048:3072],
                      tiles(w["s_wo"], 8), weights=[loaded["self1"]])
            K.clear()
        if phases > 4:
            normalise(K, "norm_cross1")
            K.clear()
            t, r = w["t_wqo"], w["t_wkv"]
            standardised_attention(K, "cross1", t[:, 0:P], r[:, 0:P], r[:, P:2 * P], t[:, P:2 * P],
                                   weights=[loaded["cross1"]])
            K.clear()
        if phases > 5:
            normalise(K, "norm_ffn1", logits1, w["m_wr"][:, :], E1, weights=[loaded["ffn1"]])
            K.clear()
            route(K, "route1", logits1, gates1, E1, False, b2=w["m_b2"][:, :], weights=[loaded["ffn1"]])
            K.clear()
            mixture(K, "ffn1", gates1, w["m_w1"], w["m_b1"], tiles(w["m_w2"], 32), out, stored,
                    weights=[loaded["ffn1"]])
            K.clear()
        else:
            with nc.Block() as block:
                @block.sync
                def _(sp):
                    for q, n in loaded.values():
                        sp.wait_ge(q, n)
                    sp.dma_start(out.rearrange("b t d -> t b d"), K.x[:, :, :]).then_inc(stored, 16)
                    sp.wait_ge(stored, 16)


def layout(inputs):
    import numpy as np

    I = {k: np.asarray(v) for k, v in inputs.items()}

    def rows(a):
        return a.reshape(-1, P, a.shape[-1]).transpose(1, 0, 2).reshape(P, -1)

    L = {"x": I["x"], "ctxT": I["ctx_768"].transpose(2, 0, 1)}
    L["a_w"] = np.concatenate([I["L0_attn_" + n].T for n in ("Wq", "Wk", "Wv", "Wo")], 1)
    L["a_b"] = np.stack([I["L0_attn_" + n] for n in ("bq", "bk", "bv")], 1)
    L["a_bo"] = I["L0_attn_bo"][None, :]
    L["c_wq"] = I["L0_xattn_Wq"]
    L["c_wkv"] = np.concatenate([I["L0_xattn_Wk"], I["L0_xattn_Wv"]], 1)
    L["c_wo"] = rows(I["L0_xattn_Wo"])
    L["c_bo"] = I["L0_xattn_bo"][None, :]
    L["f_wr"] = np.concatenate([I["L0_ffn_Wg"], I["L0_ffn_Wsg"]], 0).T
    L["f_wgu"] = np.concatenate([I["L0_ffn_We_gate"].reshape(-1, P), I["L0_ffn_Ws_gate"],
                                 I["L0_ffn_We_up"].reshape(-1, P), I["L0_ffn_Ws_up"]], 0).T
    L["f_wd"] = rows(np.concatenate([I["L0_ffn_We_down"].transpose(0, 2, 1).reshape(-1, P), I["L0_ffn_Ws_down"].T], 0))
    L["s_wqkv"] = np.concatenate([I["L1_attn_" + n].reshape(-1, P) for n in ("W_Q", "W_K", "W_V")], 0).T
    L["s_wo"] = rows(I["L1_attn_W_O"].T)
    L["t_wqo"] = np.concatenate([I["L1_xattn_Wq"].T, I["L1_xattn_Wo"].T], 1)
    L["t_wkv"] = np.concatenate([I["L1_xattn_Wk"].T, I["L1_xattn_Wv"].T], 1)
    L["m_wr"] = I["L1_ffn_centroids"].T
    L["m_w1"] = I["L1_ffn_W1"].transpose(1, 0, 2).reshape(P, -1)
    L["m_b1"] = I["L1_ffn_b1"].reshape(-1, P).T
    L["m_w2"] = rows(I["L1_ffn_W2"].reshape(-1, P))
    L["m_b2"] = I["L1_ffn_b2"]
    i = np.arange(P)
    L["ident"] = np.eye(P, dtype=np.float32)
    L["mask"] = np.where(i[None, :] <= i[:, None], 0.0, NEG).astype(np.float32)
    L["headmask"] = (i[:, None] // 8 == np.arange(16)[None, :]).astype(np.float32)
    L["iota"] = np.tile(np.arange(16, dtype=np.float32), (P, 1))
    unit = np.arange(NC0 * P)
    L["f_sel"] = (np.minimum(unit // 64, E0)[None, :] == np.arange(G0)[:, None]).astype(np.float32)
    return {k: np.ascontiguousarray(v) for k, v in L.items()}


def kernel(**inputs):
    import concourse.bacc as bacc
    from concourse.bass_utils import run_bass_kernel_spmd

    nc = bacc.Bacc("TRN2", target_bir_lowering=False, num_devices=1)
    arrays, aps = {}, {}
    for name, a in layout(inputs).items():
        arrays[f"in_{name}"] = a
        aps[name] = nc.dram_tensor(f"in_{name}", a.shape, mybir.dt.from_np(a.dtype), kind="ExternalInput").ap()
    out = nc.dram_tensor("out", (NB, P, P), F32, kind="ExternalOutput").ap()
    decoder(nc, aps, out)
    r = run_bass_kernel_spmd(nc, [arrays], core_ids=[0])
    return r.results[0]["out"]
```

```python
from contextlib import ExitStack

import concourse.bass as bass
from concourse import mybir

F32 = mybir.dt.float32
BF16 = mybir.dt.bfloat16
F32R = mybir.dt.float32r
U32 = mybir.dt.uint32
ALU = mybir.AluOpType
ACT = mybir.ActivationFunctionType
AX = mybir.AxisListType

P = 128
NB = 16
CTX = 96
GB = 4
NG = NB // GB
EPS = 1e-5
NEG = -1e30
FLT_MAX = 3e38
E0, E1 = 16, 8
NC0 = 10
G0 = E0 + 1


def wait(eng, sem, value):
    if isinstance(value, int) and value <= 0:
        return
    eng.wait_ge(sem, value)


def seq(b):
    return slice(b, b + 1) if isinstance(b, int) else bass.ds(b, 1)


class Shared:

    def __init__(self, nc):
        self.nc, self.phase_sems, self.cleared = nc, [], []

    def sem(self, name):
        self.phase_sems.append(self.nc.alloc_semaphore(name))
        return self.phase_sems[-1]

    def clear(self):
        for s in self.cleared:
            self.nc.release_semaphore(s)
        for s in self.phase_sems:
            self.nc.gpsimd.sem_clear(s)
        self.phase_sems, self.cleared = [], self.phase_sems


class At:

    def __init__(self, n, par, pairs):
        self.n, self.par, self.pairs = n, par, pairs

    def __add__(self, k):
        return At(self.n + k, (self.par + k) % 2, self.pairs + (self.par + k) // 2)

    def __sub__(self, k):
        return self + -k

    def inside(self):
        return not isinstance(self.n, int) or 0 <= self.n < NB


def pipeline(eng, body):
    for n in range(-2, 2):
        body(At(n, n % 2, n // 2))
    with eng.Fori(1, NB // 2 - 1) as k:
        body(At(2 * k, 0, k))
        body(At(2 * k + 1, 1, k))
    for n in range(NB - 2, NB + 1):
        body(At(n, n % 2, n // 2))


def follows(g):
    return not isinstance(g, int) or g > 0


def loop_groups(eng, body):
    body(0)
    with eng.Fori(1, NG) as g:
        body(g)


def attention(K, name, heads, hd, causal, wq, wk, wv, wo, bq=None, bk=None, bv=None, bo=None,
              p_on_act=False, ctxT=None, weights=(), later=(), kblk=None, v=None, clean=None,
              masked_max=False):
    nc, cross = K.nc, ctxT is not None
    nt = heads * hd // P
    nq = heads // 4
    hb = max(1, nt // 4)
    small = hd < 64
    scale = float(hd) ** -0.5
    sc, tr, ov = K.bank[2:4], K.bank[4:6], K.bank[6:8]
    if cross:
        order = {"v": 0, "x": 1, "k": 0, "q": 1, "o": 0}
    else:
        order = {"k": 0, "v": 1, "o": 0, "x": 1, "q": 0} if hb == 1 else {"k": 0, "v": 0, "o": 0, "x": 1, "q": 0}

    def bank_of(use, n=0):
        return K.bank[order[use] + n]

    with ExitStack() as ctx:
        def sb(n, shape, dt=F32):
            return ctx.enter_context(nc.sbuf_tensor(f"{name}_{n}", shape, dt))

        def sem(n):
            return K.sem(f"{name}_{n}")

        st, mv, ve, rs = sb("st", [P, 6]), sb("mv", [P, 2]), sb("ve", [P, 1]), sb("rs", [P, 1])
        carrier, carriers = sb("carrier", [P, 1]), sb("carriers", [P, 4, 2])
        xn, xT = sb("xn", [P, P]), sb("xT", [P, 2, P])
        kT = sb("kT", [P, 2, P]) if small else None
        cb = sb("cb", [P, 2, P]) if cross else xT
        qT = sb("qT", [P, 2, nt, P])
        kblk = sb("kblk", [P, 2, heads, P]) if small else kblk
        v = v if small else sb("v", [P, 2, nt * P])
        p = sb("p", [P, 4, 4, P])
        pT = sb("pT", [P, 2, 4, P])
        oT = sb("oT", [P, nt, P])
        negmax, total, rtotal = sb("negmax", [P, 4, 4]), sb("total", [P, 4, 4]), sb("rtotal", [P, 4, 4])

        stats, rooted = sem("stats"), sem("rooted")
        normed, turned, x_turned = sem("normed"), sem("turned"), sem("x_turned")
        ctx_loaded = [sem("ctx_loaded0"), sem("ctx_loaded1")]
        q_made, k_made, v_made = sem("q_made"), sem("k_made"), sem("v_made")
        q_kept, k_kept, k_kept2, v_kept = sem("q_kept"), sem("k_kept"), sem("k_kept2"), sem("v_kept")
        k_spread = [sem("k_spread0"), sem("k_spread1")]
        scored, maxed, exped, inverted, scaled = (sem(n) for n in ("scored", "maxed", "exped", "inverted", "scaled"))
        p_turned, attended, o_kept, projected, added = (
            sem(n) for n in ("p_turned", "attended", "o_kept", "projected", "added"))
        p_kept = [sem("p_kept0"), sem("p_kept1")]
        block = ctx.enter_context(nc.Block())

        def quad(b, j):
            return nq * b.n + j

        def slot(b, j):
            return j if nq == 4 else 2 * b.par + j

        def kept_p(b, j):
            return (nq // 2) * b.n + j // 2 + 1

        def last_use(eng, use, b):
            if cross:
                {"v": lambda: (wait(eng, added, b.n - 2), keys(eng, b)), "x": lambda: wait(eng, q_kept, b.n),
                 "k": lambda: wait(eng, v_kept, b.n), "q": lambda: None,
                 "o": lambda: (keys(eng, b + 3), wait(eng, v_kept, min_seq(b.n + 3)))}[use]()
            elif hb == 1:
                {"k": lambda: wait(eng, q_kept, min_seq(b.n + 1)), "v": lambda: wait(eng, x_turned, min_seq(b.n + 1)),
                 "o": lambda: keys(eng, b + 2), "x": lambda: wait(eng, v_kept, b.n),
                 "q": lambda: (wait(eng, added, b.n - 2), keys(eng, b - 1))}[use]()
            else:
                {"k": lambda: wait(eng, q_kept, 2 * min_seq(b.n + 1)), "v": lambda: keys(eng, b),
                 "o": lambda: wait(eng, v_kept, 2 * min_seq(b.n + 3)), "x": lambda: wait(eng, v_kept, 2 * b.n),
                 "q": lambda: (wait(eng, added, b.n - 2), wait(eng, v_kept, 2 * b.n - 1),
                               wait(eng, x_turned, b.n + 1))}[use]()

        def min_seq(n):
            return min(n, NB) if isinstance(n, int) else n

        def keys(eng, b):
            n = min_seq(b.n + 1)
            wait(eng, k_kept, hb * n)
            if not small:
                wait(eng, k_kept2, hb * n)

        def body(b, make_k, spread_k, make_v, make_q, turn_x, project, score, turn_p, attend, stats_x, norm_x):
            if nq == 4:
                score(b, 2)
                stats_x(b + 2)
                turn_p(b, 0)
                make_k(b + 1)
                spread_k(b + 1, 0)
                attend(b - 1, 3)
                score(b, 3)
                spread_k(b + 1, 1)
                norm_x(b + 2)
                turn_p(b, 1)
                make_v(b + 1)
                attend(b, 0)
                score(b + 1, 0)
                spread_k(b + 1, 2)
                turn_p(b, 2)
                project(b - 1)
                turn_x(b + 2)
                attend(b, 1)
                score(b + 1, 1)
                spread_k(b + 1, 3)
                turn_p(b, 3)
                make_q(b + 2)
                attend(b, 2)
            else:
                score(b + 1, 0)
                stats_x(b + 2)
                turn_p(b, 0)
                make_v(b + 1)
                norm_x(b + 2)
                attend(b - 1, 1)
                score(b + 1, 1)
                turn_x(b + 2)
                turn_p(b, 1)
                make_k(b + 2)
                make_q(b + 2)
                attend(b, 0)
                project(b - 1)

        def run(eng, **steps):
            def checked(step):
                return (lambda b, *j: b.inside() and step(b, *j)) if step else (lambda *_: None)

            names = ("make_k", "spread_k", "make_v", "make_q", "turn_x", "project", "score", "turn_p", "attend", "stats_x", "norm_x")
            assert set(steps) <= set(names)
            pipeline(eng, lambda b: body(b, **{n: checked(steps.get(n)) for n in names}))

        def spread_keys(eng, ops, b, j):
            wait(eng, k_kept, b.n + 1)
            heads4 = slice(4 * j, 4 * j + 4)
            ops.tensor_tensor(kblk[:, b.par, heads4, :], kT[:, b.par, :].unsqueeze(1).to_broadcast([P, 4, P]),
                              K.headmask[:, heads4].unsqueeze(2).to_broadcast([P, 4, P]), ALU.mult).then_inc(k_spread[j % 2], 1)

        @block.tensor
        def _(pe):
            def turn_x(b):
                wait(pe, normed, b.n + 1)
                last_use(pe, "x", b)
                pe.transpose(bank_of("x")[:, 0:P], xn[:, :], K.ident[:, :]).then_inc(turned, 1)

            def make_q(b):
                wait(pe, x_turned, b.n + 1)
                last_use(pe, "q", b)
                for n in range(hb):
                    for t in range(4 * n, min(4 * n + 4, nt)):
                        mm = pe.matmul(bank_of("q", n)[:, (t % 4) * P:(t % 4 + 1) * P],
                                       wq[:, t * P:(t + 1) * P], xT[:, b.par, :], start=True, stop=True)
                    mm.then_inc(q_made, 1)

            def make_k(b):
                if cross:
                    wait(pe, ctx_loaded[b.par], 16 * (b.pairs + 1))
                else:
                    wait(pe, x_turned, b.n + 1)
                last_use(pe, "k", b)
                for n in range(hb):
                    for t in range(4 * n, min(4 * n + 4, nt)):
                        mm = pe.matmul(bank_of("k", n)[:, (t % 4) * P:(t % 4 + 1) * P],
                                       wk[:, t * P:(t + 1) * P], cb[:, b.par, :], start=True, stop=True)
                    mm.then_inc(k_made, 1)

            def make_v(b):
                width = min(512, nt * P)
                last_use(pe, "v", b)
                for n in range(hb):
                    pe.matmul(bank_of("v", n)[:, 0:width], cb[:, b.par, :],
                              wv[:, n * 512:n * 512 + width], start=True, stop=True).then_inc(v_made, 1)

            def score(b, j):
                s = sc[j % 2]
                wait(pe, q_kept, hb * (b.n + 1))
                if small:
                    wait(pe, k_spread[j % 2], 2 * b.n + j // 2 + 1)
                else:
                    keys(pe, b)
                wait(pe, maxed if masked_max else exped, quad(b, j) - 1)
                if causal and not masked_max:
                    pe.matmul(s[:, :], K.identb[:, :], K.maskb[:, :], start=True, stop=False)
                if small:
                    mm = pe.matmul(s[:, :], qT[:, b.par, 0, :], kblk[:, b.par, 4 * j:4 * j + 4, :],
                                   start=not causal, stop=True)
                else:
                    for t in range(2 * j, 2 * j + 2):
                        mm = pe.matmul(s[:, (t % 2) * 256:(t % 2 + 1) * 256], qT[:, b.par, t, :],
                                       kblk[:, b.par, 2 * t:2 * t + 2, :], start=True, stop=True)
                mm.then_inc(scored, 1)

            def turn_p(b, j):
                wait(pe, scaled, quad(b, j) + 1)
                wait(pe, p_kept[j % 2], kept_p(b, j) - 1)
                for h in range(4):
                    mm = pe.transpose(tr[j % 2][:, h * P:(h + 1) * P], p[:, slot(b, j), h, :], K.ident[:, :])
                mm.then_inc(p_turned, 1)

            def attend(b, j):
                wait(pe, p_kept[j % 2], kept_p(b, j))
                if j == 0:
                    wait(pe, v_kept, hb * (b.n + 1))
                    wait(pe, o_kept, hb * b.n)
                for h in range(4 * j, 4 * j + 4):
                    if small:
                        mm = pe.matmul(ov[0][:, 0:P], v[:, b.par, h * P:(h + 1) * P], pT[:, j % 2, h % 4, :],
                                       start=h == 0, stop=h == heads - 1)
                    else:
                        t, r = h // 2, h % 2
                        mm = pe.matmul(ov[t // 4][64 * r:64 * r + 64, (t % 4) * P:(t % 4 + 1) * P],
                                       v[:, b.par, h * 64:(h + 1) * 64], pT[:, j % 2, h % 4, :],
                                       start=True, stop=True)
                mm.then_inc(attended, 1)

            def project(b):
                wait(pe, o_kept, hb * (b.n + 1))
                last_use(pe, "o", b)
                if isinstance(b.n, int) and b.n + 3 >= NB:
                    wait(pe, added, b.n)
                o = bank_of("o")[:, 0:P]
                for t in range(nt):
                    mm = pe.matmul(o, oT[:, t, :], wo[:, t, :], start=t == 0, stop=bo is None and t == nt - 1)
                if bo is not None:
                    mm = pe.matmul(o, K.ones[0:1, :], bo[0:1, :], start=False, stop=True)
                mm.then_inc(projected, 1)

            for s, n in weights:
                pe.wait_ge(s, n)
            run(pe, make_k=make_k, make_v=make_v, make_q=make_q, turn_x=turn_x, project=project, score=score,
                turn_p=turn_p, attend=attend)

        @block.vector
        def _(dve):
            def stats_x(b):
                if isinstance(b.n, int) and b.n < NB - 2:
                    wait(dve, K.x_loaded[b.n // GB], 16)
                else:
                    for s in K.x_loaded:
                        wait(dve, s, 16)
                nc.vector.bn_stats(st[:, :], K.x[:, seq(b.n), :].rearrange("p a d -> p (a d)")).then_inc(stats, 1)
                dve.wait_ge(stats, 3 * b.n + 1)
                nc.vector.memset(carrier[:, :], 0.0)
                nc.vector.bn_aggr(mv[:, :], st[:, :]).then_inc(stats, 1)
                dve.wait_ge(stats, 3 * b.n + 2)
                nc.vector.tensor_scalar(ve[:, :], mv[:, 1:2], EPS, None, ALU.add).then_inc(stats, 1)

            def norm_x(b):
                wait(dve, rooted, b.n + 1)
                wait(dve, turned, b.n)
                nc.vector.tensor_scalar(xn[:, :], K.x[:, seq(b.n), :].rearrange("p a d -> p (a d)"),
                                        mv[:, 0:1], rs[:, 0:1], ALU.subtract, ALU.mult).then_inc(normed, 1)

            def turn_x(b):
                wait(dve, turned, b.n + 1)
                nc.vector.tensor_copy(xT[:, b.par, :], bank_of("x")[:, 0:P]).then_inc(x_turned, 1)

            def make_q(b):
                for n in range(hb):
                    wait(dve, q_made, hb * b.n + n + 1)
                    w = min(4, nt)
                    src = bank_of("q", n)[:, 0:w * P]
                    dst = qT[:, b.par, 4 * n:4 * n + w, :].rearrange("p t d -> p (t d)")
                    if small:
                        nc.vector.tensor_scalar(dst, src, bq[:, 0:1], scale, ALU.add, ALU.mult).then_inc(q_kept, 1)
                    else:
                        nc.vector.tensor_scalar(dst, src, scale, None, ALU.mult).then_inc(q_kept, 1)

            def make_k(b):
                for n in range(hb):
                    wait(dve, k_made, hb * b.n + n + 1)
                    src = bank_of("k", n)
                    if small:
                        wait(dve, k_spread[1], 2 * (b.n - 1))
                        nc.vector.tensor_scalar(kT[:, b.par, :], src[:, 0:P], bk[:, 0:1], None, ALU.add).then_inc(k_kept, 1)
                    else:
                        dst = kblk[0:64, b.par, 8 * n:8 * n + 8, :].rearrange("p (t r) d -> p t r d", r=2)[:, :, 0, :]
                        nc.vector.tensor_copy(dst, src[0:64, :].rearrange("p (t d) -> p t d", t=4)).then_inc(k_kept, 1)

            def spread_k(b, j):
                if j % 2 == 0:
                    spread_keys(dve, nc.vector, b, j)

            def make_v(b):
                wait(dve, attended, nq * (b.n - 1))
                for n in range(hb):
                    wait(dve, v_made, hb * b.n + n + 1)
                    src = bank_of("v", n)
                    if small:
                        dst = v[:, b.par, :].rearrange("p (h s) -> p h s", s=136)[:, :, 0:hd]
                        nc.vector.tensor_copy(dst, src[:, 0:P].rearrange("p (h d) -> p h d", h=heads)).then_inc(v_kept, 1)
                    else:
                        nc.vector.tensor_copy(v[:, b.par, n * 512:(n + 1) * 512], src[:, :]).then_inc(v_kept, 1)

            def invert(b, j):
                wait(dve, exped, quad(b, j) + 1)
                nc.vector.reciprocal(rtotal[:, slot(b, j), :], total[:, slot(b, j), :]).then_inc(inverted, 1)

            def score(b, j):
                wait(dve, scored, quad(b, j) + 1)
                if masked_max:
                    carrier4 = carriers[:, slot(b, j), :]
                    nc.vector.memset(carrier4[:, 0:1], 0.0)
                    wait(dve, p_turned, quad(b, j) - 3)
                    nc.vector.memset(carrier4[:, 1:2], 0.0)
                    for h in range(4):
                        m = nc.vector.tensor_tensor_reduce(
                            p[:, slot(b, j), h, :], sc[j % 2][:, h * P:(h + 1) * P], K.mask[:, :], -1.0, FLT_MAX,
                            ALU.add, ALU.min, negmax[:, slot(b, j), h:h + 1])
                    m.then_inc(maxed, 1)
                else:
                    nc.vector.tensor_reduce(negmax[:, slot(b, j), :], sc[j % 2][:, :].rearrange("p (h k) -> p h k", h=4),
                                            AX.X, ALU.max, negate=True).then_inc(maxed, 1)
                if j:
                    invert(b, j - 1)
                elif (b - 1).inside():
                    invert(b - 1, nq - 1)

            def turn_p(b, j):
                if isinstance(b.n, int) and b.n == NB - 1 and j == nq - 2:
                    invert(b, nq - 1)
                if p_on_act and j % 2:
                    return
                wait(dve, p_turned, quad(b, j) + 1)
                wait(dve, attended, quad(b, j) - 1)
                nc.vector.tensor_copy(pT[:, j % 2, :, :].rearrange("p h q -> p (h q)"), tr[j % 2][:, :]).then_inc(p_kept[j % 2], 1)

            def project(b):
                wait(dve, projected, b.n + 1)
                xb = K.x[:, seq(b.n), :].rearrange("p a d -> p (a d)")
                nc.vector.tensor_tensor(xb, bank_of("o")[:, 0:P], xb, ALU.add).then_inc(added, 1)

            for s, n in weights:
                dve.wait_ge(s, n)
            run(dve, **({"spread_k": spread_k} if small else {}), stats_x=stats_x, norm_x=norm_x, turn_x=turn_x, make_q=make_q, make_k=make_k, make_v=make_v,
                score=score, turn_p=turn_p, project=project)

        @block.gpsimd
        def _(pool):
            def stats_x(b):
                wait(pool, stats, 3 * b.n + 3)
                nc.gpsimd.tensor_tensor(rs[:, :], ve[:, :], K.mhalf[:, 0:1], ALU.pow).then_inc(rooted, 1)

            def score(b, j):
                if not j and not (b - 1).inside():
                    return
                b, j = (b, j - 1) if j else (b - 1, nq - 1)
                divide(b, j)

            def spread_k(b, j):
                if j % 2:
                    spread_keys(pool, nc.gpsimd, b, j)

            def divide(b, j):
                wait(pool, inverted, quad(b, j) + 1)
                q = p[:, slot(b, j), :, :]
                nc.gpsimd.tensor_tensor(q, q, rtotal[:, slot(b, j), :].unsqueeze(2).to_broadcast([P, 4, P]),
                                        ALU.mult).then_inc(scaled, 1)

            def turn_p(b, j):
                if isinstance(b.n, int) and b.n == NB - 1 and j == nq - 2:
                    divide(b, nq - 1)

            for s, n in weights:
                pool.wait_ge(s, n)
            run(pool, **({"spread_k": spread_k} if small else {}), stats_x=stats_x, score=score, turn_p=turn_p)
            if clean is not None:
                nc.gpsimd.memset(clean, 0.0)

        if later:
            @block.sync
            def _(sp):
                for to, source, loaded in later:
                    sp.dma_start(to, source).then_inc(loaded, 16)

        if cross:
            @block.sync
            def _(sp):
                def make_k(b):
                    wait(sp, v_made, b.n - 1)
                    sp.dma_start(cb[:, b.par, :], ctxT[:, seq(b.n), :].rearrange("p a d -> p (a d)")).then_inc(ctx_loaded[b.par], 16)

                run(sp, make_k=make_k)

        @block.scalar
        def _(act):
            def score(b, j):
                wait(act, maxed, quad(b, j) + 1)
                wait(act, p_turned, quad(b, j) - 3)
                for h in range(4):
                    at = p[:, slot(b, j), h, :]
                    source = at if masked_max else sc[j % 2][:, h * P:(h + 1) * P]
                    e = nc.scalar.activation(at, source, ACT.Exp, scale=-1.0 if masked_max else 1.0,
                                             bias=negmax[:, slot(b, j), h:h + 1],
                                             accum_out=total[:, slot(b, j), h:h + 1])
                e.then_inc(exped, 1)

            def make_k(b):
                for n in range(hb):
                    wait(act, k_made, hb * b.n + n + 1)
                    dst = kblk[64:128, b.par, 8 * n:8 * n + 8, :].rearrange("p (t r) d -> p t r d", r=2)[:, :, 1, :]
                    nc.scalar.activation(dst, bank_of("k", n)[64:128, :].rearrange("p (t d) -> p t d", t=4),
                                         ACT.Copy).then_inc(k_kept2, 1)

            def turn_p(b, j):
                if j % 2:
                    wait(act, p_turned, quad(b, j) + 1)
                    wait(act, attended, quad(b, j) - 1)
                    nc.scalar.activation(pT[:, 1, :, :].rearrange("p h q -> p (h q)"), tr[1][:, :],
                                         ACT.Copy).then_inc(p_kept[1], 1)

            def attend(b, j):
                if j < nq - 1:
                    return
                wait(act, attended, nq * (b.n + 1))
                wait(act, projected, b.n)
                for n in range(hb):
                    w = min(4, nt)
                    dst = oT[:, 4 * n:4 * n + w, :].rearrange("p t d -> p (t d)")
                    if small:
                        nc.scalar.activation(dst, ov[n][:, 0:w * P], ACT.Identity, bias=bv[:, 0:1]).then_inc(o_kept, 1)
                    else:
                        nc.scalar.activation(dst, ov[n][:, 0:w * P], ACT.Copy).then_inc(o_kept, 1)

            for s, n in weights:
                act.wait_ge(s, n)
            run(act, score=score, attend=attend, **({} if small else {"make_k": make_k}),
                **({"turn_p": turn_p} if p_on_act else {}))


def pieces(weights_split, g):
    for tensors in weights_split:
        n = tensors[0].shape[-1] // NG
        yield [t[:, g * n:(g + 1) * n] for t in tensors]


def normalise(K, name, xT=None, split=None, logits=None, wr=None, n=0, weights=(), weights_split=(),
              weights_high=(), thirds=None):
    nc = K.nc
    W = GB * P
    turned_ps, product_ps, logit_ps = K.bank[0:2], K.bank[2:4], K.bank[4:6]
    with ExitStack() as ctx:
        def sb(s, shape, dt=F32):
            return ctx.enter_context(nc.sbuf_tensor(f"{name}_{s}", shape, dt))

        def sem(s):
            return K.sem(f"{name}_{s}")

        st, mv = sb("st", [P, NB, 6]), sb("mv", [P, NB, 2])
        ve, rs, xn = sb("ve", [P, NB]), sb("rs", [P, NB]), sb("xn", [P, 2, GB, P])
        xg = sb("xg", [P, 2, W]) if split else None
        product = sb("product", [n, 2, W]) if split else None
        stats, rooted = sem("stats"), sem("rooted")
        normed, turned, kept, parted_high, parted_low = (
            sem(s) for s in ("normed", "turned", "kept", "parted_high", "parted_low"))
        multiplied, product_kept, product_turned, saved = (
            sem(s) for s in ("multiplied", "product_kept", "product_turned", "saved"))
        high_made, third = sem("high_made"), sem("third")
        block = ctx.enter_context(nc.Block())

        @block.tensor
        def _(pe):
            for s, c in weights:
                pe.wait_ge(s, c)
            for g in range(NG + 2 if split else NG):
                if g < NG:
                    pe.wait_ge(normed, g + 1)
                    wait(pe, kept, g - 1)
                    if split:
                        wait(pe, parted_high, g - 1)
                    for i in range(GB):
                        mm = pe.transpose(turned_ps[g % 2][:, i * P:(i + 1) * P], xn[:, g % 2, i, :], K.ident[:, :])
                    mm.then_inc(turned, 1)
                r = g - 1
                if split and 0 <= r < NG:
                    pe.wait_ge(kept, r + 1)
                    wait(pe, product_kept, r - 1)
                    pe.matmul(product_ps[r % 2][0:n, :], wr, xg[:, r % 2, :], start=True, stop=True).then_inc(multiplied, 1)
                r = g - 2
                if split and r >= 0:
                    pe.wait_ge(product_kept, r + 1)
                    wait(pe, saved, r - 1)
                    for i in range(GB):
                        mm = pe.transpose(logit_ps[r % 2][:, 32 * i:32 * i + n],
                                          product[:, r % 2, i * P:(i + 1) * P], K.ident[0:n, 0:n])
                    mm.then_inc(product_turned, 1)

        @block.vector
        def _(dve):
            for k, group in enumerate((range(GB), range(GB, NB))):
                cols = slice(group[0], group[-1] + 1)
                for b in group:
                    last = nc.vector.bn_stats(st[:, b, :], K.x[:, b, :])
                last.then_inc(stats, 1)
                dve.wait_ge(stats, 3 * k + 1)
                for b in group:
                    last = nc.vector.bn_aggr(mv[:, b, :], st[:, b, :])
                last.then_inc(stats, 1)
                dve.wait_ge(stats, 3 * k + 2)
                nc.vector.tensor_scalar(ve[:, cols], mv[:, cols, 1], EPS, None, ALU.add).then_inc(stats, 1)
            for g in range(NG + 3 if split else NG):
                if g < NG:
                    dve.wait_ge(rooted, 1 if g == 0 else 2)
                    wait(dve, turned, g - 1)
                    for i in range(GB):
                        b = GB * g + i
                        last = nc.vector.tensor_scalar(xn[:, g % 2, i, :], K.x[:, b, :], mv[:, b, 0:1],
                                                       rs[:, b:b + 1], ALU.subtract, ALU.mult)
                    last.then_inc(normed, 1)
                r = g - 2
                if split and 0 <= r < NG:
                    dve.wait_ge(multiplied, r + 1)
                    wait(dve, product_turned, r - 1)
                    nc.vector.tensor_copy(product[:, r % 2, :], product_ps[r % 2][0:n, :]).then_inc(product_kept, 1)
                r = g - 3
                if split and r >= 0:
                    dve.wait_ge(product_turned, r + 1)
                    nc.vector.tensor_copy(
                        logits[:, GB * r:GB * (r + 1), :],
                        logit_ps[r % 2][:, 0:P].rearrange("p (i e) -> p i e", i=GB)[:, :, 0:n]).then_inc(saved, 1)

        @block.scalar
        def _(act):
            for s, c in weights:
                act.wait_ge(s, c)
            for g in range(NG):
                for w, high, _ in pieces(weights_split, g):
                    nc.scalar.activation(high, w, ACT.Copy).then_inc(high_made, 1)
                for w, high in pieces(weights_high, g):
                    nc.scalar.activation(high, w, ACT.Copy)
                act.wait_ge(turned, g + 1)
                if split:
                    wait(act, parted_low, g - 1)
                    wait(act, multiplied, g - 1)
                to = xg[:, g % 2, :] if split else xT[:, g * W:(g + 1) * W]
                nc.scalar.activation(to, turned_ps[g % 2][:, :], ACT.Copy).then_inc(kept, 1)
                if split:
                    nc.scalar.activation(split[0][:, g * W:(g + 1) * W], turned_ps[g % 2][:, :],
                                         ACT.Copy).then_inc(parted_high, 1)

        @block.gpsimd
        def _(pool):
            for k, cols in enumerate((slice(0, GB), slice(GB, NB))):
                pool.wait_ge(stats, 3 * k + 3)
                nc.gpsimd.tensor_tensor(rs[:, cols], ve[:, cols], K.mhalf[:, cols], ALU.pow).then_inc(rooted, 1)
            for s, c in weights:
                pool.wait_ge(s, c)
            count = 0
            for g in range(NG):
                for w, high, low in pieces(weights_split, g):
                    count += 1
                    pool.wait_ge(high_made, count)
                    nc.gpsimd.tensor_tensor(low, w, high.bitcast(F32), ALU.subtract)
                if split:
                    pool.wait_ge(parted_high, g + 1)
                    cols = slice(g * W, (g + 1) * W)
                    nc.gpsimd.tensor_tensor(split[1][:, cols], xg[:, g % 2, :], split[0][:, cols].bitcast(F32),
                                            ALU.subtract).then_inc(parted_low, 1)
            if thirds:
                done = [0]

                def link(ins):
                    done[0] += 1
                    ins.then_inc(third, 1)
                    pool.wait_ge(third, done[0])

                part_in_three(nc.gpsimd, link, *thirds)


def part_in_three(eng, link, x, rest, parts):
    link(eng.tensor_copy(parts[0], x))
    link(eng.tensor_tensor(rest, x, parts[0], ALU.subtract))
    link(eng.tensor_copy(parts[1], rest))
    link(eng.tensor_tensor(rest, rest, parts[1], ALU.subtract))
    link(eng.tensor_copy(parts[2], rest))


def part_matmul(pe, out, a, b, start=True, stop=True):
    pe.matmul(out, a[0], b[0], start=start, stop=False)
    pe.matmul(out, a[0], b[1], start=False, stop=False)
    return pe.matmul(out, a[1], b[0], start=False, stop=stop)


def route(K, name, logits, gates, experts, shared, gT, weights_split=(), casts=()):
    nc = K.nc
    E = experts
    with ExitStack() as ctx:
        def sb(s, shape, dt=F32):
            return ctx.enter_context(nc.sbuf_tensor(f"{name}_{s}", shape, dt))

        def sem(s):
            return K.sem(f"{name}_{s}")

        e, prob = sb("e", [P, NB, E]), sb("prob", [P, NB, E])
        z, mx, tot = sb("z", [P, NB]), sb("mx", [P, NB]), sb("tot", [P, NB])
        top, idx, idxf = sb("top", [P, NB, 8]), sb("idx", [P, NB, 8], U32), sb("idxf", [P, NB, 8])
        hot0, hot1 = sb("hot0", [P, NB, E]), sb("hot1", [P, NB, E])
        G = E + 1 if shared else E
        parts, rest = sb("parts", [P, NB, P], BF16), sb("rest", [P, NB, G])
        turned_ps = [b[:, :].bitcast(BF16)[:, 0:GB * P] for b in K.bank[0:2]]
        chain, shifted, exped, routed = sem("chain"), sem("shifted"), sem("exped"), sem("routed")
        zeroed, turned, kept, weights_high = sem("zeroed"), sem("turned"), sem("kept"), sem("weights_high")
        CHAIN = 16 if shared else 13
        block = ctx.enter_context(nc.Block())

        def over(t):
            return t.unsqueeze(2).to_broadcast([P, NB, E])

        @block.scalar
        def _(act):
            if shared:
                act.wait_ge(shifted, 1)
                nc.scalar.activation(z[:, :], logits[:, :, E], ACT.Exp, scale=-1.0)
                nc.scalar.activation(prob[:, :, :], e[:, :, :], ACT.Exp).then_inc(exped, 1)
            else:
                nc.scalar.activation(e[:, :, :], logits[:, :, :], ACT.Exp, scale=-1.0).then_inc(exped, 1)
            for w, high, _ in weights_split:
                nc.scalar.activation(high, w, ACT.Copy).then_inc(weights_high, 1)
            for to, source in casts:
                nc.scalar.activation(to, source, ACT.Copy)

        @block.vector
        def _(dve):
            done = [0]

            def link(ins):
                done[0] += 1
                ins.then_inc(chain, 1)
                dve.wait_ge(chain, done[0])

            if shared:
                link(nc.vector.tensor_reduce(mx[:, :], logits[:, :, 0:E], AX.X, ALU.max))
                nc.vector.tensor_tensor(e[:, :, :], logits[:, :, 0:E], over(mx[:, :]), ALU.subtract).then_inc(shifted, 1)
                dve.wait_ge(exped, 1)
                link(nc.vector.tensor_reduce(tot[:, :], prob[:, :, :], AX.X, ALU.add))
                link(nc.vector.reciprocal(mx[:, :], tot[:, :]))
                link(nc.vector.tensor_tensor(prob[:, :, :], prob[:, :, :], over(mx[:, :]), ALU.mult))
            else:
                dve.wait_ge(exped, 1)
                link(nc.vector.tensor_scalar(e[:, :, :], e[:, :, :], 1.0, None, ALU.add))
                link(nc.vector.reciprocal(prob[:, :, :], e[:, :, :]))
            for b in range(NB):
                last = nc.vector.max(top[:, b, :], prob[:, b, :])
            link(last)
            for b in range(NB):
                last = nc.vector.max_index(idx[:, b, :], top[:, b, :], prob[:, b, :])
            link(last)
            link(nc.vector.tensor_copy(idxf[:, :, :], idx[:, :, :]))
            iota = K.iota[:, 0:E].unsqueeze(1).to_broadcast([P, NB, E])
            nc.vector.tensor_tensor(hot0[:, :, :], iota, over(idxf[:, :, 0]), ALU.is_equal)
            nc.vector.tensor_tensor(tot[:, :], top[:, :, 0], top[:, :, 1], ALU.add)
            link(nc.vector.tensor_tensor(hot1[:, :, :], iota, over(idxf[:, :, 1]), ALU.is_equal))
            nc.vector.reciprocal(mx[:, :], tot[:, :])
            link(nc.vector.tensor_tensor(hot0[:, :, :], hot0[:, :, :], hot1[:, :, :], ALU.add))
            link(nc.vector.tensor_tensor(hot0[:, :, :], hot0[:, :, :], prob[:, :, :], ALU.mult))
            last = nc.vector.tensor_tensor(gates[:, :, 0:E], hot0[:, :, :], over(mx[:, :]), ALU.mult)
            if shared:
                link(nc.vector.tensor_scalar(z[:, :], z[:, :], 1.0, None, ALU.add))
                last = nc.vector.reciprocal(gates[:, :, E], z[:, :])
            last.then_inc(routed, 1)
            g3 = [parts[:, :, k * 32:k * 32 + G] for k in range(3)]
            dve.wait_ge(zeroed, 1)
            dve.wait_ge(routed, 1)
            part_in_three(nc.vector, link, gates[:, :, :], rest[:, :, :], g3)
            assert done[0] == CHAIN, done
            for g in range(NG):
                dve.wait_ge(turned, g + 1)
                nc.vector.tensor_copy(gT[:, g * GB * P:(g + 1) * GB * P], turned_ps[g % 2][:, :]).then_inc(kept, 1)

        @block.gpsimd
        def _(pool):
            nc.gpsimd.memset(parts[:, :, :], 0.0).then_inc(zeroed, 1)
            for i, (w, high, low) in enumerate(weights_split):
                pool.wait_ge(weights_high, i + 1)
                nc.gpsimd.tensor_tensor(low, w, high.bitcast(F32), ALU.subtract)

        @block.tensor
        def _(pe):
            pe.wait_ge(chain, CHAIN)
            for g in range(NG):
                wait(pe, kept, g - 1)
                for i in range(GB):
                    mm = pe.transpose(turned_ps[g % 2][:, i * P:(i + 1) * P], parts[:, GB * g + i, :], K.identb[:, :])
                mm.then_inc(turned, 1)


def shared_mixture(K, name, gT, w_gate, w_up, w_down, sel):
    nc = K.nc
    gate_ps, up_ps, spread_ps, down_ps, out_ps = K.bank[0:2], K.bank[2:4], K.bank[4:6], K.bank[6], K.bank[7]
    W = GB * P
    with ExitStack() as ctx:
        def sb(s, shape, dt=F32):
            return ctx.enter_context(nc.sbuf_tensor(f"{name}_{s}", shape, dt))

        def sem(s):
            return K.sem(f"{name}_{s}")

        silu, prod, hidden = sb("silu", [P, 2, W]), sb("prod", [P, 2, W]), sb("hidden", [P, 2, W])
        high, low = sb("high", [P, 2, W], F32R), sb("low", [P, 2, W], F32R)
        yT = sb("yT", [P, W])
        gated, raised, spread, silued, produced, weighed, parted_high, parted_low, multiplied = (
            sem(s) for s in ("gated", "raised", "spread", "silued", "produced", "weighed", "parted_high",
                             "parted_low", "multiplied"))
        y_kept, y_turned, added = sem("y_kept"), sem("y_turned"), sem("added")
        block = ctx.enter_context(nc.Block())

        def before(eng, sem, g, c, k):
            wait(eng, sem, NC0 * g + c - k + 1)

        @block.tensor
        def _(pe):
            def up(g, c):
                xg = [x[:, bass.ds(g * W, W)] for x in K.xsplit]
                cols = slice(c * P, (c + 1) * P)
                before(pe, silued, g, c, 2)
                part_matmul(pe, gate_ps[c % 2][:, :], [w[:, cols] for w in w_gate], xg).then_inc(gated, 1)
                before(pe, produced, g, c, 2)
                part_matmul(pe, up_ps[c % 2][:, :], [w[:, cols] for w in w_up], xg).then_inc(raised, 1)
                before(pe, weighed, g, c, 2)
                pe.matmul(spread_ps[c % 2][:, :], sel[:, cols], gT[:, bass.ds(g * W, W)],
                          start=True, stop=True).then_inc(spread, 1)

            def down(g, c):
                before(pe, parted_low, g, c, 0)
                if c == 0:
                    wait(pe, y_kept, g)
                part_matmul(pe, down_ps[:, :], [w[:, c, :] for w in w_down],
                            [high[:, c % 2, :], low[:, c % 2, :]], start=c == 0, stop=c == NC0 - 1).then_inc(multiplied, 1)

            def turn(g):
                wait(pe, y_kept, g + 1)
                for i in range(GB):
                    mm = pe.transpose(out_ps[:, i * P:(i + 1) * P], yT[:, i * P:(i + 1) * P], K.ident[:, :])
                mm.then_inc(y_turned, 1)

            def group(g):
                for c in range(NC0):
                    up(g, c)
                    if c >= 2:
                        down(g, c - 2)
                    elif follows(g):
                        down(g - 1, NC0 - 2 + c)
                    if c == 3 and follows(g):
                        turn(g - 1)

            loop_groups(pe, group)
            down(NG - 1, NC0 - 2)
            down(NG - 1, NC0 - 1)
            turn(NG - 1)

        @block.scalar
        def _(act):
            def keep_y(g):
                wait(act, multiplied, NC0 * (g + 1))
                nc.scalar.activation(yT[:, :], down_ps[:, :], ACT.Copy).then_inc(y_kept, 1)

            def group(g):
                for c in range(NC0):
                    before(act, gated, g, c, 0)
                    before(act, produced, g, c, 2)
                    nc.scalar.activation(silu[:, c % 2, :], gate_ps[c % 2][:, :], ACT.Silu).then_inc(silued, 1)
                    if c == 2 and follows(g):
                        keep_y(g - 1)

            loop_groups(act, group)
            keep_y(NG - 1)

        @block.vector
        def _(dve):
            def add(g):
                wait(dve, y_turned, g + 1)
                xg = K.x[:, bass.ds(g * GB, GB), :]
                nc.vector.tensor_tensor(xg, out_ps[:, :].rearrange("p (i d) -> p i d", i=GB), xg, ALU.add).then_inc(added, 1)

            def group(g):
                for c in range(NC0):
                    before(dve, silued, g, c, 0)
                    before(dve, raised, g, c, 0)
                    before(dve, weighed, g, c, 2)
                    nc.vector.tensor_tensor(prod[:, c % 2, :], silu[:, c % 2, :], up_ps[c % 2][:, :],
                                            ALU.mult).then_inc(produced, 1)
                    before(dve, produced, g, c, 0)
                    before(dve, spread, g, c, 0)
                    before(dve, parted_low, g, c, 2)
                    nc.vector.tensor_tensor(hidden[:, c % 2, :], prod[:, c % 2, :], spread_ps[c % 2][:, :],
                                            ALU.mult).then_inc(weighed, 1)
                    before(dve, weighed, g, c, 0)
                    before(dve, multiplied, g, c, 2)
                    nc.vector.tensor_copy(high[:, c % 2, :], hidden[:, c % 2, :]).then_inc(parted_high, 1)
                    if c == 5 and follows(g):
                        add(g - 1)

            loop_groups(dve, group)
            add(NG - 1)

        @block.gpsimd
        def _(pool):
            def group(g):
                for c in range(NC0):
                    before(pool, parted_high, g, c, 0)
                    before(pool, multiplied, g, c, 2)
                    nc.gpsimd.tensor_tensor(low[:, c % 2, :], hidden[:, c % 2, :], high[:, c % 2, :].bitcast(F32),
                                            ALU.subtract).then_inc(parted_low, 1)

            loop_groups(pool, group)


def mixture(K, name, gT, w1, b1, w2, b2, sel, out, stored):
    nc = K.nc
    W = GB * P
    NT = 32
    up_ps, spread_ps, down_ps, out_ps = K.bank[0:4], K.bank[4:6], K.bank[6], K.bank[7]
    with ExitStack() as ctx:
        def sb(s, shape, dt=F32):
            return ctx.enter_context(nc.sbuf_tensor(f"{name}_{s}", shape, dt))

        def sem(s):
            return K.sem(f"{name}_{s}")

        geluT, hidden = sb("geluT", [P, 4, W]), sb("hidden", [P, 4, W])
        high, low = sb("high", [P, 4, W], F32R), sb("low", [P, 4, W], F32R)
        yT = sb("yT", [P, W])
        raised, gelued, spread, weighed, parted_high, parted_low, multiplied = (
            sem(s) for s in ("raised", "gelued", "spread", "weighed", "parted_high", "parted_low", "multiplied"))
        y_kept, y_turned, added = sem("y_kept"), sem("y_turned"), sem("added")
        block = ctx.enter_context(nc.Block())
        LAG = 3

        def before(eng, sem, g, c, k):
            wait(eng, sem, NT * g + c - k + 1)

        @block.tensor
        def _(pe):
            def up(g, c):
                e = c // 4
                before(pe, gelued, g, c, 4)
                part_matmul(pe, up_ps[c % 4][:, :], [w[:, c * P:(c + 1) * P] for w in w1],
                            [x[:, bass.ds(g * W, W)] for x in K.xsplit]).then_inc(raised, 1)
                if c % 4 == 0:
                    before(pe, weighed, g, c, 5)
                    pe.matmul(spread_ps[e % 2][:, :], sel[:, e * P:(e + 1) * P], gT[:, bass.ds(g * W, W)],
                              start=True, stop=True).then_inc(spread, 1)

            def down(g, c):
                before(pe, parted_low, g, c, 0)
                if c == 0:
                    wait(pe, y_kept, g)
                    for k in range(3):
                        pe.matmul(down_ps[:, :], b2[:, k * P:(k + 1) * P], gT[:, bass.ds(g * W, W)],
                                  start=k == 0, stop=False)
                part_matmul(pe, down_ps[:, :], [w[:, c, :] for w in w2], [high[:, c % 4, :], low[:, c % 4, :]],
                            start=False, stop=c == NT - 1).then_inc(multiplied, 1)

            def turn(g):
                wait(pe, y_kept, g + 1)
                for i in range(GB):
                    mm = pe.transpose(out_ps[:, i * P:(i + 1) * P], yT[:, i * P:(i + 1) * P], K.ident[:, :])
                mm.then_inc(y_turned, 1)

            def group(g):
                for c in range(NT):
                    up(g, c)
                    if c >= LAG:
                        down(g, c - LAG)
                    elif follows(g):
                        down(g - 1, NT - LAG + c)
                    if c == 5 and follows(g):
                        turn(g - 1)

            loop_groups(pe, group)
            for c in range(NT - LAG, NT):
                down(NG - 1, c)
            turn(NG - 1)

        @block.scalar
        def _(act):
            def keep_y(g):
                wait(act, multiplied, NT * (g + 1))
                nc.scalar.activation(yT[:, :], down_ps[:, :], ACT.Copy).then_inc(y_kept, 1)

            def group(g):
                for c in range(NT):
                    before(act, raised, g, c, 0)
                    before(act, weighed, g, c, 4)
                    nc.scalar.activation(geluT[:, c % 4, :], up_ps[c % 4][:, :], ACT.Gelu,
                                         bias=b1[:, c:c + 1]).then_inc(gelued, 1)
                    if c == LAG - 1 and follows(g):
                        keep_y(g - 1)

            loop_groups(act, group)
            keep_y(NG - 1)

        @block.vector
        def _(dve):
            def add(g):
                wait(dve, y_turned, g + 1)
                xg = K.x[:, bass.ds(g * GB, GB), :]
                nc.vector.tensor_tensor(xg, out_ps[:, :].rearrange("p (i d) -> p i d", i=GB), xg, ALU.add).then_inc(added, 1)

            def weigh(g, c):
                before(dve, gelued, g, c, 0)
                if c % 4 == 0:
                    wait(dve, spread, E1 * g + c // 4 + 1)
                before(dve, parted_low, g, c, 4)
                nc.vector.tensor_tensor(hidden[:, c % 4, :], geluT[:, c % 4, :], spread_ps[c // 4 % 2][:, :],
                                        ALU.mult).then_inc(weighed, 1)

            def part(g, c):
                before(dve, weighed, g, c, 0)
                before(dve, multiplied, g, c, 4)
                nc.vector.tensor_copy(high[:, c % 4, :], hidden[:, c % 4, :]).then_inc(parted_high, 1)

            def group(g):
                for c in range(NT):
                    weigh(g, c)
                    part(g, c)
                    if c == 8 and follows(g):
                        add(g - 1)

            loop_groups(dve, group)
            add(NG - 1)

        @block.gpsimd
        def _(pool):
            def group(g):
                for c in range(NT):
                    before(pool, parted_high, g, c, 0)
                    before(pool, multiplied, g, c, 4)
                    nc.gpsimd.tensor_tensor(low[:, c % 4, :], hidden[:, c % 4, :], high[:, c % 4, :].bitcast(F32),
                                            ALU.subtract).then_inc(parted_low, 1)

            loop_groups(pool, group)

        @block.sync
        def _(sp):
            for g in range(NG):
                sp.wait_ge(added, g + 1)
                sp.dma_start(out[GB * g:GB * (g + 1), :, :].rearrange("b t d -> t b d"),
                             K.x[:, GB * g:GB * (g + 1), :]).then_inc(stored, 16)
            sp.wait_ge(stored, 16 * NG)


def standardised_attention(K, name, xT, wq, wk, wv, wo, weights=(), weights_low=()):
    nc = K.nc
    W = GB * P
    q_ps, k_ps, v_ps, score_ps = K.bank[0], K.bank[1], K.bank[2], K.bank[3:5]
    spread_ps, turned_ps, attended_ps = K.bank[5], K.bank[6], K.bank[7]
    out_ps = turned_ps
    with ExitStack() as ctx:
        def sb(s, shape, dt=F32):
            return ctx.enter_context(nc.sbuf_tensor(f"{name}_{s}", shape, dt))

        def sem(s):
            return K.sem(f"{name}_{s}")

        qT, kT, v = sb("qT", [P, W]), sb("kT", [P, W]), sb("v", [P, 2, W])
        p, pT, oT = sb("p", [P, 2, W]), sb("pT", [P, W]), sb("oT", [P, W])
        st, mv, means, dev, vp = (sb("st", [P, GB, 6]), sb("mv", [P, GB, 2]), sb("means", [P, GB]),
                                  sb("dev", [P, GB]), sb("vp", [P, GB]))
        ve, rs, negmax, shift, tot, rtot = (sb(s, [P, 2, GB]) for s in ("ve", "rs", "negmax", "shift", "tot", "rtot"))
        q_made, k_made, v_made, q_kept, k_kept, v_kept = (
            sem(s) for s in ("q_made", "k_made", "v_made", "q_kept", "k_kept", "v_kept"))
        scored, averaged, mean_spread, deviated, var_spread, varied, rooted, shifted = (
            sem(s) for s in ("scored", "averaged", "mean_spread", "deviated", "var_spread", "varied", "rooted",
                             "shifted"))
        exped, scaled, turned, p_kept, attended, o_kept, projected, added = (
            sem(s) for s in ("exped", "scaled", "turned", "p_kept", "attended", "o_kept", "projected", "added"))
        chain = sem("chain")
        block = ctx.enter_context(nc.Block())

        def part(t, i):
            return t[..., i * P:(i + 1) * P]

        def run(step, *parts):
            for g in range(-1, NG + 2):
                step(g, *((lambda n, f=f: f(n) if 0 <= n < NG else None) for f in parts))

        @block.tensor
        def _(pe):
            def project_in(g):
                cols = slice(g * W, (g + 1) * W)
                context = K.ctxT[:, GB * g:GB * (g + 1), :]
                wait(pe, q_kept, g)
                pe.matmul(q_ps[:, :], wq, xT[:, cols], start=True, stop=True).then_inc(q_made, 1)
                wait(pe, k_kept, g)
                pe.matmul(k_ps[:, :], wk, context.rearrange("p i t -> p (i t)"), start=True, stop=True).then_inc(k_made, 1)

            def project_v(g):
                context = K.ctxT[:, GB * g:GB * (g + 1), :]
                wait(pe, v_kept, g)
                for i in range(GB):
                    mm = pe.matmul(part(v_ps, i), context[:, i, :], wv, start=True, stop=True)
                mm.then_inc(v_made, 1)

            def score(g):
                pe.wait_ge(q_kept, g + 1)
                pe.wait_ge(k_kept, g + 1)
                wait(pe, exped, g - 1)
                for i in range(GB):
                    mm = pe.matmul(part(score_ps[g % 2], i), part(qT, i), part(kT, i), start=True, stop=True)
                mm.then_inc(scored, 1)

            def spread_mean(g):
                pe.wait_ge(averaged, g + 1)
                pe.matmul(spread_ps[:, 0:GB], K.mean[:, :], means[:, :], start=True, stop=True).then_inc(mean_spread, 1)

            def spread_var(g):
                pe.wait_ge(deviated, g + 1)
                pe.matmul(spread_ps[:, 8:8 + GB], K.mean[:, :], vp[:, :], start=True, stop=True).then_inc(var_spread, 1)

            def turn_p(g):
                pe.wait_ge(scaled, g + 1)
                wait(pe, added, g)
                for i in range(GB):
                    mm = pe.transpose(part(turned_ps, i), part(p[:, g % 2, :], i), K.ident[:, :])
                mm.then_inc(turned, 1)

            def attend(g):
                pe.wait_ge(p_kept, g + 1)
                wait(pe, o_kept, g)
                for i in range(GB):
                    mm = pe.matmul(part(attended_ps, i), part(v[:, g % 2, :], i), part(pT, i), start=True, stop=True)
                mm.then_inc(attended, 1)

            def project(g):
                pe.wait_ge(o_kept, g + 1)
                for i in range(GB):
                    mm = pe.matmul(part(out_ps, i), part(oT, i), wo, start=True, stop=True)
                mm.then_inc(projected, 1)

            for s, c in weights:
                pe.wait_ge(s, c)
            def step(g, score, project, project_in, spread_mean, turn_p, project_v, spread_var, attend):
                score(g)
                project(g - 2)
                project_in(g + 1)
                spread_mean(g)
                turn_p(g - 1)
                project_v(g + 1)
                spread_var(g)
                attend(g - 1)

            run(step, score, project, project_in, spread_mean, turn_p, project_v, spread_var, attend)

        @block.scalar
        def _(act):
            def exp(g):
                act.wait_ge(shifted, g + 1)
                wait(act, turned, g - 1)
                for i in range(GB):
                    e = nc.scalar.activation(part(p[:, g % 2, :], i), part(score_ps[g % 2], i), ACT.Exp,
                                             bias=shift[:, g % 2, i:i + 1], scale=rs[:, g % 2, i:i + 1],
                                             accum_out=tot[:, g % 2, i:i + 1])
                e.then_inc(exped, 1)

            def keep_in(g):
                act.wait_ge(q_made, g + 1)
                wait(act, scored, g)
                nc.scalar.activation(qT[:, :], q_ps[:, :], ACT.Copy).then_inc(q_kept, 1)
                act.wait_ge(k_made, g + 1)
                nc.scalar.activation(kT[:, :], k_ps[:, :], ACT.Copy).then_inc(k_kept, 1)

            def keep_p(g):
                act.wait_ge(turned, g + 1)
                wait(act, attended, g)
                nc.scalar.activation(pT[:, :], turned_ps[:, :], ACT.Copy).then_inc(p_kept, 1)

            def keep_o(g):
                act.wait_ge(attended, g + 1)
                wait(act, projected, g)
                nc.scalar.activation(oT[:, :], attended_ps[:, :], ACT.Copy).then_inc(o_kept, 1)

            def step(g, exp, keep_in, keep_p, keep_o):
                exp(g - 1)
                keep_in(g + 1)
                keep_p(g - 1)
                keep_o(g - 1)

            run(step, exp, keep_in, keep_p, keep_o)

        @block.vector
        def _(dve):
            done = [0]

            def link(ins):
                done[0] += 1
                ins.then_inc(chain, 1)
                dve.wait_ge(chain, done[0])

            def keep_v(g):
                dve.wait_ge(v_made, g + 1)
                wait(dve, attended, g - 1)
                nc.vector.tensor_copy(v[:, g % 2, :], v_ps[:, :]).then_inc(v_kept, 1)

            def scale(g):
                dve.wait_ge(exped, g + 1)
                link(nc.vector.reciprocal(rtot[:, g % 2, :], tot[:, g % 2, :]))
                p4 = p[:, g % 2, :].rearrange("p (i k) -> p i k", i=GB)
                nc.vector.tensor_tensor(p4, p4, rtot[:, g % 2, :].unsqueeze(2).to_broadcast([P, GB, P]),
                                        ALU.mult).then_inc(scaled, 1)

            def average(g):
                dve.wait_ge(scored, g + 1)
                for i in range(GB):
                    last = nc.vector.bn_stats(st[:, i, :], part(score_ps[g % 2], i))
                link(last)
                for i in range(GB):
                    last = nc.vector.bn_aggr(mv[:, i, :], st[:, i, :])
                link(last)
                wait(dve, mean_spread, g)
                nc.vector.tensor_copy(means[:, :], mv[:, :, 0]).then_inc(averaged, 1)
                nc.vector.tensor_reduce(negmax[:, g % 2, :], score_ps[g % 2][:, :].rearrange("p (i k) -> p i k", i=GB),
                                        AX.X, ALU.max, negate=True)

            def deviate(g):
                dve.wait_ge(mean_spread, g + 1)
                dve.wait_ge(averaged, g + 1)
                link(nc.vector.tensor_tensor(dev[:, :], means[:, :], spread_ps[:, 0:GB], ALU.subtract))
                link(nc.vector.tensor_tensor(dev[:, :], dev[:, :], dev[:, :], ALU.mult))
                nc.vector.tensor_tensor(vp[:, :], dev[:, :], mv[:, :, 1], ALU.add).then_inc(deviated, 1)

            def add(g):
                dve.wait_ge(projected, g + 1)
                xg = K.x[:, GB * g:GB * (g + 1), :]
                nc.vector.tensor_tensor(xg, out_ps[:, :].rearrange("p (i d) -> p i d", i=GB), xg, ALU.add).then_inc(added, 1)

            def find_shift(g):
                dve.wait_ge(var_spread, g + 1)
                nc.vector.tensor_scalar(ve[:, g % 2, :], spread_ps[:, 8:8 + GB], EPS, None, ALU.add).then_inc(varied, 1)
                dve.wait_ge(rooted, g + 1)
                nc.vector.tensor_tensor(shift[:, g % 2, :], negmax[:, g % 2, :], rs[:, g % 2, :], ALU.mult).then_inc(shifted, 1)

            def step(g, average, scale, add, deviate, find_shift, keep_v):
                average(g)
                scale(g - 1)
                add(g - 2)
                deviate(g)
                find_shift(g)
                keep_v(g + 1)

            run(step, average, scale, add, deviate, find_shift, keep_v)

        @block.gpsimd
        def _(pool):
            for g in range(NG):
                pool.wait_ge(varied, g + 1)
                nc.gpsimd.tensor_tensor(rs[:, g % 2, :], ve[:, g % 2, :], K.mhalf[:, 0:GB], ALU.pow).then_inc(rooted, 1)
                for w, high, low in pieces(weights_low, g):
                    nc.gpsimd.tensor_tensor(low, w, high.bitcast(F32), ALU.subtract)


def decoder(nc, A, out, phases=7):
    K = Shared(nc)
    with ExitStack() as ctx:
        def sb(n, shape, dt=F32):
            return ctx.enter_context(nc.sbuf_tensor(n, shape, dt))

        def sem(n):
            return ctx.enter_context(nc.semaphore(n))

        K.bank = [ctx.enter_context(nc.psum_tensor(f"bank{i}", [P, 512], F32)) for i in range(8)]
        K.x = sb("x_sb", [P, NB, P])
        K.ctxT = sb("ctxT_sb", [P, NB, P])
        K.ident, K.identb = sb("ident_sb", [P, P]), sb("identb", [P, P], BF16)
        K.mask, K.maskb = sb("mask_sb", [P, P]), sb("maskb", [P, 4, P], BF16)
        K.headmask, K.iota = sb("headmask_sb", [P, 16]), sb("iota_sb", [P, 16])
        K.ones, K.mean = sb("ones", [1, P]), sb("mean", [P, P])
        K.mhalf = sb("mhalf", [P, NB])
        K.xsplit = [sb("x_high", [P, NB * P], F32R), sb("x_low", [P, NB * P], F32R)]
        logits0, gates0 = sb("logits0", [P, NB, G0]), sb("gates0", [P, NB, G0])
        logits1, gates1 = sb("logits1", [P, NB, E1]), sb("gates1", [P, NB, E1])
        gT = sb("gT", [P, NB * P], BF16)
        sel0, sel1 = sb("sel0", [P, NC0 * P], BF16), sb("sel1", [P, E1 * P], BF16)
        b2, b2_rest = sb("b2", [P, 3 * P], BF16), sb("b2_rest", [P, P])
        K.x_loaded = [sem(f"x_loaded{g}") for g in range(NG)]
        consts_loaded = sem("consts_loaded")
        stored = sem("stored")
        w, loaded = {}, {}
        attn1 = ctx.enter_context(ExitStack())
        layer0 = ctx.enter_context(ExitStack())
        attn0 = ctx.enter_context(ExitStack())

        with nc.Block() as block:
            groups = {"self0": ["a_w", "a_b", "a_bo"], "cross0": ["c_wq", "c_wkv", "c_wo", "c_bo"],
                      "ffn0": ["f_wr", "f_wgu", "f_wd", "f_sel"], "self1": ["s_wqkv", "s_wo"],
                      "cross1": ["t_wqo", "t_wkv"], "ffn1": ["m_wr", "m_w1", "m_b1", "m_w2", "m_b2", "m_sel"]}
            for gname, scope in (("cross1", ctx), ("ffn1", ctx), ("self1", attn1), ("self0", layer0),
                                 ("cross0", layer0), ("ffn0", layer0)):
                loaded[gname] = (sem(f"loaded_{gname}"), 16 * len(groups[gname]))
                for n in groups[gname]:
                    w[n] = scope.enter_context(nc.sbuf_tensor(f"{n}_sb", list(A[n].shape), F32))
                if scope is attn1:
                    kblk = scope.enter_context(nc.sbuf_tensor("kblk", [P, 2, 16, P], F32))
            v_small = attn0.enter_context(nc.sbuf_tensor("v_small", [P, 2, 16 * 136], F32))

            @block.sync
            def _(sp):
                for g in range(NG):
                    sp.dma_start(K.x[:, GB * g:GB * (g + 1), :],
                                 A["x"][GB * g:GB * (g + 1), :, :].rearrange("b t d -> t b d")).then_inc(K.x_loaded[g], 16)

            @block.scalar
            def _(act):
                for n, t in (("ident", K.ident), ("mask", K.mask), ("headmask", K.headmask), ("iota", K.iota)):
                    act.dma_start(t[:, :], A[n]).then_inc(consts_loaded, 16)
                for n in groups["self0"]:
                    act.dma_start(w[n][:, :], A[n]).then_inc(loaded["self0"][0], 16)

            @block.gpsimd
            def _(pool):
                nc.gpsimd.memset(v_small[:, :, :], 0.0)

            @block.vector
            def _(dve):
                nc.vector.memset(K.ones[:, :], 1.0)
                nc.vector.memset(K.mean[:, :], 1.0 / P)
                nc.vector.memset(K.mhalf[:, :], -0.5)
                dve.wait_ge(consts_loaded, 64)
                nc.vector.tensor_copy(K.identb[:, :], K.ident[:, :])
                nc.vector.tensor_copy(K.maskb[:, :, :], K.mask[:, :].unsqueeze(1).to_broadcast([P, 4, P]))

        later = [(w[n][:, :], A[n], loaded[g][0]) for g in ("cross0", "ffn0", "self1", "cross1", "ffn1") for n in groups[g]]
        later.append((K.ctxT[:, :, :], A["ctxT"], loaded["cross1"][0]))
        loaded["cross1"] = (loaded["cross1"][0], loaded["cross1"][1] + 16)
        a = w["a_w"]
        tiles = lambda t, n: t[:, :].rearrange("p (t d) -> p t d", t=n)
        attention(K, "self0", 16, 8, True, a[:, 0:P], a[:, P:2 * P], a[:, 2 * P:3 * P],
                  tiles(a[:, 3 * P:4 * P], 1), w["a_b"][:, 0:1], w["a_b"][:, 1:2], w["a_b"][:, 2:3], w["a_bo"], p_on_act=True,
                  weights=[loaded["self0"]], later=later, v=v_small, clean=kblk[:, :, :, :])
        K.clear()
        attn0.close()
        if phases > 1:
            c = w["c_wkv"]
            attention(K, "cross0", 8, 64, False, w["c_wq"], c[:, 0:512], c[:, 512:1024],
                      tiles(w["c_wo"], 4), bo=w["c_bo"], ctxT=A["ctxT"], weights=[loaded["cross0"]],
                      kblk=kblk[:, :, 0:8, :])
            K.clear()
        if phases > 2:
            u = w["f_wgu"]
            with ExitStack() as parts:
                def part(n, width):
                    return [parts.enter_context(nc.sbuf_tensor(f"{n}_{k}", [P, width], F32R)) for k in ("high", "low")]

                gu, d = part("f_wgu", 2 * NC0 * P), part("f_wd", NC0 * P)
                normalise(K, "norm_ffn0", None, K.xsplit, logits0, w["f_wr"][:, :], G0, weights=[loaded["ffn0"]],
                          weights_split=[(u[:, :], gu[0][:, :], gu[1][:, :])])
                K.clear()
                route(K, "route0", logits0, gates0, E0, True, gT, casts=[(sel0[:, :], w["f_sel"][:, :])],
                      weights_split=[(w["f_wd"][:, :], d[0][:, :], d[1][:, :])])
                K.clear()
                shared_mixture(K, "ffn0", gT, [t[:, 0:NC0 * P] for t in gu], [t[:, NC0 * P:2 * NC0 * P] for t in gu],
                               [tiles(t, NC0) for t in d], sel0)
                K.clear()
        layer0.close()
        if phases > 3:
            s = w["s_wqkv"]
            attention(K, "self1", 16, 64, True, s[:, 0:1024], s[:, 1024:2048], s[:, 2048:3072],
                      tiles(w["s_wo"], 8), weights=[loaded["self1"]], kblk=kblk, masked_max=True)
            K.clear()
        attn1.close()
        if phases > 4:
            with ExitStack() as scope:
                def part(n, width):
                    return [scope.enter_context(nc.sbuf_tensor(f"{n}_{k}", [P, width], F32R)) for k in ("high", "low")]

                w1, w2 = part("m_w1", 4 * E1 * P), part("m_w2", 4 * E1 * P)
                with nc.sbuf_tensor("xT_sb", [P, NB * P], F32) as xT:
                    normalise(K, "norm_cross1", xT, weights=[loaded["ffn1"]],
                              weights_high=[(w["m_w1"][:, :], w1[0][:, :]), (w["m_w2"][:, :], w2[0][:, :])])
                    K.clear()
                    t, r = w["t_wqo"], w["t_wkv"]
                    standardised_attention(K, "cross1", xT, t[:, 0:P], r[:, 0:P], r[:, P:2 * P], t[:, P:2 * P],
                                           weights=[loaded["cross1"]],
                                           weights_low=[(w["m_w1"][:, :], w1[0][:, :], w1[1][:, :]),
                                                        (w["m_w2"][:, :], w2[0][:, :], w2[1][:, :])])
                    K.clear()
                if phases > 5:
                    third = lambda t: [t[:, k * P:(k + 1) * P] for k in range(3)]
                    normalise(K, "norm_ffn1", None, K.xsplit, logits1, w["m_wr"][:, :], E1, weights=[loaded["ffn1"]],
                              thirds=(w["m_b2"][:, :], b2_rest[:, :], third(b2)))
                    K.clear()
                    route(K, "route1", logits1, gates1, E1, False, gT, casts=[(sel1[:, :], w["m_sel"][:, :])])
                    K.clear()
                    mixture(K, "ffn1", gT, w1, w["m_b1"], [tiles(t, 32) for t in w2], b2, sel1, out, stored)
                    K.clear()
        if phases < 6:
            with nc.Block() as block:
                @block.sync
                def _(sp):
                    for gname, (q, n) in loaded.items():
                        sp.wait_ge(q, n)
                    sp.dma_start(out.rearrange("b t d -> t b d"), K.x[:, :, :]).then_inc(stored, 16)
                    sp.wait_ge(stored, 16)


def layout(inputs):
    import numpy as np

    I = {k: np.asarray(v) for k, v in inputs.items()}

    def rows(a):
        return a.reshape(-1, P, a.shape[-1]).transpose(1, 0, 2).reshape(P, -1)

    def pad(a):
        return np.concatenate([a, np.zeros((P - a.shape[0], *a.shape[1:]), a.dtype)], 0)

    L = {"x": I["x"], "ctxT": pad(I["ctx_768"].transpose(2, 0, 1))}
    L["a_w"] = np.concatenate([I["L0_attn_" + n].T for n in ("Wq", "Wk", "Wv", "Wo")], 1)
    L["a_b"] = np.stack([I["L0_attn_" + n] for n in ("bq", "bk", "bv")], 1)
    L["a_bo"] = I["L0_attn_bo"][None, :]
    L["c_wq"] = I["L0_xattn_Wq"]
    L["c_wkv"] = pad(np.concatenate([I["L0_xattn_Wk"], I["L0_xattn_Wv"]], 1))
    L["c_wo"] = rows(I["L0_xattn_Wo"])
    L["c_bo"] = I["L0_xattn_bo"][None, :]
    L["f_wr"] = np.concatenate([I["L0_ffn_Wg"], I["L0_ffn_Wsg"]], 0).T
    L["f_wgu"] = np.concatenate([I["L0_ffn_We_gate"].reshape(-1, P), I["L0_ffn_Ws_gate"],
                                 I["L0_ffn_We_up"].reshape(-1, P), I["L0_ffn_Ws_up"]], 0).T
    L["f_wd"] = rows(np.concatenate([I["L0_ffn_We_down"].transpose(0, 2, 1).reshape(-1, P), I["L0_ffn_Ws_down"].T], 0))
    L["s_wqkv"] = np.concatenate([I["L1_attn_" + n].reshape(-1, P) for n in ("W_Q", "W_K", "W_V")], 0).T
    L["s_wo"] = rows(I["L1_attn_W_O"].T)
    L["t_wqo"] = np.concatenate([I["L1_xattn_Wq"].T, I["L1_xattn_Wo"].T], 1)
    L["t_wkv"] = pad(np.concatenate([I["L1_xattn_Wk"].T, I["L1_xattn_Wv"].T], 1))
    L["m_wr"] = I["L1_ffn_centroids"].T
    L["m_w1"] = I["L1_ffn_W1"].transpose(1, 0, 2).reshape(P, -1)
    L["m_b1"] = I["L1_ffn_b1"].reshape(-1, P).T
    L["m_w2"] = rows(I["L1_ffn_W2"].reshape(-1, P))
    L["m_b2"] = np.zeros((P, P), np.float32)
    for r in (0, 32, 64):
        L["m_b2"][r:r + E1] = I["L1_ffn_b2"]
    i = np.arange(P)
    L["ident"] = np.eye(P, dtype=np.float32)
    L["mask"] = np.where(i[None, :] <= i[:, None], 0.0, NEG).astype(np.float32)
    L["headmask"] = (i[:, None] // 8 == np.arange(16)[None, :]).astype(np.float32)
    L["iota"] = np.tile(np.arange(16, dtype=np.float32), (P, 1))
    part_row = i[:, None] % 32 + np.where(i[:, None] < 96, 0, P)
    L["f_sel"] = (np.minimum(np.arange(NC0 * P) // 64, E0)[None, :] == part_row).astype(np.float32)
    L["m_sel"] = (np.arange(E1 * P)[None, :] // P == part_row).astype(np.float32)
    return {k: np.ascontiguousarray(v) for k, v in L.items()}


def kernel(**inputs):
    import concourse.bacc as bacc
    from concourse.bass_utils import run_bass_kernel_spmd

    nc = bacc.Bacc("TRN2", target_bir_lowering=False, num_devices=1)
    arrays, aps = {}, {}
    for name, a in layout(inputs).items():
        arrays[f"in_{name}"] = a
        aps[name] = nc.dram_tensor(f"in_{name}", a.shape, mybir.dt.from_np(a.dtype), kind="ExternalInput").ap()
    out = nc.dram_tensor("out", (NB, P, P), F32, kind="ExternalOutput").ap()
    decoder(nc, aps, out)
    r = run_bass_kernel_spmd(nc, [arrays], core_ids=[0])
    return r.results[0]["out"]
```

```python
from contextlib import ExitStack

import concourse.bass as bass
from concourse import mybir

F32 = mybir.dt.float32
BF16 = mybir.dt.bfloat16
F32R = mybir.dt.float32r
U32 = mybir.dt.uint32
ALU = mybir.AluOpType
ACT = mybir.ActivationFunctionType
AX = mybir.AxisListType

P = 128
NB = 16
CTX = 96
GB = 4
NG = NB // GB
EPS = 1e-5
NEG = -1e30
FLT_MAX = 3e38
E0, E1 = 16, 8
NC0 = 10
G0 = E0 + 1


def wait(eng, sem, value):
    if isinstance(value, int) and value <= 0:
        return
    eng.wait_ge(sem, value)


def seq(b):
    return slice(b, b + 1) if isinstance(b, int) else bass.ds(b, 1)


class Shared:

    def __init__(self, nc):
        self.nc, self.phase_sems, self.cleared = nc, [], []

    def sem(self, name):
        self.phase_sems.append(self.nc.alloc_semaphore(name))
        return self.phase_sems[-1]

    def clear(self, by=None):
        for s in self.cleared:
            self.nc.release_semaphore(s)
        for s in self.phase_sems:
            (by or self.nc.sync).sem_clear(s)
        self.phase_sems, self.cleared = [], self.phase_sems


class At:

    def __init__(self, n, par, pairs):
        self.n, self.par, self.pairs = n, par, pairs

    def __add__(self, k):
        return At(self.n + k, (self.par + k) % 2, self.pairs + (self.par + k) // 2)

    def __sub__(self, k):
        return self + -k

    def inside(self):
        return not isinstance(self.n, int) or 0 <= self.n < NB


def pipeline(eng, body):
    for n in range(-2, 2):
        body(At(n, n % 2, n // 2))
    with eng.Fori(1, NB // 2 - 1) as k:
        body(At(2 * k, 0, k))
        body(At(2 * k + 1, 1, k))
    for n in range(NB - 2, NB + 1):
        body(At(n, n % 2, n // 2))


def follows(g):
    return not isinstance(g, int) or g > 0


def loop_groups(eng, body):
    body(0)
    with eng.Fori(1, NG) as g:
        body(g)


def attention(K, name, heads, hd, causal, wq, wk, wv, wo, bq=None, bk=None, bv=None, bo=None,
              p_on_act=False, ctxT=None, weights=(), later=(), kblk=None, v=None, clean=(),
              next_stats=False):
    nc, cross = K.nc, ctxT is not None
    nt = heads * hd // P
    nq = heads // 4
    hb = max(1, nt // 4)
    small = hd < 64
    scale = float(hd) ** -0.5
    sc, tr, ov = K.bank[2:4], K.bank[4:6], K.bank[6:8]
    if cross:
        order = {"v": 0, "x": 1, "k": 0, "q": 1, "o": 0}
    else:
        order = {"k": 0, "v": 1, "o": 0, "x": 1, "q": 0} if hb == 1 else {"k": 0, "v": 0, "o": 0, "x": 1, "q": 0}

    def bank_of(use, n=0):
        return K.bank[order[use] + n]

    with ExitStack() as ctx:
        def sb(n, shape, dt=F32):
            return ctx.enter_context(nc.sbuf_tensor(f"{name}_{n}", shape, dt))

        def sem(n):
            return K.sem(f"{name}_{n}")

        st, mv, ve, rs = sb("st", [P, 6]), sb("mv", [P, 2]), sb("ve", [P, 1]), sb("rs", [P, 1])
        wv_parts = [] if small else [sb(f"wv_{k}", [P, nt * P], F32R) for k in ("high", "low")]
        cb_parts = [] if small else [sb(f"cb_{k}", [P, 2, P], F32R) for k in ("high", "low")]
        carrier, carriers = sb("carrier", [P, 1]), sb("carriers", [P, 4, 2])
        xn, xT = sb("xn", [P, P]), sb("xT", [P, 2, P])
        kT = sb("kT", [P, 2, P]) if small else None
        cb = sb("cb", [P, 2, P]) if cross else xT
        qT = sb("qT", [P, 2, nt, P])
        kblk = sb("kblk", [P, 2, heads, P]) if small else kblk
        v = v if small else sb("v", [P, 2, nt * P])
        p = sb("p", [P, 4, 4, P])
        pT = sb("pT", [P, 2, 4, P])
        oT = sb("oT", [P, nt, P])
        negmax, total, rtotal = sb("negmax", [P, 4, 4]), sb("total", [P, 4, 4]), sb("rtotal", [P, 4, 4])

        wv_high, wv_low, cb_high, cb_low = sem("wv_high"), sem("wv_low"), sem("cb_high"), sem("cb_low")
        stats, rooted = sem("stats"), sem("rooted")
        normed, turned, x_turned = sem("normed"), sem("turned"), sem("x_turned")
        ctx_loaded = [sem("ctx_loaded0"), sem("ctx_loaded1")]
        q_made, k_made, v_made = sem("q_made"), sem("k_made"), sem("v_made")
        q_kept, k_kept, k_kept2, v_kept = sem("q_kept"), sem("k_kept"), sem("k_kept2"), sem("v_kept")
        k_spread = [sem("k_spread0"), sem("k_spread1")]
        scored, maxed, exped, inverted, scaled = (sem(n) for n in ("scored", "maxed", "exped", "inverted", "scaled"))
        p_turned, attended, o_kept, projected, added = (
            sem(n) for n in ("p_turned", "attended", "o_kept", "projected", "added"))
        p_kept = [sem("p_kept0"), sem("p_kept1")]
        block = ctx.enter_context(nc.Block())

        def quad(b, j):
            return nq * b.n + j

        def slot(b, j):
            return j if nq == 4 else 2 * b.par + j

        def kept_p(b, j):
            return (nq // 2) * b.n + j // 2 + 1

        def last_use(eng, use, b):
            if cross:
                {"v": lambda: (wait(eng, added, b.n - 2), keys(eng, b)), "x": lambda: wait(eng, q_kept, b.n),
                 "k": lambda: wait(eng, v_kept, b.n), "q": lambda: None,
                 "o": lambda: (keys(eng, b + 3), wait(eng, v_kept, min_seq(b.n + 3)))}[use]()
            elif hb == 1:
                {"k": lambda: wait(eng, q_kept, min_seq(b.n + 1)), "v": lambda: wait(eng, x_turned, min_seq(b.n + 1)),
                 "o": lambda: keys(eng, b + 2), "x": lambda: wait(eng, v_kept, b.n),
                 "q": lambda: (wait(eng, added, b.n - 2), keys(eng, b - 1))}[use]()
            else:
                {"k": lambda: wait(eng, q_kept, 2 * min_seq(b.n + 1)), "v": lambda: keys(eng, b),
                 "o": lambda: wait(eng, v_kept, 2 * min_seq(b.n + 3)), "x": lambda: wait(eng, v_kept, 2 * b.n),
                 "q": lambda: (wait(eng, added, b.n - 2), wait(eng, v_kept, 2 * b.n - 1),
                               wait(eng, x_turned, b.n + 1))}[use]()

        def min_seq(n):
            return min(n, NB) if isinstance(n, int) else n

        def keys(eng, b):
            n = min_seq(b.n + 1)
            wait(eng, k_kept, hb * n)
            if not small:
                wait(eng, k_kept2, hb * n)

        def body(b, make_k, spread_k, make_v, make_q, turn_x, project, score, turn_p, attend, stats_x, norm_x,
                 part_context):
            if nq == 4 and not small:
                score(b, 2)
                turn_p(b, 0)
                stats_x(b + 2)
                make_k(b + 1)
                attend(b - 1, 3)
                score(b, 3)
                turn_p(b, 1)
                norm_x(b + 2)
                make_v(b + 1)
                score(b + 1, 0)
                attend(b, 0)
                attend(b, 1)
                turn_p(b, 2)
                project(b - 1)
                turn_x(b + 2)
                score(b + 1, 1)
                part_context(b + 2)
                turn_p(b, 3)
                make_q(b + 2)
                attend(b, 2)
            elif nq == 4:
                stats_x(b + 2)
                spread_k(b + 1, 1)
                attend(b - 1, 3)
                score(b, 3)
                turn_p(b, 0)
                norm_x(b + 2)
                make_v(b + 1)
                turn_p(b, 1)
                score(b + 1, 0)
                spread_k(b + 1, 2)
                project(b - 1)
                attend(b, 0)
                turn_x(b + 2)
                score(b + 1, 1)
                turn_p(b, 2)
                attend(b, 1)
                turn_p(b, 3)
                make_q(b + 2)
                spread_k(b + 1, 3)
                score(b + 1, 2)
                make_k(b + 2)
                spread_k(b + 2, 0)
                attend(b, 2)
            else:
                attend(b - 1, 1)
                stats_x(b + 2)
                score(b + 1, 0)
                norm_x(b + 2)
                make_v(b + 1)
                score(b + 1, 1)
                turn_x(b + 2)
                turn_p(b, 0)
                make_k(b + 2)
                turn_p(b, 1)
                make_q(b + 2)
                part_context(b + 2)
                attend(b, 0)
                project(b - 1)

        def run(eng, **steps):
            def checked(step):
                return (lambda b, *j: b.inside() and step(b, *j)) if step else (lambda *_: None)

            names = ("make_k", "spread_k", "make_v", "make_q", "turn_x", "project", "score", "turn_p", "attend", "stats_x", "norm_x",
                     "part_context")
            assert set(steps) <= set(names)
            pipeline(eng, lambda b: body(b, **{n: checked(steps.get(n)) for n in names}))

        def spread_keys(eng, ops, b, j):
            wait(eng, k_kept, b.n + 1)
            heads4 = slice(4 * j, 4 * j + 4)
            ops.tensor_tensor(kblk[:, b.par, heads4, :], kT[:, b.par, :].unsqueeze(1).to_broadcast([P, 4, P]),
                              K.headmask[:, heads4].unsqueeze(2).to_broadcast([P, 4, P]), ALU.mult).then_inc(k_spread[j % 2], 1)

        @block.tensor
        def _(pe):
            def turn_x(b):
                wait(pe, normed, b.n + 1)
                last_use(pe, "x", b)
                pe.transpose(bank_of("x")[:, 0:P], xn[:, :], K.ident[:, :]).then_inc(turned, 1)

            def make_q(b):
                wait(pe, x_turned, b.n + 1)
                last_use(pe, "q", b)
                for n in range(hb):
                    for t in range(4 * n, min(4 * n + 4, nt)):
                        mm = pe.matmul(bank_of("q", n)[:, (t % 4) * P:(t % 4 + 1) * P],
                                       wq[:, t * P:(t + 1) * P], xT[:, b.par, :], start=True, stop=True)
                    mm.then_inc(q_made, 1)

            def make_k(b):
                if cross:
                    wait(pe, ctx_loaded[b.par], 16 * (b.pairs + 1))
                else:
                    wait(pe, x_turned, b.n + 1)
                last_use(pe, "k", b)
                for n in range(hb):
                    for t in range(4 * n, min(4 * n + 4, nt)):
                        mm = pe.matmul(bank_of("k", n)[:, (t % 4) * P:(t % 4 + 1) * P],
                                       wk[:, t * P:(t + 1) * P], cb[:, b.par, :], start=True, stop=True)
                    mm.then_inc(k_made, 1)

            def make_v(b):
                last_use(pe, "v", b)
                if small:
                    pe.matmul(bank_of("v")[:, 0:P], cb[:, b.par, :], wv, start=True, stop=True).then_inc(v_made, 1)
                    return
                wait(pe, wv_low, 1)
                wait(pe, cb_low, b.n + 1)
                for n in range(hb):
                    part_matmul(pe, bank_of("v", n)[:, :], [c[:, b.par, :] for c in cb_parts],
                                [w[:, n * 512:(n + 1) * 512] for w in wv_parts]).then_inc(v_made, 1)

            def score(b, j):
                s = sc[j % 2]
                wait(pe, q_kept, hb * (b.n + 1))
                if small:
                    wait(pe, k_spread[j % 2], 2 * b.n + j // 2 + 1)
                else:
                    keys(pe, b)
                wait(pe, maxed if causal else exped, quad(b, j) - 1)
                if small:
                    mm = pe.matmul(s[:, :], qT[:, b.par, 0, :], kblk[:, b.par, 4 * j:4 * j + 4, :],
                                   start=True, stop=True)
                else:
                    for t in range(2 * j, 2 * j + 2):
                        mm = pe.matmul(s[:, (t % 2) * 256:(t % 2 + 1) * 256], qT[:, b.par, t, :],
                                       kblk[:, b.par, 2 * t:2 * t + 2, :], start=True, stop=True)
                mm.then_inc(scored, 1)

            def turn_p(b, j):
                wait(pe, scaled, quad(b, j) + 1)
                wait(pe, p_kept[j % 2], kept_p(b, j) - 1)
                for h in range(4):
                    mm = pe.transpose(tr[j % 2][:, h * P:(h + 1) * P], p[:, slot(b, j), h, :], K.ident[:, :])
                mm.then_inc(p_turned, 1)

            def attend(b, j):
                wait(pe, p_kept[j % 2], kept_p(b, j))
                if j == 0:
                    wait(pe, v_kept, hb * (b.n + 1))
                    wait(pe, o_kept, hb * b.n)
                for h in range(4 * j, 4 * j + 4):
                    if small:
                        mm = pe.matmul(ov[0][:, 0:P], v[:, b.par, h * P:(h + 1) * P], pT[:, j % 2, h % 4, :],
                                       start=h == 0, stop=h == heads - 1)
                    else:
                        t, r = h // 2, h % 2
                        mm = pe.matmul(ov[t // 4][64 * r:64 * r + 64, (t % 4) * P:(t % 4 + 1) * P],
                                       v[:, b.par, h * 64:(h + 1) * 64], pT[:, j % 2, h % 4, :],
                                       start=True, stop=True)
                mm.then_inc(attended, 1)

            def project(b):
                wait(pe, o_kept, hb * (b.n + 1))
                last_use(pe, "o", b)
                if isinstance(b.n, int) and b.n + 3 >= NB:
                    wait(pe, added, b.n)
                o = bank_of("o")[:, 0:P]
                for t in range(nt):
                    mm = pe.matmul(o, oT[:, t, :], wo[:, t, :], start=t == 0, stop=bo is None and t == nt - 1)
                if bo is not None:
                    mm = pe.matmul(o, K.ones[0:1, :], bo[0:1, :], start=False, stop=True)
                mm.then_inc(projected, 1)

            for s, n in weights:
                pe.wait_ge(s, n)
            run(pe, make_k=make_k, make_v=make_v, make_q=make_q, turn_x=turn_x, project=project, score=score,
                turn_p=turn_p, attend=attend)

        @block.vector
        def _(dve):
            def stats_x(b):
                if isinstance(b.n, int) and b.n < NB - 2:
                    wait(dve, K.x_loaded[b.n // GB], 16)
                else:
                    for s in K.x_loaded:
                        wait(dve, s, 16)
                nc.vector.bn_stats(st[:, :], K.x[:, seq(b.n), :].rearrange("p a d -> p (a d)")).then_inc(stats, 1)
                dve.wait_ge(stats, 3 * b.n + 1)
                nc.vector.memset(carrier[:, :], 0.0)
                nc.vector.bn_aggr(mv[:, :], st[:, :]).then_inc(stats, 1)
                dve.wait_ge(stats, 3 * b.n + 2)
                nc.vector.tensor_scalar(ve[:, :], mv[:, 1:2], EPS, None, ALU.add).then_inc(stats, 1)

            def norm_x(b):
                wait(dve, rooted, b.n + 1)
                wait(dve, turned, b.n)
                nc.vector.tensor_scalar(xn[:, :], K.x[:, seq(b.n), :].rearrange("p a d -> p (a d)"),
                                        mv[:, 0:1], rs[:, 0:1], ALU.subtract, ALU.mult).then_inc(normed, 1)

            def turn_x(b):
                wait(dve, turned, b.n + 1)
                nc.vector.tensor_copy(xT[:, b.par, :], bank_of("x")[:, 0:P]).then_inc(x_turned, 1)

            def make_q(b):
                for n in range(hb):
                    wait(dve, q_made, hb * b.n + n + 1)
                    w = min(4, nt)
                    src = bank_of("q", n)[:, 0:w * P]
                    dst = qT[:, b.par, 4 * n:4 * n + w, :].rearrange("p t d -> p (t d)")
                    if small:
                        nc.vector.tensor_scalar(dst, src, bq[:, 0:1], scale, ALU.add, ALU.mult).then_inc(q_kept, 1)
                    else:
                        nc.vector.tensor_scalar(dst, src, scale, None, ALU.mult).then_inc(q_kept, 1)

            def make_k(b):
                for n in range(hb):
                    wait(dve, k_made, hb * b.n + n + 1)
                    src = bank_of("k", n)
                    if small:
                        wait(dve, k_spread[1], 2 * (b.n - 1))
                        nc.vector.tensor_scalar(kT[:, b.par, :], src[:, 0:P], bk[:, 0:1], None, ALU.add).then_inc(k_kept, 1)
                    else:
                        dst = kblk[0:64, b.par, 8 * n:8 * n + 8, :].rearrange("p (t r) d -> p t r d", r=2)[:, :, 0, :]
                        nc.vector.tensor_copy(dst, src[0:64, :].rearrange("p (t d) -> p t d", t=4)).then_inc(k_kept, 1)

            def spread_k(b, j):
                if j % 2 == 0:
                    spread_keys(dve, nc.vector, b, j)

            def make_v(b):
                wait(dve, attended, nq * (b.n - 1))
                for n in range(hb):
                    wait(dve, v_made, hb * b.n + n + 1)
                    src = bank_of("v", n)
                    if small:
                        dst = v[:, b.par, :].rearrange("p (h s) -> p h s", s=136)[:, :, 0:hd]
                        nc.vector.tensor_copy(dst, src[:, 0:P].rearrange("p (h d) -> p h d", h=heads)).then_inc(v_kept, 1)
                    else:
                        nc.vector.tensor_copy(v[:, b.par, n * 512:(n + 1) * 512], src[:, :]).then_inc(v_kept, 1)

            def invert(b, j):
                wait(dve, exped, quad(b, j) + 1)
                nc.vector.reciprocal(rtotal[:, slot(b, j), :], total[:, slot(b, j), :]).then_inc(inverted, 1)

            def score(b, j):
                wait(dve, scored, quad(b, j) + 1)
                if causal:
                    carrier4 = carriers[:, slot(b, j), :]
                    nc.vector.memset(carrier4[:, 0:1], 0.0)
                    wait(dve, p_turned, quad(b, j) - 3)
                    nc.vector.memset(carrier4[:, 1:2], 0.0)
                    for h in range(4):
                        m = nc.vector.tensor_tensor_reduce(
                            p[:, slot(b, j), h, :], sc[j % 2][:, h * P:(h + 1) * P], K.mask[:, :], -1.0, FLT_MAX,
                            ALU.add, ALU.min, negmax[:, slot(b, j), h:h + 1])
                    m.then_inc(maxed, 1)
                else:
                    nc.vector.tensor_reduce(negmax[:, slot(b, j), :], sc[j % 2][:, :].rearrange("p (h k) -> p h k", h=4),
                                            AX.X, ALU.max, negate=True).then_inc(maxed, 1)
                if j:
                    invert(b, j - 1)
                elif (b - 1).inside():
                    invert(b - 1, nq - 1)

            def turn_p(b, j):
                if isinstance(b.n, int) and b.n == NB - 1 and j == nq - 2:
                    invert(b, nq - 1)
                if p_on_act and j % 2:
                    return
                wait(dve, p_turned, quad(b, j) + 1)
                wait(dve, attended, quad(b, j) - 1)
                nc.vector.tensor_copy(pT[:, j % 2, :, :].rearrange("p h q -> p (h q)"), tr[j % 2][:, :]).then_inc(p_kept[j % 2], 1)

            def new_stats(b):
                wait(dve, added, b.n + 1)
                nc.vector.bn_stats(K.st[:, seq(b.n), :].rearrange("p a s -> p (a s)"),
                                   K.x[:, seq(b.n), :].rearrange("p a d -> p (a d)"))

            def project(b):
                if next_stats and (b - 1).inside():
                    new_stats(b - 1)
                wait(dve, projected, b.n + 1)
                xb = K.x[:, seq(b.n), :].rearrange("p a d -> p (a d)")
                nc.vector.tensor_tensor(xb, bank_of("o")[:, 0:P], xb, ALU.add).then_inc(added, 1)
                if next_stats and isinstance(b.n, int) and b.n == NB - 1:
                    new_stats(b)

            for s, n in weights:
                dve.wait_ge(s, n)
            run(dve, **({"spread_k": spread_k} if small else {}), stats_x=stats_x, norm_x=norm_x, turn_x=turn_x, make_q=make_q, make_k=make_k, make_v=make_v,
                score=score, turn_p=turn_p, project=project)

        @block.gpsimd
        def _(pool):
            def stats_x(b):
                wait(pool, stats, 3 * b.n + 3)
                nc.gpsimd.tensor_tensor(rs[:, :], ve[:, :], K.mhalf[:, 0:1], ALU.pow).then_inc(rooted, 1)
                if not small and isinstance(b.n, int) and b.n == 0:
                    wait(pool, wv_high, 1)
                    nc.gpsimd.tensor_tensor(wv_parts[1][:, :], wv, wv_parts[0][:, :].bitcast(F32), ALU.subtract).then_inc(wv_low, 1)

            def part_context(b):
                wait(pool, cb_high, b.n + 1)
                nc.gpsimd.tensor_tensor(cb_parts[1][:, b.par, :], cb[:, b.par, :], cb_parts[0][:, b.par, :].bitcast(F32),
                                        ALU.subtract).then_inc(cb_low, 1)

            def score(b, j):
                if not j and not (b - 1).inside():
                    return
                b, j = (b, j - 1) if j else (b - 1, nq - 1)
                divide(b, j)

            def spread_k(b, j):
                if j % 2:
                    spread_keys(pool, nc.gpsimd, b, j)

            def divide(b, j):
                wait(pool, inverted, quad(b, j) + 1)
                q = p[:, slot(b, j), :, :]
                nc.gpsimd.tensor_tensor(q, q, rtotal[:, slot(b, j), :].unsqueeze(2).to_broadcast([P, 4, P]),
                                        ALU.mult).then_inc(scaled, 1)

            def turn_p(b, j):
                if isinstance(b.n, int) and b.n == NB - 1 and j == nq - 2:
                    divide(b, nq - 1)

            for s, n in weights:
                pool.wait_ge(s, n)
            run(pool, **({"spread_k": spread_k} if small else {"part_context": part_context}), stats_x=stats_x, score=score, turn_p=turn_p)
            for t in clean:
                nc.gpsimd.memset(t, 0.0)

        if later:
            @block.sync
            def _(sp):
                for to, source, loaded in later:
                    sp.dma_start(to, source).then_inc(loaded, 16)

        if cross:
            @block.sync
            def _(sp):
                def make_k(b):
                    wait(sp, v_made, b.n - 1)
                    sp.dma_start(cb[:, b.par, :], ctxT[:, seq(b.n), :].rearrange("p a d -> p (a d)")).then_inc(ctx_loaded[b.par], 16)

                run(sp, make_k=make_k)

        @block.scalar
        def _(act):
            def score(b, j):
                wait(act, maxed, quad(b, j) + 1)
                wait(act, p_turned, quad(b, j) - 3)
                for h in range(4):
                    at = p[:, slot(b, j), h, :]
                    source = at if causal else sc[j % 2][:, h * P:(h + 1) * P]
                    e = nc.scalar.activation(at, source, ACT.Exp, scale=-1.0 if causal else 1.0,
                                             bias=negmax[:, slot(b, j), h:h + 1],
                                             accum_out=total[:, slot(b, j), h:h + 1])
                e.then_inc(exped, 1)

            def make_k(b):
                for n in range(hb):
                    wait(act, k_made, hb * b.n + n + 1)
                    dst = kblk[64:128, b.par, 8 * n:8 * n + 8, :].rearrange("p (t r) d -> p t r d", r=2)[:, :, 1, :]
                    nc.scalar.activation(dst, bank_of("k", n)[64:128, :].rearrange("p (t d) -> p t d", t=4),
                                         ACT.Copy).then_inc(k_kept2, 1)

            def turn_p(b, j):
                if j % 2:
                    wait(act, p_turned, quad(b, j) + 1)
                    wait(act, attended, quad(b, j) - 1)
                    nc.scalar.activation(pT[:, 1, :, :].rearrange("p h q -> p (h q)"), tr[1][:, :],
                                         ACT.Copy).then_inc(p_kept[1], 1)

            def attend(b, j):
                if j < nq - 1:
                    return
                wait(act, attended, nq * (b.n + 1))
                wait(act, projected, b.n)
                for n in range(hb):
                    w = min(4, nt)
                    dst = oT[:, 4 * n:4 * n + w, :].rearrange("p t d -> p (t d)")
                    if small:
                        nc.scalar.activation(dst, ov[n][:, 0:w * P], ACT.Identity, bias=bv[:, 0:1]).then_inc(o_kept, 1)
                    else:
                        nc.scalar.activation(dst, ov[n][:, 0:w * P], ACT.Copy).then_inc(o_kept, 1)

            def part_context(b):
                if cross:
                    wait(act, ctx_loaded[b.par], 16 * (b.pairs + 1))
                else:
                    wait(act, x_turned, b.n + 1)
                wait(act, v_made, hb * (b.n - 1))
                nc.scalar.activation(cb_parts[0][:, b.par, :], cb[:, b.par, :], ACT.Copy).then_inc(cb_high, 1)

            for s, n in weights:
                act.wait_ge(s, n)
            if not small:
                nc.scalar.activation(wv_parts[0][:, :], wv, ACT.Copy).then_inc(wv_high, 1)
            run(act, **({} if small else {"part_context": part_context}), score=score, attend=attend, **({} if small else {"make_k": make_k}),
                **({"turn_p": turn_p} if p_on_act else {}))


def pieces(weights_split, g):
    for tensors in weights_split:
        n = tensors[0].shape[-1] // NG
        yield [t[:, g * n:(g + 1) * n] for t in tensors]


def normalise(K, name, xT=None, split=None, logits=None, wr=None, n=0, weights=(), weights_split=(),
              weights_high=(), thirds=None, gates=None, experts=0, shared=False, gT=None, weights_late=(), casts=()):
    nc = K.nc
    W = GB * P
    turned_ps, product_ps, logit_ps = K.bank[0:2], K.bank[2:4], K.bank[4:6]
    with ExitStack() as ctx:
        def sb(s, shape, dt=F32):
            return ctx.enter_context(nc.sbuf_tensor(f"{name}_{s}", shape, dt))

        def sem(s):
            return K.sem(f"{name}_{s}")

        st, mv = K.st, sb("mv", [P, NB, 2])
        ve, rs, xn = sb("ve", [P, NB]), sb("rs", [P, NB]), sb("xn", [P, 2, GB, P])
        xg = sb("xg", [P, 2, W]) if split else None
        product = sb("product", [n, 2, W]) if split else None
        stats, rooted = sem("stats"), sem("rooted")
        normed, turned, kept, parted_high, parted_low = (
            sem(s) for s in ("normed", "turned", "kept", "parted_high", "parted_low"))
        multiplied, product_kept, product_turned, saved = (
            sem(s) for s in ("multiplied", "product_kept", "product_turned", "saved"))
        high_made, late_made, third = sem("high_made"), sem("late_made"), sem("third")
        router = Router(K, sb, sem, logits, gates, experts, shared, gT) if split else None
        block = ctx.enter_context(nc.Block())

        @block.tensor
        def _(pe):
            for s, c in weights:
                pe.wait_ge(s, c)
            for g in range(NG + 2 if split else NG):
                if g < NG:
                    pe.wait_ge(normed, g + 1)
                    wait(pe, kept, g - 1)
                    if split:
                        wait(pe, parted_high, g - 1)
                    for i in range(GB):
                        mm = pe.transpose(turned_ps[g % 2][:, i * P:(i + 1) * P], xn[:, g % 2, i, :], K.ident[:, :])
                    mm.then_inc(turned, 1)
                r = g - 1
                if split and 0 <= r < NG:
                    pe.wait_ge(kept, r + 1)
                    wait(pe, product_kept, r - 1)
                    pe.matmul(product_ps[r % 2][0:n, :], wr, xg[:, r % 2, :], start=True, stop=True).then_inc(multiplied, 1)
                r = g - 2
                if split and r >= 0:
                    pe.wait_ge(product_kept, r + 1)
                    wait(pe, saved, r - 1)
                    for i in range(GB):
                        mm = pe.transpose(logit_ps[r % 2][:, 32 * i:32 * i + n],
                                          product[:, r % 2, i * P:(i + 1) * P], K.ident[0:n, 0:n])
                    mm.then_inc(product_turned, 1)
            if split:
                for g in range(NG):
                    router.turn(pe, g)

        @block.vector
        def _(dve):
            for k, group in enumerate((range(GB), range(GB, NB))):
                cols = slice(group[0], group[-1] + 1)
                for b in group:
                    last = nc.vector.bn_aggr(mv[:, b, :], st[:, b, :])
                last.then_inc(stats, 1)
                dve.wait_ge(stats, 2 * k + 1)
                nc.vector.tensor_scalar(ve[:, cols], mv[:, cols, 1], EPS, None, ALU.add).then_inc(stats, 1)
            for g in range(NG + 3 if split else NG):
                if g < NG:
                    dve.wait_ge(rooted, 1 if g == 0 else 2)
                    wait(dve, turned, g - 1)
                    for i in range(GB):
                        b = GB * g + i
                        last = nc.vector.tensor_scalar(xn[:, g % 2, i, :], K.x[:, b, :], mv[:, b, 0:1],
                                                       rs[:, b:b + 1], ALU.subtract, ALU.mult)
                    last.then_inc(normed, 1)
                r = g - 2
                if split and 0 <= r < NG:
                    dve.wait_ge(multiplied, r + 1)
                    wait(dve, product_turned, r - 1)
                    nc.vector.tensor_copy(product[:, r % 2, :], product_ps[r % 2][0:n, :]).then_inc(product_kept, 1)
                r = g - 3
                if split and r >= 0:
                    dve.wait_ge(product_turned, r + 1)
                    nc.vector.tensor_copy(
                        logits[:, GB * r:GB * (r + 1), :],
                        logit_ps[r % 2][:, 0:P].rearrange("p (i e) -> p i e", i=GB)[:, :, 0:n]).then_inc(saved, 1)
            if split:
                dve.wait_ge(saved, NG)
                router.choose(dve)
                for g in range(NG):
                    router.keep(dve, g)

        @block.scalar
        def _(act):
            for s, c in weights:
                act.wait_ge(s, c)
            for g in range(NG):
                for w, high, _ in pieces(weights_split, g):
                    nc.scalar.activation(high, w, ACT.Copy).then_inc(high_made, 1)
                for w, high in pieces(weights_high, g):
                    nc.scalar.activation(high, w, ACT.Copy)
                act.wait_ge(turned, g + 1)
                if split:
                    wait(act, parted_low, g - 1)
                    wait(act, multiplied, g - 1)
                to = xg[:, g % 2, :] if split else xT[:, g * W:(g + 1) * W]
                nc.scalar.activation(to, turned_ps[g % 2][:, :], ACT.Copy).then_inc(kept, 1)
                if split:
                    nc.scalar.activation(split[0][:, g * W:(g + 1) * W], turned_ps[g % 2][:, :],
                                         ACT.Copy).then_inc(parted_high, 1)
            if split:
                act.wait_ge(saved, NG)
                router.exponents(act)
            for w, high, _ in weights_late:
                nc.scalar.activation(high, w, ACT.Copy).then_inc(late_made, 1)
            for to, source in casts:
                nc.scalar.activation(to, source, ACT.Copy)

        @block.gpsimd
        def _(pool):
            for k, cols in enumerate((slice(0, GB), slice(GB, NB))):
                pool.wait_ge(stats, 2 * k + 2)
                nc.gpsimd.tensor_tensor(rs[:, cols], ve[:, cols], K.mhalf[:, cols], ALU.pow).then_inc(rooted, 1)
            for s, c in weights:
                pool.wait_ge(s, c)
            count = 0
            for g in range(NG):
                for w, high, low in pieces(weights_split, g):
                    count += 1
                    pool.wait_ge(high_made, count)
                    nc.gpsimd.tensor_tensor(low, w, high.bitcast(F32), ALU.subtract)
                if split:
                    pool.wait_ge(parted_high, g + 1)
                    cols = slice(g * W, (g + 1) * W)
                    nc.gpsimd.tensor_tensor(split[1][:, cols], xg[:, g % 2, :], split[0][:, cols].bitcast(F32),
                                            ALU.subtract).then_inc(parted_low, 1)
            if split:
                router.zero()
            for i, (w, high, low) in enumerate(weights_late):
                pool.wait_ge(late_made, i + 1)
                nc.gpsimd.tensor_tensor(low, w, high.bitcast(F32), ALU.subtract)
            if thirds:
                done = [0]

                def link(ins):
                    done[0] += 1
                    ins.then_inc(third, 1)
                    pool.wait_ge(third, done[0])

                part_in_three(nc.gpsimd, link, *thirds)


def part_in_three(eng, link, x, rest, parts):
    link(eng.tensor_copy(parts[0], x))
    link(eng.tensor_tensor(rest, x, parts[0], ALU.subtract))
    link(eng.tensor_copy(parts[1], rest))
    link(eng.tensor_tensor(rest, rest, parts[1], ALU.subtract))
    link(eng.tensor_copy(parts[2], rest))


def part_matmul(pe, out, a, b, start=True, stop=True):
    pe.matmul(out, a[0], b[0], start=start, stop=False)
    pe.matmul(out, a[0], b[1], start=False, stop=False)
    return pe.matmul(out, a[1], b[0], start=False, stop=stop)


class Router:

    def __init__(self, K, sb, sem, logits, gates, experts, shared, gT):
        self.K, self.logits, self.gates, self.E, self.shared, self.gT = K, logits, gates, experts, shared, gT
        E = experts
        self.e, self.prob = sb("e", [P, NB, E]), sb("prob", [P, NB, E])
        self.z, self.mx, self.tot = sb("z", [P, NB]), sb("mx", [P, NB]), sb("tot", [P, NB])
        self.top, self.idx, self.idxf = sb("top", [P, NB, 8]), sb("idx", [P, NB, 8], U32), sb("idxf", [P, NB, 8])
        self.hot0, self.hot1 = sb("hot0", [P, NB, E]), sb("hot1", [P, NB, E])
        self.G = E + 1 if shared else E
        self.parts, self.rest = sb("parts", [P, NB, P], BF16), sb("rest", [P, NB, self.G])
        self.turned_ps = [b[:, :].bitcast(BF16)[:, 0:GB * P] for b in K.bank[6:8]]
        self.chain, self.shifted, self.exped, self.routed = sem("chain"), sem("shifted"), sem("exped"), sem("routed")
        self.zeroed, self.gates_turned, self.gates_kept = sem("zeroed"), sem("gates_turned"), sem("gates_kept")
        self.steps = 16 if shared else 13
        self.done = 0

    def zero(self):
        self.K.nc.gpsimd.memset(self.parts[:, :, :], 0.0).then_inc(self.zeroed, 1)

    def exponents(self, act):
        nc = self.K.nc
        if self.shared:
            act.wait_ge(self.shifted, 1)
            nc.scalar.activation(self.z[:, :], self.logits[:, :, self.E], ACT.Exp, scale=-1.0)
            nc.scalar.activation(self.prob[:, :, :], self.e[:, :, :], ACT.Exp).then_inc(self.exped, 1)
        else:
            nc.scalar.activation(self.e[:, :, :], self.logits[:, :, :], ACT.Exp, scale=-1.0).then_inc(self.exped, 1)

    def choose(self, dve):
        K, nc, E = self.K, self.K.nc, self.E
        e, prob, z, mx, tot, top, idx, idxf, hot0, hot1, gates, logits, rest = (
            t[:, :] for t in (self.e, self.prob, self.z, self.mx, self.tot, self.top, self.idx, self.idxf, self.hot0,
                              self.hot1, self.gates, self.logits, self.rest))

        def link(ins):
            self.done += 1
            ins.then_inc(self.chain, 1)
            dve.wait_ge(self.chain, self.done)

        def over(t):
            return t.unsqueeze(2).to_broadcast([P, NB, E])

        if self.shared:
            link(nc.vector.tensor_reduce(mx, logits[:, :, 0:E], AX.X, ALU.max))
            nc.vector.tensor_tensor(e, logits[:, :, 0:E], over(mx), ALU.subtract).then_inc(self.shifted, 1)
            dve.wait_ge(self.exped, 1)
            link(nc.vector.tensor_reduce(tot, prob, AX.X, ALU.add))
            link(nc.vector.reciprocal(mx, tot))
            link(nc.vector.tensor_tensor(prob, prob, over(mx), ALU.mult))
        else:
            dve.wait_ge(self.exped, 1)
            link(nc.vector.tensor_scalar(e, e, 1.0, None, ALU.add))
            link(nc.vector.reciprocal(prob, e))
        for b in range(NB):
            last = nc.vector.max(top[:, b, :], prob[:, b, :])
        link(last)
        for b in range(NB):
            last = nc.vector.max_index(idx[:, b, :], top[:, b, :], prob[:, b, :])
        link(last)
        link(nc.vector.tensor_copy(idxf, idx))
        iota = K.iota[:, 0:E].unsqueeze(1).to_broadcast([P, NB, E])
        nc.vector.tensor_tensor(hot0, iota, over(idxf[:, :, 0]), ALU.is_equal)
        nc.vector.tensor_tensor(tot, top[:, :, 0], top[:, :, 1], ALU.add)
        link(nc.vector.tensor_tensor(hot1, iota, over(idxf[:, :, 1]), ALU.is_equal))
        nc.vector.reciprocal(mx, tot)
        link(nc.vector.tensor_tensor(hot0, hot0, hot1, ALU.add))
        link(nc.vector.tensor_tensor(hot0, hot0, prob, ALU.mult))
        last = nc.vector.tensor_tensor(gates[:, :, 0:E], hot0, over(mx), ALU.mult)
        if self.shared:
            link(nc.vector.tensor_scalar(z, z, 1.0, None, ALU.add))
            last = nc.vector.reciprocal(gates[:, :, E], z)
        last.then_inc(self.routed, 1)
        dve.wait_ge(self.zeroed, 1)
        dve.wait_ge(self.routed, 1)
        part_in_three(nc.vector, link, gates, rest, [self.parts[:, :, k * 32:k * 32 + self.G] for k in range(3)])
        assert self.done == self.steps, self.done

    def turn(self, pe, g):
        pe.wait_ge(self.chain, self.steps)
        wait(pe, self.gates_kept, g - 1)
        for i in range(GB):
            mm = pe.transpose(self.turned_ps[g % 2][:, i * P:(i + 1) * P], self.parts[:, GB * g + i, :], self.K.identb[:, :])
        mm.then_inc(self.gates_turned, 1)

    def keep(self, dve, g):
        dve.wait_ge(self.gates_turned, g + 1)
        self.K.nc.vector.tensor_copy(self.gT[:, g * GB * P:(g + 1) * GB * P],
                                     self.turned_ps[g % 2][:, :]).then_inc(self.gates_kept, 1)


def shared_mixture(K, name, gT, w_gate, w_up, w_down, sel):
    nc = K.nc
    gate_ps, up_ps, spread_ps, down_ps, out_ps = K.bank[0:2], K.bank[2:4], K.bank[4:6], K.bank[6], K.bank[7]
    W = GB * P
    with ExitStack() as ctx:
        def sb(s, shape, dt=F32):
            return ctx.enter_context(nc.sbuf_tensor(f"{name}_{s}", shape, dt))

        def sem(s):
            return K.sem(f"{name}_{s}")

        silu, prod, hidden = sb("silu", [P, 2, W]), sb("prod", [P, 2, W]), sb("hidden", [P, 2, W])
        high, low = sb("high", [P, 2, W], F32R), sb("low", [P, 2, W], F32R)
        yT = sb("yT", [P, W])
        gated, raised, spread, silued, produced, weighed, parted_high, parted_low, multiplied = (
            sem(s) for s in ("gated", "raised", "spread", "silued", "produced", "weighed", "parted_high",
                             "parted_low", "multiplied"))
        y_kept, y_turned, added = sem("y_kept"), sem("y_turned"), sem("added")
        block = ctx.enter_context(nc.Block())

        def before(eng, sem, g, c, k):
            wait(eng, sem, NC0 * g + c - k + 1)

        @block.tensor
        def _(pe):
            def up(g, c):
                xg = [x[:, bass.ds(g * W, W)] for x in K.xsplit]
                cols = slice(c * P, (c + 1) * P)
                before(pe, silued, g, c, 2)
                part_matmul(pe, gate_ps[c % 2][:, :], [w[:, cols] for w in w_gate], xg).then_inc(gated, 1)
                before(pe, produced, g, c, 2)
                part_matmul(pe, up_ps[c % 2][:, :], [w[:, cols] for w in w_up], xg).then_inc(raised, 1)
                before(pe, weighed, g, c, 2)
                pe.matmul(spread_ps[c % 2][:, :], sel[:, cols], gT[:, bass.ds(g * W, W)],
                          start=True, stop=True).then_inc(spread, 1)

            def down(g, c):
                before(pe, parted_low, g, c, 0)
                if c == 0:
                    wait(pe, y_kept, g)
                part_matmul(pe, down_ps[:, :], [w[:, c, :] for w in w_down],
                            [high[:, c % 2, :], low[:, c % 2, :]], start=c == 0, stop=c == NC0 - 1).then_inc(multiplied, 1)

            def turn(g):
                wait(pe, y_kept, g + 1)
                for i in range(GB):
                    mm = pe.transpose(out_ps[:, i * P:(i + 1) * P], yT[:, i * P:(i + 1) * P], K.ident[:, :])
                mm.then_inc(y_turned, 1)

            def group(g):
                for c in range(NC0):
                    up(g, c)
                    if c >= 2:
                        down(g, c - 2)
                    elif follows(g):
                        down(g - 1, NC0 - 2 + c)
                    if c == 3 and follows(g):
                        turn(g - 1)

            loop_groups(pe, group)
            down(NG - 1, NC0 - 2)
            down(NG - 1, NC0 - 1)
            turn(NG - 1)

        @block.scalar
        def _(act):
            def keep_y(g):
                wait(act, multiplied, NC0 * (g + 1))
                nc.scalar.activation(yT[:, :], down_ps[:, :], ACT.Copy).then_inc(y_kept, 1)

            def group(g):
                for c in range(NC0):
                    before(act, gated, g, c, 0)
                    before(act, produced, g, c, 2)
                    nc.scalar.activation(silu[:, c % 2, :], gate_ps[c % 2][:, :], ACT.Silu).then_inc(silued, 1)
                    if c == 2 and follows(g):
                        keep_y(g - 1)

            loop_groups(act, group)
            keep_y(NG - 1)

        @block.vector
        def _(dve):
            def add(g):
                wait(dve, y_turned, g + 1)
                xg = K.x[:, bass.ds(g * GB, GB), :]
                nc.vector.tensor_tensor(xg, out_ps[:, :].rearrange("p (i d) -> p i d", i=GB), xg, ALU.add).then_inc(added, 1)

            def group(g):
                for c in range(NC0):
                    before(dve, silued, g, c, 0)
                    before(dve, raised, g, c, 0)
                    before(dve, weighed, g, c, 2)
                    nc.vector.tensor_tensor(prod[:, c % 2, :], silu[:, c % 2, :], up_ps[c % 2][:, :],
                                            ALU.mult).then_inc(produced, 1)
                    before(dve, produced, g, c, 0)
                    before(dve, spread, g, c, 0)
                    before(dve, parted_low, g, c, 2)
                    nc.vector.tensor_tensor(hidden[:, c % 2, :], prod[:, c % 2, :], spread_ps[c % 2][:, :],
                                            ALU.mult).then_inc(weighed, 1)
                    before(dve, weighed, g, c, 0)
                    before(dve, multiplied, g, c, 2)
                    nc.vector.tensor_copy(high[:, c % 2, :], hidden[:, c % 2, :]).then_inc(parted_high, 1)
                    if c == 5 and follows(g):
                        add(g - 1)

            loop_groups(dve, group)
            add(NG - 1)

        @block.gpsimd
        def _(pool):
            def group(g):
                for c in range(NC0):
                    before(pool, parted_high, g, c, 0)
                    before(pool, multiplied, g, c, 2)
                    nc.gpsimd.tensor_tensor(low[:, c % 2, :], hidden[:, c % 2, :], high[:, c % 2, :].bitcast(F32),
                                            ALU.subtract).then_inc(parted_low, 1)

            loop_groups(pool, group)


def mixture(K, name, gT, w1, b1, w2, b2, sel, out, stored):
    nc = K.nc
    W = GB * P
    NT = 32
    up_ps, spread_ps, down_ps, out_ps = K.bank[0:4], K.bank[4:6], K.bank[6], K.bank[7]
    with ExitStack() as ctx:
        def sb(s, shape, dt=F32):
            return ctx.enter_context(nc.sbuf_tensor(f"{name}_{s}", shape, dt))

        def sem(s):
            return K.sem(f"{name}_{s}")

        geluT, hidden = sb("geluT", [P, 4, W]), sb("hidden", [P, 4, W])
        high, low = sb("high", [P, 4, W], F32R), sb("low", [P, 4, W], F32R)
        yT = sb("yT", [P, W])
        raised, gelued, spread, weighed, parted_high, parted_low, multiplied = (
            sem(s) for s in ("raised", "gelued", "spread", "weighed", "parted_high", "parted_low", "multiplied"))
        y_kept, y_turned, added = sem("y_kept"), sem("y_turned"), sem("added")
        block = ctx.enter_context(nc.Block())
        LAG = 3

        def before(eng, sem, g, c, k):
            wait(eng, sem, NT * g + c - k + 1)

        @block.tensor
        def _(pe):
            def up(g, c):
                e = c // 4
                before(pe, gelued, g, c, 4)
                part_matmul(pe, up_ps[c % 4][:, :], [w[:, c * P:(c + 1) * P] for w in w1],
                            [x[:, bass.ds(g * W, W)] for x in K.xsplit]).then_inc(raised, 1)
                if c % 4 == 0:
                    before(pe, weighed, g, c, 5)
                    pe.matmul(spread_ps[e % 2][:, :], sel[:, e * P:(e + 1) * P], gT[:, bass.ds(g * W, W)],
                              start=True, stop=True).then_inc(spread, 1)

            def down(g, c):
                before(pe, parted_low, g, c, 0)
                if c == 0:
                    wait(pe, y_kept, g)
                    for k in range(3):
                        pe.matmul(down_ps[:, :], b2[:, k * P:(k + 1) * P], gT[:, bass.ds(g * W, W)],
                                  start=k == 0, stop=False)
                part_matmul(pe, down_ps[:, :], [w[:, c, :] for w in w2], [high[:, c % 4, :], low[:, c % 4, :]],
                            start=False, stop=c == NT - 1).then_inc(multiplied, 1)

            def turn(g):
                wait(pe, y_kept, g + 1)
                for i in range(GB):
                    mm = pe.transpose(out_ps[:, i * P:(i + 1) * P], yT[:, i * P:(i + 1) * P], K.ident[:, :])
                mm.then_inc(y_turned, 1)

            def group(g):
                for c in range(NT):
                    up(g, c)
                    if c >= LAG:
                        down(g, c - LAG)
                    elif follows(g):
                        down(g - 1, NT - LAG + c)
                    if c == 5 and follows(g):
                        turn(g - 1)

            loop_groups(pe, group)
            for c in range(NT - LAG, NT):
                down(NG - 1, c)
            turn(NG - 1)

        @block.scalar
        def _(act):
            def keep_y(g):
                wait(act, multiplied, NT * (g + 1))
                nc.scalar.activation(yT[:, :], down_ps[:, :], ACT.Copy).then_inc(y_kept, 1)

            def group(g):
                for c in range(NT):
                    before(act, raised, g, c, 0)
                    before(act, weighed, g, c, 4)
                    nc.scalar.activation(geluT[:, c % 4, :], up_ps[c % 4][:, :], ACT.Gelu,
                                         bias=b1[:, c:c + 1]).then_inc(gelued, 1)
                    if c == LAG - 1 and follows(g):
                        keep_y(g - 1)

            loop_groups(act, group)
            keep_y(NG - 1)

        @block.vector
        def _(dve):
            def add(g):
                wait(dve, y_turned, g + 1)
                xg = K.x[:, bass.ds(g * GB, GB), :]
                nc.vector.tensor_tensor(xg, out_ps[:, :].rearrange("p (i d) -> p i d", i=GB), xg, ALU.add).then_inc(added, 1)

            def weigh(g, c):
                before(dve, gelued, g, c, 0)
                if c % 4 == 0:
                    wait(dve, spread, E1 * g + c // 4 + 1)
                before(dve, parted_low, g, c, 4)
                nc.vector.tensor_tensor(hidden[:, c % 4, :], geluT[:, c % 4, :], spread_ps[c // 4 % 2][:, :],
                                        ALU.mult).then_inc(weighed, 1)

            def part(g, c):
                before(dve, weighed, g, c, 0)
                before(dve, multiplied, g, c, 4)
                nc.vector.tensor_copy(high[:, c % 4, :], hidden[:, c % 4, :]).then_inc(parted_high, 1)

            def group(g):
                for c in range(NT):
                    weigh(g, c)
                    part(g, c)
                    if c == 8 and follows(g):
                        add(g - 1)

            loop_groups(dve, group)
            add(NG - 1)

        @block.gpsimd
        def _(pool):
            def group(g):
                for c in range(NT):
                    before(pool, parted_high, g, c, 0)
                    before(pool, multiplied, g, c, 4)
                    nc.gpsimd.tensor_tensor(low[:, c % 4, :], hidden[:, c % 4, :], high[:, c % 4, :].bitcast(F32),
                                            ALU.subtract).then_inc(parted_low, 1)

            loop_groups(pool, group)

        @block.sync
        def _(sp):
            for g in range(NG):
                sp.wait_ge(added, g + 1)
                sp.dma_start(out[GB * g:GB * (g + 1), :, :].rearrange("b t d -> t b d"),
                             K.x[:, GB * g:GB * (g + 1), :]).then_inc(stored, 16)
            sp.wait_ge(stored, 16 * NG)


def standardised_attention(K, name, xT, wq, wk, wv, wo, weights=(), weights_low=()):
    nc = K.nc
    W = GB * P
    q_ps, k_ps, v_ps, score_ps = K.bank[0], K.bank[1], K.bank[2], K.bank[3:5]
    spread_ps, turned_ps, attended_ps = K.bank[5], K.bank[6], K.bank[7]
    out_ps = turned_ps
    with ExitStack() as ctx:
        def sb(s, shape, dt=F32):
            return ctx.enter_context(nc.sbuf_tensor(f"{name}_{s}", shape, dt))

        def sem(s):
            return K.sem(f"{name}_{s}")

        qT, kT, v = sb("qT", [P, W]), sb("kT", [P, W]), sb("v", [P, 2, W])
        p, pT, oT = sb("p", [P, 2, W]), sb("pT", [P, W]), sb("oT", [P, W])
        st, mv, means, dev, vp = (sb("st", [P, GB, 6]), sb("mv", [P, GB, 2]), sb("means", [P, GB]),
                                  sb("dev", [P, GB]), sb("vp", [P, GB]))
        ve, rs, negmax, shift, tot, rtot = (sb(s, [P, 2, GB]) for s in ("ve", "rs", "negmax", "shift", "tot", "rtot"))
        q_made, k_made, v_made, q_kept, k_kept, v_kept = (
            sem(s) for s in ("q_made", "k_made", "v_made", "q_kept", "k_kept", "v_kept"))
        scored, averaged, mean_spread, deviated, var_spread, varied, rooted, shifted = (
            sem(s) for s in ("scored", "averaged", "mean_spread", "deviated", "var_spread", "varied", "rooted",
                             "shifted"))
        exped, scaled, turned, p_kept, attended, o_kept, projected, added = (
            sem(s) for s in ("exped", "scaled", "turned", "p_kept", "attended", "o_kept", "projected", "added"))
        chain = sem("chain")
        block = ctx.enter_context(nc.Block())

        def part(t, i):
            return t[..., i * P:(i + 1) * P]

        def run(step, *parts):
            for g in range(-1, NG + 2):
                step(g, *((lambda n, f=f: f(n) if 0 <= n < NG else None) for f in parts))

        @block.tensor
        def _(pe):
            def project_in(g):
                cols = slice(g * W, (g + 1) * W)
                context = K.ctxT[:, GB * g:GB * (g + 1), :]
                wait(pe, q_kept, g)
                pe.matmul(q_ps[:, :], wq, xT[:, cols], start=True, stop=True).then_inc(q_made, 1)
                wait(pe, k_kept, g)
                pe.matmul(k_ps[:, :], wk, context.rearrange("p i t -> p (i t)"), start=True, stop=True).then_inc(k_made, 1)

            def project_v(g):
                context = K.ctxT[:, GB * g:GB * (g + 1), :]
                wait(pe, v_kept, g)
                for i in range(GB):
                    mm = pe.matmul(part(v_ps, i), context[:, i, :], wv, start=True, stop=True)
                mm.then_inc(v_made, 1)

            def score(g):
                pe.wait_ge(q_kept, g + 1)
                pe.wait_ge(k_kept, g + 1)
                wait(pe, exped, g - 1)
                for i in range(GB):
                    mm = pe.matmul(part(score_ps[g % 2], i), part(qT, i), part(kT, i), start=True, stop=True)
                mm.then_inc(scored, 1)

            def spread_mean(g):
                pe.wait_ge(averaged, g + 1)
                pe.matmul(spread_ps[:, 0:GB], K.mean[:, :], means[:, :], start=True, stop=True).then_inc(mean_spread, 1)

            def spread_var(g):
                pe.wait_ge(deviated, g + 1)
                pe.matmul(spread_ps[:, 8:8 + GB], K.mean[:, :], vp[:, :], start=True, stop=True).then_inc(var_spread, 1)

            def turn_p(g):
                pe.wait_ge(scaled, g + 1)
                wait(pe, added, g)
                for i in range(GB):
                    mm = pe.transpose(part(turned_ps, i), part(p[:, g % 2, :], i), K.ident[:, :])
                mm.then_inc(turned, 1)

            def attend(g):
                pe.wait_ge(p_kept, g + 1)
                wait(pe, o_kept, g)
                for i in range(GB):
                    mm = pe.matmul(part(attended_ps, i), part(v[:, g % 2, :], i), part(pT, i), start=True, stop=True)
                mm.then_inc(attended, 1)

            def project(g):
                pe.wait_ge(o_kept, g + 1)
                for i in range(GB):
                    mm = pe.matmul(part(out_ps, i), part(oT, i), wo, start=True, stop=True)
                mm.then_inc(projected, 1)

            for s, c in weights:
                pe.wait_ge(s, c)
            def step(g, score, project, project_in, spread_mean, turn_p, project_v, spread_var, attend):
                score(g)
                project(g - 2)
                project_in(g + 1)
                spread_mean(g)
                turn_p(g - 1)
                project_v(g + 1)
                spread_var(g)
                attend(g - 1)

            run(step, score, project, project_in, spread_mean, turn_p, project_v, spread_var, attend)

        @block.scalar
        def _(act):
            def exp(g):
                act.wait_ge(shifted, g + 1)
                wait(act, turned, g - 1)
                for i in range(GB):
                    e = nc.scalar.activation(part(p[:, g % 2, :], i), part(score_ps[g % 2], i), ACT.Exp,
                                             bias=shift[:, g % 2, i:i + 1], scale=rs[:, g % 2, i:i + 1],
                                             accum_out=tot[:, g % 2, i:i + 1])
                e.then_inc(exped, 1)

            def keep_in(g):
                act.wait_ge(q_made, g + 1)
                wait(act, scored, g)
                nc.scalar.activation(qT[:, :], q_ps[:, :], ACT.Copy).then_inc(q_kept, 1)
                act.wait_ge(k_made, g + 1)
                nc.scalar.activation(kT[:, :], k_ps[:, :], ACT.Copy).then_inc(k_kept, 1)

            def keep_p(g):
                act.wait_ge(turned, g + 1)
                wait(act, attended, g)
                nc.scalar.activation(pT[:, :], turned_ps[:, :], ACT.Copy).then_inc(p_kept, 1)

            def keep_o(g):
                act.wait_ge(attended, g + 1)
                wait(act, projected, g)
                nc.scalar.activation(oT[:, :], attended_ps[:, :], ACT.Copy).then_inc(o_kept, 1)

            def step(g, exp, keep_in, keep_p, keep_o):
                exp(g - 1)
                keep_in(g + 1)
                keep_p(g - 1)
                keep_o(g - 1)

            run(step, exp, keep_in, keep_p, keep_o)

        @block.vector
        def _(dve):
            done = [0]

            def link(ins):
                done[0] += 1
                ins.then_inc(chain, 1)
                dve.wait_ge(chain, done[0])

            def keep_v(g):
                dve.wait_ge(v_made, g + 1)
                wait(dve, attended, g - 1)
                nc.vector.tensor_copy(v[:, g % 2, :], v_ps[:, :]).then_inc(v_kept, 1)

            def scale(g):
                dve.wait_ge(exped, g + 1)
                link(nc.vector.reciprocal(rtot[:, g % 2, :], tot[:, g % 2, :]))
                p4 = p[:, g % 2, :].rearrange("p (i k) -> p i k", i=GB)
                nc.vector.tensor_tensor(p4, p4, rtot[:, g % 2, :].unsqueeze(2).to_broadcast([P, GB, P]),
                                        ALU.mult).then_inc(scaled, 1)

            def average(g):
                dve.wait_ge(scored, g + 1)
                for i in range(GB):
                    last = nc.vector.bn_stats(st[:, i, :], part(score_ps[g % 2], i))
                link(last)
                for i in range(GB):
                    last = nc.vector.bn_aggr(mv[:, i, :], st[:, i, :])
                link(last)
                wait(dve, mean_spread, g)
                nc.vector.tensor_copy(means[:, :], mv[:, :, 0]).then_inc(averaged, 1)
                nc.vector.tensor_reduce(negmax[:, g % 2, :], score_ps[g % 2][:, :].rearrange("p (i k) -> p i k", i=GB),
                                        AX.X, ALU.max, negate=True)

            def deviate(g):
                dve.wait_ge(mean_spread, g + 1)
                dve.wait_ge(averaged, g + 1)
                link(nc.vector.tensor_tensor(dev[:, :], means[:, :], spread_ps[:, 0:GB], ALU.subtract))
                link(nc.vector.tensor_tensor(dev[:, :], dev[:, :], dev[:, :], ALU.mult))
                nc.vector.tensor_tensor(vp[:, :], dev[:, :], mv[:, :, 1], ALU.add).then_inc(deviated, 1)

            def add(g):
                dve.wait_ge(projected, g + 1)
                xg = K.x[:, GB * g:GB * (g + 1), :]
                nc.vector.tensor_tensor(xg, out_ps[:, :].rearrange("p (i d) -> p i d", i=GB), xg, ALU.add).then_inc(added, 1)
                dve.wait_ge(added, g + 1)
                for b in range(GB * g, GB * (g + 1)):
                    nc.vector.bn_stats(K.st[:, b, :], K.x[:, b, :])

            def find_shift(g):
                dve.wait_ge(var_spread, g + 1)
                nc.vector.tensor_scalar(ve[:, g % 2, :], spread_ps[:, 8:8 + GB], EPS, None, ALU.add).then_inc(varied, 1)
                dve.wait_ge(rooted, g + 1)
                nc.vector.tensor_tensor(shift[:, g % 2, :], negmax[:, g % 2, :], rs[:, g % 2, :], ALU.mult).then_inc(shifted, 1)

            def step(g, average, scale, add, deviate, find_shift, keep_v):
                average(g)
                scale(g - 1)
                add(g - 2)
                deviate(g)
                find_shift(g)
                keep_v(g + 1)

            run(step, average, scale, add, deviate, find_shift, keep_v)

        @block.gpsimd
        def _(pool):
            for g in range(NG):
                pool.wait_ge(varied, g + 1)
                nc.gpsimd.tensor_tensor(rs[:, g % 2, :], ve[:, g % 2, :], K.mhalf[:, 0:GB], ALU.pow).then_inc(rooted, 1)
                for w, high, low in pieces(weights_low, g):
                    nc.gpsimd.tensor_tensor(low, w, high.bitcast(F32), ALU.subtract)


def decoder(nc, A, out, phases=7):
    K = Shared(nc)
    with ExitStack() as ctx:
        def sb(n, shape, dt=F32):
            return ctx.enter_context(nc.sbuf_tensor(n, shape, dt))

        def sem(n):
            return ctx.enter_context(nc.semaphore(n))

        K.bank = [ctx.enter_context(nc.psum_tensor(f"bank{i}", [P, 512], F32)) for i in range(8)]
        K.x, K.st = sb("x_sb", [P, NB, P]), sb("x_stats", [P, NB, 6])
        K.ctxT = sb("ctxT_sb", [P, NB, P])
        K.ident, K.identb = sb("ident_sb", [P, P]), sb("identb", [P, P], BF16)
        K.mask = sb("mask_sb", [P, P])
        K.headmask, K.iota = sb("headmask_sb", [P, 16]), sb("iota_sb", [P, 16])
        K.ones, K.mean = sb("ones", [1, P]), sb("mean", [P, P])
        K.mhalf = sb("mhalf", [P, NB])
        logits0, gates0 = sb("logits0", [P, NB, G0]), sb("gates0", [P, NB, G0])
        logits1, gates1 = sb("logits1", [P, NB, E1]), sb("gates1", [P, NB, E1])
        gT = sb("gT", [P, NB * P], BF16)
        sel0, sel1 = sb("sel0", [P, NC0 * P], BF16), sb("sel1", [P, E1 * P], BF16)
        b2, b2_rest = sb("b2", [P, 3 * P], BF16), sb("b2_rest", [P, P])
        K.x_loaded = [sem(f"x_loaded{g}") for g in range(NG)]
        consts_loaded = sem("consts_loaded")
        stored = sem("stored")
        w, loaded = {}, {}
        attn1 = ctx.enter_context(ExitStack())
        layer0 = ctx.enter_context(ExitStack())
        attn0 = ctx.enter_context(ExitStack())

        with nc.Block() as block:
            groups = {"self0": ["a_w", "a_b", "a_bo"], "cross0": ["c_wq", "c_wkv", "c_wo", "c_bo"],
                      "ffn0": ["f_wr", "f_wgu", "f_wd", "f_sel"], "self1": ["s_wqkv", "s_wo"],
                      "cross1": ["t_wqo", "t_wkv"], "ffn1": ["m_wr", "m_w1", "m_b1", "m_w2", "m_b2", "m_sel"]}
            for gname, scope in (("cross1", ctx), ("ffn1", ctx), ("self1", attn1), ("self0", layer0),
                                 ("cross0", layer0), ("ffn0", layer0)):
                loaded[gname] = (sem(f"loaded_{gname}"), 16 * len(groups[gname]))
                for n in groups[gname]:
                    w[n] = scope.enter_context(nc.sbuf_tensor(f"{n}_sb", list(A[n].shape), F32))
                if scope is attn1:
                    kblk = scope.enter_context(nc.sbuf_tensor("kblk", [P, 2, 16, P], F32))
            v_small = attn0.enter_context(nc.sbuf_tensor("v_small", [P, 2, 16 * 136], F32))

            @block.sync
            def _(sp):
                for g in range(NG):
                    sp.dma_start(K.x[:, GB * g:GB * (g + 1), :],
                                 A["x"][GB * g:GB * (g + 1), :, :].rearrange("b t d -> t b d")).then_inc(K.x_loaded[g], 16)

            @block.scalar
            def _(act):
                for n, t in (("ident", K.ident), ("mask", K.mask), ("headmask", K.headmask), ("iota", K.iota)):
                    act.dma_start(t[:, :], A[n]).then_inc(consts_loaded, 16)
                for n in groups["self0"]:
                    act.dma_start(w[n][:, :], A[n]).then_inc(loaded["self0"][0], 16)

            @block.gpsimd
            def _(pool):
                nc.gpsimd.memset(v_small[:, :, :], 0.0)

            @block.vector
            def _(dve):
                nc.vector.memset(K.ones[:, :], 1.0)
                nc.vector.memset(K.mean[:, :], 1.0 / P)
                nc.vector.memset(K.mhalf[:, :], -0.5)
                dve.wait_ge(consts_loaded, 64)
                nc.vector.tensor_copy(K.identb[:, :], K.ident[:, :])

        later = [(w[n][:, :], A[n], loaded[g][0]) for g in ("cross0", "ffn0", "self1", "cross1", "ffn1") for n in groups[g]]
        later.append((K.ctxT[:, :, :], A["ctxT"], loaded["cross1"][0]))
        loaded["cross1"] = (loaded["cross1"][0], loaded["cross1"][1] + 16)
        a = w["a_w"]
        tiles = lambda t, n: t[:, :].rearrange("p (t d) -> p t d", t=n)
        attention(K, "self0", 16, 8, True, a[:, 0:P], a[:, P:2 * P], a[:, 2 * P:3 * P],
                  tiles(a[:, 3 * P:4 * P], 1), w["a_b"][:, 0:1], w["a_b"][:, 1:2], w["a_b"][:, 2:3], w["a_bo"], p_on_act=True,
                  weights=[loaded["self0"]], later=later, v=v_small, clean=[kblk[:, :, :, :]])
        K.clear(by=nc.scalar)
        attn0.close()
        if phases > 1:
            c = w["c_wkv"]
            attention(K, "cross0", 8, 64, False, w["c_wq"], c[:, 0:512], c[:, 512:1024],
                      tiles(w["c_wo"], 4), bo=w["c_bo"], ctxT=A["ctxT"], weights=[loaded["cross0"]],
                      kblk=kblk[:, :, 0:8, :], next_stats=True)
            K.clear()
        if phases > 2:
            u = w["f_wgu"]
            with ExitStack() as parts:
                def part(n, width):
                    return [parts.enter_context(nc.sbuf_tensor(f"{n}_{k}", [P, width], F32R)) for k in ("high", "low")]

                gu, d, K.xsplit = part("f_wgu", 2 * NC0 * P), part("f_wd", NC0 * P), part("x0", NB * P)
                normalise(K, "norm_ffn0", None, K.xsplit, logits0, w["f_wr"][:, :], G0, weights=[loaded["ffn0"]],
                          weights_split=[(u[:, :], gu[0][:, :], gu[1][:, :])],
                          gates=gates0, experts=E0, shared=True, gT=gT, casts=[(sel0[:, :], w["f_sel"][:, :])],
                          weights_late=[(w["f_wd"][:, :], d[0][:, :], d[1][:, :])])
                K.clear()
                shared_mixture(K, "ffn0", gT, [t[:, 0:NC0 * P] for t in gu], [t[:, NC0 * P:2 * NC0 * P] for t in gu],
                               [tiles(t, NC0) for t in d], sel0)
                K.clear()
        layer0.close()
        if phases > 3:
            s = w["s_wqkv"]
            attention(K, "self1", 16, 64, True, s[:, 0:1024], s[:, 1024:2048], s[:, 2048:3072],
                      tiles(w["s_wo"], 8), weights=[loaded["self1"]], kblk=kblk, next_stats=True)
            K.clear()
        attn1.close()
        if phases > 4:
            with ExitStack() as scope:
                def part(n, width):
                    return [scope.enter_context(nc.sbuf_tensor(f"{n}_{k}", [P, width], F32R)) for k in ("high", "low")]

                w1, w2 = part("m_w1", 4 * E1 * P), part("m_w2", 4 * E1 * P)
                with nc.sbuf_tensor("xT_sb", [P, NB * P], F32) as xT:
                    normalise(K, "norm_cross1", xT, weights=[loaded["ffn1"]],
                              weights_high=[(w["m_w1"][:, :], w1[0][:, :]), (w["m_w2"][:, :], w2[0][:, :])])
                    K.clear()
                    t, r = w["t_wqo"], w["t_wkv"]
                    standardised_attention(K, "cross1", xT, t[:, 0:P], r[:, 0:P], r[:, P:2 * P], t[:, P:2 * P],
                                           weights=[loaded["cross1"]],
                                           weights_low=[(w["m_w1"][:, :], w1[0][:, :], w1[1][:, :]),
                                                        (w["m_w2"][:, :], w2[0][:, :], w2[1][:, :])])
                    K.clear()
                if phases > 5:
                    K.xsplit = part("x1", NB * P)
                    third = lambda t: [t[:, k * P:(k + 1) * P] for k in range(3)]
                    normalise(K, "norm_ffn1", None, K.xsplit, logits1, w["m_wr"][:, :], E1, weights=[loaded["ffn1"]],
                              gates=gates1, experts=E1, gT=gT, casts=[(sel1[:, :], w["m_sel"][:, :])],
                              thirds=(w["m_b2"][:, :], b2_rest[:, :], third(b2)))
                    K.clear()
                    mixture(K, "ffn1", gT, w1, w["m_b1"], [tiles(t, 32) for t in w2], b2, sel1, out, stored)
                    K.clear()
        if phases < 6:
            with nc.Block() as block:
                @block.sync
                def _(sp):
                    for gname, (q, n) in loaded.items():
                        sp.wait_ge(q, n)
                    sp.dma_start(out.rearrange("b t d -> t b d"), K.x[:, :, :]).then_inc(stored, 16)
                    sp.wait_ge(stored, 16)


def layout(inputs):
    import numpy as np

    I = {k: np.asarray(v) for k, v in inputs.items()}

    def rows(a):
        return a.reshape(-1, P, a.shape[-1]).transpose(1, 0, 2).reshape(P, -1)

    def pad(a):
        return np.concatenate([a, np.zeros((P - a.shape[0], *a.shape[1:]), a.dtype)], 0)

    L = {"x": I["x"], "ctxT": pad(I["ctx_768"].transpose(2, 0, 1))}
    L["a_w"] = np.concatenate([I["L0_attn_" + n].T for n in ("Wq", "Wk", "Wv", "Wo")], 1)
    L["a_b"] = np.stack([I["L0_attn_" + n] for n in ("bq", "bk", "bv")], 1)
    L["a_bo"] = I["L0_attn_bo"][None, :]
    L["c_wq"] = I["L0_xattn_Wq"]
    L["c_wkv"] = pad(np.concatenate([I["L0_xattn_Wk"], I["L0_xattn_Wv"]], 1))
    L["c_wo"] = rows(I["L0_xattn_Wo"])
    L["c_bo"] = I["L0_xattn_bo"][None, :]
    L["f_wr"] = np.concatenate([I["L0_ffn_Wg"], I["L0_ffn_Wsg"]], 0).T
    L["f_wgu"] = np.concatenate([I["L0_ffn_We_gate"].reshape(-1, P), I["L0_ffn_Ws_gate"],
                                 I["L0_ffn_We_up"].reshape(-1, P), I["L0_ffn_Ws_up"]], 0).T
    L["f_wd"] = rows(np.concatenate([I["L0_ffn_We_down"].transpose(0, 2, 1).reshape(-1, P), I["L0_ffn_Ws_down"].T], 0))
    L["s_wqkv"] = np.concatenate([I["L1_attn_" + n].reshape(-1, P) for n in ("W_Q", "W_K", "W_V")], 0).T
    L["s_wo"] = rows(I["L1_attn_W_O"].T)
    L["t_wqo"] = np.concatenate([I["L1_xattn_Wq"].T, I["L1_xattn_Wo"].T], 1)
    L["t_wkv"] = pad(np.concatenate([I["L1_xattn_Wk"].T, I["L1_xattn_Wv"].T], 1))
    L["m_wr"] = I["L1_ffn_centroids"].T
    L["m_w1"] = I["L1_ffn_W1"].transpose(1, 0, 2).reshape(P, -1)
    L["m_b1"] = I["L1_ffn_b1"].reshape(-1, P).T
    L["m_w2"] = rows(I["L1_ffn_W2"].reshape(-1, P))
    L["m_b2"] = np.zeros((P, P), np.float32)
    for r in (0, 32, 64):
        L["m_b2"][r:r + E1] = I["L1_ffn_b2"]
    i = np.arange(P)
    L["ident"] = np.eye(P, dtype=np.float32)
    L["mask"] = np.where(i[None, :] <= i[:, None], 0.0, NEG).astype(np.float32)
    L["headmask"] = (i[:, None] // 8 == np.arange(16)[None, :]).astype(np.float32)
    L["iota"] = np.tile(np.arange(16, dtype=np.float32), (P, 1))
    part_row = i[:, None] % 32 + np.where(i[:, None] < 96, 0, P)
    L["f_sel"] = (np.minimum(np.arange(NC0 * P) // 64, E0)[None, :] == part_row).astype(np.float32)
    L["m_sel"] = (np.arange(E1 * P)[None, :] // P == part_row).astype(np.float32)
    return {k: np.ascontiguousarray(v) for k, v in L.items()}


def kernel(**inputs):
    import concourse.bacc as bacc
    from concourse.bass_utils import run_bass_kernel_spmd

    nc = bacc.Bacc("TRN2", target_bir_lowering=False, num_devices=1)
    arrays, aps = {}, {}
    for name, a in layout(inputs).items():
        arrays[f"in_{name}"] = a
        aps[name] = nc.dram_tensor(f"in_{name}", a.shape, mybir.dt.from_np(a.dtype), kind="ExternalInput").ap()
    out = nc.dram_tensor("out", (NB, P, P), F32, kind="ExternalOutput").ap()
    decoder(nc, aps, out)
    r = run_bass_kernel_spmd(nc, [arrays], core_ids=[0])
    return r.results[0]["out"]
```
